# Optimizing a Trainium2 kernel written in Bass

```python
import numpy as np
import jax
import jax.numpy as jnp

def _softmax(x, axis=-1):
    return jax.nn.softmax(x, axis=axis)

def _gelu(x):
    return jax.nn.gelu(x, approximate=True)

def _silu(x):
    return jax.nn.silu(x)

def _sigmoid(x):
    return jax.nn.sigmoid(x)

def _layernorm(x, axis=-1, eps=1e-05):
    m = jnp.mean(x, axis=axis, keepdims=True)
    v = jnp.var(x, axis=axis, keepdims=True)
    return (x - m) / jnp.sqrt(v + eps)

def _scatter_add(tgt, idx, src, axis=0):
    return tgt.at[idx].add(src)

def _segment_sum(src, seg, n):
    return jax.ops.segment_sum(src, seg, n)
kernel_name = 'mk_perceiver_d1_seqx_r8_4a14c9'

def setup_inputs(seed: int=0):
    np.random.seed(seed)
    _w = jnp.asarray

    def _rec_inputs():
        import jax
        import jax.numpy as jnp
        _rk = jax.random.key(seed)
        x = -0.0002928 + 1 * jax.random.normal(jax.random.fold_in(_rk, 1), (64, 32, 128), jnp.float32)
        _lenS = 32 - jax.random.randint(jax.random.fold_in(_rk, 7), (64,), 0, max(1, 32 // 4) + 1, jnp.int32)
        _lenS2 = 257 - jax.random.randint(jax.random.fold_in(_rk, 8), (64,), 0, max(1, 257 // 4) + 1, jnp.int32)
        _ctx_1024P = jax.random.normal(jax.random.fold_in(_rk, 11), (64, 16, 128), jnp.float32)
        _ctx_1024c = jax.random.dirichlet(jax.random.fold_in(_rk, 511), 0.3 * jnp.ones((16,), jnp.float32), (64, 257))
        _ctx_1024t = jnp.einsum('bsk,bkd->bsd', _ctx_1024c, _ctx_1024P)
        _ctx_1024t = _ctx_1024t * jax.lax.rsqrt(jnp.mean(jnp.square(_ctx_1024t)) + 1e-12) * 0.953939
        ctx_1024 = -1.39393e-06 + 0.999914 * (_ctx_1024t + 0.3 * jax.random.normal(jax.random.fold_in(_rk, 611), (64, 257, 128), jnp.float32))
        _validS = jnp.arange(32)[None, :] < _lenS[:, None]
        _validS2 = jnp.arange(257)[None, :] < _lenS2[:, None]
        _causal = jnp.tril(jnp.ones((32, 32), dtype=bool))
        mask_Bx1xSxS2_bf1 = jnp.ones((64, 1, 32, 257), dtype=bool)
        return (x, ctx_1024, mask_Bx1xSxS2_bf1)
    x, ctx_1024, mask_Bx1xSxS2_bf1 = _rec_inputs()

    def _L0_xattn_setup():
        import math
        import jax, jax.numpy as jnp
        import numpy as np
        B, T, E = (2, 256, 128)
        H, DK, DV = (16, 64, 64)
        key = jax.random.key(seed)
        ks = jax.random.split(key, 7)
        x_query = jax.random.normal(ks[0], (B, T, E), dtype=jnp.float32)
        x_key = jax.random.normal(ks[1], (B, T, E), dtype=jnp.float32)
        x_value = jax.random.normal(ks[2], (B, T, E), dtype=jnp.float32)
        mask = jnp.ones((B, 1, T, T), dtype=bool)
        w_q = jax.random.normal(ks[3], (H, E, DK), dtype=jnp.float32) / math.sqrt(E)
        w_k = jax.random.normal(ks[4], (H, E, DK), dtype=jnp.float32) / math.sqrt(E)
        w_v = jax.random.normal(ks[5], (H, E, DV), dtype=jnp.float32) / math.sqrt(E)
        w_o = jax.random.normal(ks[6], (H, DV, E), dtype=jnp.float32) / math.sqrt(DV * H)
        return {'x_query': x_query, 'x_key': x_key, 'x_value': x_value, 'mask': mask, 'w_q': w_q, 'w_k': w_k, 'w_v': w_v, 'w_o': w_o}
    _L0_xattn_all = _L0_xattn_setup()
    _L0_xattn_in = {k: v for k, v in _L0_xattn_all.items() if k in ('w_q', 'w_k', 'w_v', 'w_o')}
    del _L0_xattn_all

    def _L0_attn_setup():
        import jax, jax.numpy as jnp
        import numpy as np
        import math
        H = 8
        D = 32
        DEPTH = 1
        LAMBDA_INIT = 0.8 - 0.6 * math.exp(-0.3 * DEPTH)
        EPS = 1e-08
        key = jax.random.key(seed)
        ks = jax.random.split(key, 9)
        B, T, IN_DIM, OUT_DIM = (2, 256, 128, 128)
        E = 2 * H * D
        inp = {'x': jax.random.normal(ks[0], (B, T, IN_DIM), dtype=jnp.float32), 'Wq': jax.random.normal(ks[1], (IN_DIM, E), dtype=jnp.float32) * IN_DIM ** (-0.5), 'Wkv': jax.random.normal(ks[2], (IN_DIM, 2 * E), dtype=jnp.float32) * IN_DIM ** (-0.5), 'Wout': jax.random.normal(ks[3], (E, OUT_DIM), dtype=jnp.float32) * E ** (-0.5), 'lambda_q1': 0.1 * jax.random.normal(ks[4], (D,), dtype=jnp.float32), 'lambda_k1': 0.1 * jax.random.normal(ks[5], (D,), dtype=jnp.float32), 'lambda_q2': 0.1 * jax.random.normal(ks[6], (D,), dtype=jnp.float32), 'lambda_k2': 0.1 * jax.random.normal(ks[7], (D,), dtype=jnp.float32), 'gamma': jnp.ones((2 * D,), dtype=jnp.float32)}
        return inp
    _L0_attn_all = _L0_attn_setup()
    _L0_attn_in = {k: v for k, v in _L0_attn_all.items() if k in ('Wq', 'Wkv', 'Wout', 'lambda_q1', 'lambda_k1', 'lambda_q2', 'lambda_k2', 'gamma')}
    del _L0_attn_all

    def _L0_ffn_setup():
        import jax, jax.numpy as jnp
        import numpy as np
        D_MODEL = 128
        HIDDEN = 512
        NUM_ROUTED = 7
        TOP_K = 2

        def _swiglu(x_flat, wg, wu, wd):
            g = jnp.einsum('nd,edh->enh', x_flat, wg)
            u = jnp.einsum('nd,edh->enh', x_flat, wu)
            h = jax.nn.silu(g) * u
            return jnp.einsum('enh,ehd->end', h, wd)
        key = jax.random.key(seed)
        ks = jax.random.split(key, 8)
        s = 0.02
        return {'x': jax.random.normal(ks[0], (4, 256, D_MODEL), jnp.float32), 'router_w': jax.random.normal(ks[1], (NUM_ROUTED, D_MODEL), jnp.float32) * s, 'w_gate': jax.random.normal(ks[2], (NUM_ROUTED, D_MODEL, HIDDEN), jnp.float32) * s, 'w_up': jax.random.normal(ks[3], (NUM_ROUTED, D_MODEL, HIDDEN), jnp.float32) * s, 'w_down': jax.random.normal(ks[4], (NUM_ROUTED, HIDDEN, D_MODEL), jnp.float32) * s, 'sw_gate': jax.random.normal(ks[5], (1, D_MODEL, HIDDEN), jnp.float32) * s, 'sw_up': jax.random.normal(ks[6], (1, D_MODEL, HIDDEN), jnp.float32) * s, 'sw_down': jax.random.normal(ks[7], (1, HIDDEN, D_MODEL), jnp.float32) * s}
    _L0_ffn_all = _L0_ffn_setup()
    _L0_ffn_in = {k: v for k, v in _L0_ffn_all.items() if k in ('router_w', 'w_gate', 'w_up', 'w_down', 'sw_gate', 'sw_up', 'sw_down')}
    del _L0_ffn_all
    return {'x': x, 'ctx_1024': ctx_1024, 'mask_Bx1xSxS2_bf1': mask_Bx1xSxS2_bf1, 'L0_xattn_w_q': _L0_xattn_in['w_q'], 'L0_xattn_w_k': _L0_xattn_in['w_k'], 'L0_xattn_w_v': _L0_xattn_in['w_v'], 'L0_xattn_w_o': _L0_xattn_in['w_o'], 'L0_attn_Wq': _L0_attn_in['Wq'], 'L0_attn_Wkv': _L0_attn_in['Wkv'], 'L0_attn_Wout': _L0_attn_in['Wout'], 'L0_attn_lambda_q1': _L0_attn_in['lambda_q1'], 'L0_attn_lambda_k1': _L0_attn_in['lambda_k1'], 'L0_attn_lambda_q2': _L0_attn_in['lambda_q2'], 'L0_attn_lambda_k2': _L0_attn_in['lambda_k2'], 'L0_attn_gamma': _L0_attn_in['gamma'], 'L0_ffn_router_w': _L0_ffn_in['router_w'], 'L0_ffn_w_gate': _L0_ffn_in['w_gate'], 'L0_ffn_w_up': _L0_ffn_in['w_up'], 'L0_ffn_w_down': _L0_ffn_in['w_down'], 'L0_ffn_sw_gate': _L0_ffn_in['sw_gate'], 'L0_ffn_sw_up': _L0_ffn_in['sw_up'], 'L0_ffn_sw_down': _L0_ffn_in['sw_down']}

def reference(x, ctx_1024, mask_Bx1xSxS2_bf1, L0_xattn_w_q, L0_xattn_w_k, L0_xattn_w_v, L0_xattn_w_o, L0_attn_Wq, L0_attn_Wkv, L0_attn_Wout, L0_attn_lambda_q1, L0_attn_lambda_k1, L0_attn_lambda_q2, L0_attn_lambda_k2, L0_attn_gamma, L0_ffn_router_w, L0_ffn_w_gate, L0_ffn_w_up, L0_ffn_w_down, L0_ffn_sw_gate, L0_ffn_sw_up, L0_ffn_sw_down):
    import jax
    import jax.numpy as jnp

    def _L0_xattn_ref(x_query, x_key, x_value, mask, w_q, w_k, w_v, w_o):
        import math
        import jax, jax.numpy as jnp
        import numpy as np
        B, T, E = (2, 256, 128)
        H, DK, DV = (16, 64, 64)
        kq_dim = w_q.shape[-1]
        w_qk = jnp.einsum('HIO,HiO->HIi', w_q, w_k)
        w_vo = jnp.einsum('HIO,HOi->HIi', w_v, w_o)
        attention = jnp.einsum('HIi,BTI,Bti->BHTt', w_qk, x_query, x_key)
        attention = attention / math.sqrt(kq_dim)
        attention = jnp.where(mask, attention, -1e+30)
        attention = jax.nn.softmax(attention, axis=-1)
        output = jnp.einsum('HIi,BtI->BHti', w_vo, x_value)
        output = jnp.einsum('BHTt,BHtI->BTI', attention, output)
        return output

    def _L0_attn_ref(x, Wq, Wkv, Wout, lambda_q1, lambda_k1, lambda_q2, lambda_k2, gamma):
        import jax, jax.numpy as jnp
        import numpy as np
        import math
        H = 8
        D = 32
        DEPTH = 1
        LAMBDA_INIT = 0.8 - 0.6 * math.exp(-0.3 * DEPTH)
        EPS = 1e-08
        B, T, _ = x.shape
        scaling = D ** (-0.5)
        q = (x @ Wq).reshape(B, T, 2 * H, D).transpose(0, 2, 1, 3) * scaling
        kv = x @ Wkv
        k, v = jnp.split(kv, 2, axis=-1)
        k = k.reshape(B, T, 2 * H, D).transpose(0, 2, 1, 3)
        v = v.reshape(B, T, H, 2 * D).transpose(0, 2, 1, 3)
        dots = jnp.einsum('bhqd,bhkd->bhqk', q, k)
        attn_w = jax.nn.softmax(dots.astype(jnp.float32), axis=-1).astype(dots.dtype)
        lam1 = jnp.exp(jnp.sum(lambda_q1 * lambda_k1))
        lam2 = jnp.exp(jnp.sum(lambda_q2 * lambda_k2))
        lam = lam1 - lam2 + LAMBDA_INIT
        attn_w = attn_w.reshape(B, H, 2, T, T)
        attn_w = attn_w[:, :, 0] - lam * attn_w[:, :, 1]
        attn = jnp.einsum('bhqk,bhkd->bhqd', attn_w, v)
        rms = jnp.sqrt(jnp.mean(attn * attn, axis=-1, keepdims=True))
        attn = gamma * (attn / (rms + EPS))
        attn = attn * (1.0 - LAMBDA_INIT)
        attn = attn.transpose(0, 2, 1, 3).reshape(B, T, 2 * H * D)
        return attn @ Wout

    def _L0_ffn_ref(x, router_w, w_gate, w_up, w_down, sw_gate, sw_up, sw_down):
        import jax, jax.numpy as jnp
        import numpy as np
        D_MODEL = 128
        HIDDEN = 512
        NUM_ROUTED = 7
        TOP_K = 2

        def _swiglu(x_flat, wg, wu, wd):
            g = jnp.einsum('nd,edh->enh', x_flat, wg)
            u = jnp.einsum('nd,edh->enh', x_flat, wu)
            h = jax.nn.silu(g) * u
            return jnp.einsum('enh,ehd->end', h, wd)
        orig_shape = x.shape
        x_flat = x.reshape(-1, orig_shape[-1])
        N = x_flat.shape[0]
        logits = x_flat @ router_w.T
        top_vals, top_idx = jax.lax.top_k(logits, TOP_K)
        top_w = jax.nn.softmax(top_vals, axis=-1)
        combine = jnp.sum(jax.nn.one_hot(top_idx, NUM_ROUTED, dtype=x.dtype) * top_w[..., None], axis=1)
        routed_out = _swiglu(x_flat, w_gate, w_up, w_down)
        mixed = jnp.einsum('end,ne->nd', routed_out, combine)
        shared_out = _swiglu(x_flat, sw_gate, sw_up, sw_down)
        mixed = mixed + jnp.mean(shared_out, axis=0)
        return mixed.reshape(orig_shape)
    x = x + _L0_xattn_ref(_layernorm(x, axis=-1), ctx_1024, ctx_1024, mask_Bx1xSxS2_bf1, L0_xattn_w_q, L0_xattn_w_k, L0_xattn_w_v, L0_xattn_w_o)
    x = x + _L0_attn_ref(_layernorm(x, axis=-1), L0_attn_Wq, L0_attn_Wkv, L0_attn_Wout, L0_attn_lambda_q1, L0_attn_lambda_k1, L0_attn_lambda_q2, L0_attn_lambda_k2, L0_attn_gamma)
    x = x + _L0_ffn_ref(_layernorm(x, axis=-1), L0_ffn_router_w, L0_ffn_w_gate, L0_ffn_w_up, L0_ffn_w_down, L0_ffn_sw_gate, L0_ffn_sw_up, L0_ffn_sw_down)
    return x

_drawn_inputs = setup_inputs


def setup_inputs(seed=0):
    import zlib

    import numpy as np

    out = dict(_drawn_inputs(seed))
    spreads = {'L0_attn_gamma': (1.0, 0.2)}
    factors = {'L0_attn_lambda_k1': 3.31,
     'L0_attn_lambda_q2': 6.09,
     'L0_attn_lambda_k2': 5.824,
     'L0_ffn_router_w': 8.0,
     'L0_ffn_w_gate': 8.0,
     'L0_ffn_w_up': 8.0,
     'L0_ffn_w_down': 8.0,
     'L0_ffn_sw_gate': 6.406,
     'L0_ffn_sw_up': 6.356,
     'L0_ffn_sw_down': 6.375}
    for name, (base, spread) in spreads.items():
        noise = np.random.default_rng([zlib.crc32(name.encode()), seed]).standard_normal(out[name].shape)
        drawn = base * np.exp(spread * noise) if base else spread * noise
        out[name] = jnp.asarray(drawn.astype(out[name].dtype))
    for name, factor in factors.items():
        out[name] = (out[name] * factor).astype(out[name].dtype)
    return out
```

```python
import math
from contextlib import ExitStack

import numpy as np

import concourse.bass as bass
from concourse import mybir

F32 = mybir.dt.float32
BF16 = mybir.dt.bfloat16
U8 = mybir.dt.uint8
ALU = mybir.AluOpType
ACT = mybir.ActivationFunctionType
AX = mybir.AxisListType

P = 128
B, T, E = 64, 32, 128
S2 = 257
H, DK = 16, 64
TOK = B * T
NG = TOK // P
GB = P // T
NT = H * T // P
HT = H // NT
CH = (S2 - 1) // P
PACK = CH * P + S2
XSCALE = 1.0 / math.sqrt(DK)
MASKED = -8e30

DH, DD = 8, 32
NC = 2 * DH
DE = 2 * DH * DD
LAMBDA_INIT = 0.8 - 0.6 * math.exp(-0.3 * 1)

NE, HID = 8, 512
NR = NE - 1
KT = HID // P
LN_EPS = 1e-5
RMS_EPS = 1e-8
LOW = -3.0e38


class Shared:
    pass


def early(n, k):
    return isinstance(n, int) and n < k


def layer_norm(nc, m, tag):
    with ExitStack() as ctx:
        mean_ready = ctx.enter_context(nc.semaphore(f"{tag}_mean_ready"))
        centred = ctx.enter_context(nc.semaphore(f"{tag}_centred"))
        squared = ctx.enter_context(nc.semaphore(f"{tag}_squared"))
        var_ready = ctx.enter_context(nc.semaphore(f"{tag}_var_ready"))
        std_ready = ctx.enter_context(nc.semaphore(f"{tag}_std_ready"))
        normed = ctx.enter_context(nc.semaphore(f"{tag}_normed"))
        turned = ctx.enter_context(nc.semaphore(f"{tag}_turned"))
        turned_out = ctx.enter_context(nc.semaphore(f"{tag}_turned_out"))
        block = ctx.enter_context(nc.Block())

        @block.vector
        def _(dve):
            if tag == "ln1":
                dve.wait_ge(m.x_loaded, 16)
            nc.vector.tensor_reduce(m.stat[:, 0, :], m.x[:], AX.X, ALU.add).then_inc(mean_ready, 1)
            dve.wait_ge(mean_ready, 1)
            nc.vector.tensor_scalar(m.stat[:, 1, :], m.stat[:, 0, :], 1.0 / E, None, ALU.mult).then_inc(mean_ready, 1)
            dve.wait_ge(mean_ready, 2)
            nc.vector.tensor_tensor(m.xn[:], m.x[:], m.stat[:, 1, :].unsqueeze(2).to_broadcast([P, NG, E]),
                                    ALU.subtract).then_inc(centred, 1)
            dve.wait_ge(squared, 1)
            nc.vector.tensor_reduce(m.stat[:, 0, :], m.sq[:], AX.X, ALU.add).then_inc(var_ready, 1)
            dve.wait_ge(var_ready, 1)
            nc.vector.tensor_scalar(m.stat[:, 1, :], m.stat[:, 0, :], 1.0 / E, LN_EPS, ALU.mult,
                                    ALU.add).then_inc(var_ready, 1)
            dve.wait_ge(std_ready, 1)
            nc.vector.reciprocal(m.stat[:, 3, :], m.stat[:, 2, :]).then_inc(std_ready, 1)
            dve.wait_ge(std_ready, 2)
            for k in range(NG // 4):
                part = slice(4 * k, 4 * k + 4)
                nc.vector.tensor_tensor(m.xn[:, part, :], m.xn[:, part, :],
                                        m.stat[:, 3, part].unsqueeze(2).to_broadcast([P, 4, E]),
                                        ALU.mult).then_inc(normed, 1)

        @block.scalar
        def _(act):
            act.wait_ge(centred, 1)
            nc.scalar.activation(m.sq[:], m.xn[:], ACT.Square).then_inc(squared, 1)
            act.wait_ge(var_ready, 2)
            nc.scalar.activation(m.stat[:, 2, :], m.stat[:, 1, :], ACT.Sqrt).then_inc(std_ready, 1)
            for k in range(NG // 4):
                act.wait_ge(turned, k + 1)
                nc.scalar.copy(m.xT[:, 4 * P * k:4 * P * (k + 1)], m.bank[k % 2][:]).then_inc(turned_out, 1)

        @block.tensor
        def _(pe):
            if tag == "ln1":
                pe.wait_ge(m.consts_loaded, 16)
            for k in range(NG // 4):
                pe.wait_ge(normed, k + 1)
                if k >= 2:
                    pe.wait_ge(turned_out, k - 1)
                for j in range(4):
                    last = nc.tensor.transpose(m.bank[k % 2][:, j * P:(j + 1) * P], m.xn[:, 4 * k + j, :],
                                               m.ident)
                last.then_inc(turned, 1)


def fold_weights(nc, m):
    jobs = ([(m.w_qk, hb, m.aw, 0, 1, DK) for hb in range(4)] + [(m.w_vo, hb, m.aw, 2, 3, DK) for hb in range(4)]
            + [(m.w_dd, hb, m.dw, 0, 1, DD) for hb in range(4)])
    with ExitStack() as ctx:
        folded = ctx.enter_context(nc.semaphore("folded"))
        folded_out = [ctx.enter_context(nc.semaphore(f"folded_out{k}")) for k in range(2)]
        v_row = ctx.enter_context(nc.semaphore("v_row"))
        v_row_out = ctx.enter_context(nc.semaphore("v_row_out"))
        lam_step = ctx.enter_context(nc.semaphore("lam_step"))
        lam_exp = ctx.enter_context(nc.semaphore("lam_exp"))
        block = ctx.enter_context(nc.Block())

        @block.tensor
        def _(pe):
            pe.wait_ge(m.aw_loaded, 32)
            for n, (_, hb, w, a, b, rows) in enumerate(jobs):
                if n >= 4:
                    pe.wait_ge(folded_out[n % 2], (n - 4) // 2 + 1)
                for j in range(4):
                    h = 4 * hb + j
                    last = nc.tensor.matmul(m.bank[n % 4][:, j * P:(j + 1) * P], w[0:rows, a, h, :],
                                            w[0:rows, b, h, :], start=True, stop=True)
                last.then_inc(folded, 1)
            pe.wait_ge(folded_out[0], 6)
            pe.wait_ge(folded_out[1], 6)
            for hb in range(4):
                nc.tensor.matmul(m.bank[4 + hb][0:B, :], m.last_row[:], m.w_vo[:, 4 * hb:4 * hb + 4, :],
                                 start=True, stop=True).then_inc(v_row, 1)

        def copy_out(eng, copy, k):
            for n, (dst, hb, *_) in enumerate(jobs):
                if n % 2 == k:
                    eng.wait_ge(folded, n + 1)
                    copy(dst[:, 4 * hb:4 * hb + 4, :], m.bank[n % 4][:]).then_inc(folded_out[k], 1)

        @block.scalar
        def _(act):
            copy_out(act, nc.scalar.copy, 0)
            act.wait_ge(lam_step, 2)
            nc.scalar.activation(m.lam[:, 2:4], m.lam[:, 0:2], ACT.Exp).then_inc(lam_exp, 1)

        @block.vector
        def _(dve):
            copy_out(dve, nc.vector.tensor_copy, 1)
            for hb in range(4):
                dve.wait_ge(v_row, hb + 1)
                nc.vector.tensor_copy(m.v_rows[:, hb, :], m.bank[4 + hb][0:B, :]).then_inc(v_row_out, 1)
            nc.vector.tensor_tensor(m.lam_prod[:], m.lam_in[:, 0:2, :], m.lam_in[:, 2:4, :], ALU.mult).then_inc(lam_step, 1)
            dve.wait_ge(lam_step, 1)
            nc.vector.tensor_reduce(m.lam[:, 0:2], m.lam_prod[:], AX.X, ALU.add).then_inc(lam_step, 1)
            dve.wait_ge(lam_exp, 1)
            nc.vector.tensor_tensor(m.lam[:, 4:5], m.lam[:, 3:4], m.lam[:, 2:3], ALU.subtract).then_inc(lam_step, 1)
            dve.wait_ge(lam_step, 3)
            nc.vector.tensor_scalar(m.pair_factor[:, 1:2], m.lam[:, 4:5], -LAMBDA_INIT, None, ALU.add).then_inc(lam_step, 1)
            nc.vector.tensor_scalar(m.gamma[:], m.gamma_in[:], 1.0 - LAMBDA_INIT, None, ALU.mult).then_inc(lam_step, 1)
            dve.wait_ge(lam_step, 5)
            nc.vector.tensor_scalar(m.w_out[:], m.w_out[:], m.gamma[:, 0:1], None, ALU.mult)

        @block.gpsimd
        def _(pool):
            pool.memset(m.pair_factor[:, 0:1], 1.0)
            pool.wait_ge(m.mask_loaded, 16)
            for k in range(4):
                part = slice(NG // 4 * k, NG // 4 * (k + 1))
                pool.tensor_scalar(m.mask_add[:, part, :], m.mask_in[:, part, :], -MASKED, MASKED, ALU.mult, ALU.add)

        @block.sync
        def _(sp):
            sp.wait_ge(v_row_out, 4)
            sp.dma_start(m.v_scratch[:, :], m.v_rows[:].rearrange("b a n -> b (a n)")).then_inc(m.v_stored, 16)
            sp.wait_ge(m.v_stored, 16)


def cross_attention(nc, m, ctx_pack):
    with ExitStack() as ctx:
        def sb(name, shape, dt=F32):
            return ctx.enter_context(nc.sbuf_tensor(name, shape, dt))

        def sem(name):
            return ctx.enter_context(nc.semaphore(name))

        cx = sb("cx", [P, GB, PACK])
        q = sb("q", [P, 2, GB, H, T])
        probs = sb("probs", [P, 2, NT, S2])
        probsT = sb("probsT", [P, 2, CH, H * T])
        mixed = sb("mixed", [P, 2, H, GB, T])
        row_top = sb("row_top", [P, 2, NT])
        row_max = sb("row_max", [P, 2, NT])
        row_sum = sb("row_sum", [P, 2, NT])
        row_inv = sb("row_inv", [P, 2, NT])
        last_p = sb("last_p", [P, 2, NT, GB])
        last_pd = sb("last_pd", [NT * GB, HT, GB, T])
        v_last = sb("v_last", [NT * GB, 2, HT * E])

        cx_loaded = [sem(f"cx_loaded{s}") for s in range(GB)]
        v_loaded = [sem(f"v_loaded{s}") for s in range(2)]
        scores_ready = sem("scores_ready")
        max_ready = sem("max_ready")
        max_step = sem("max_step")
        exp_done = sem("exp_done")
        inv_ready = sem("inv_ready")
        probs_ready = sem("probs_ready")
        last_p_ready = sem("last_p_ready")
        probsT_ready = sem("probsT_ready")
        probsT_out0 = sem("probsT_out0")
        probsT_out1 = sem("probsT_out1")
        mixed_ready = sem("mixed_ready")
        mixed_out = sem("mixed_out")
        q_ready = sem("q_ready")
        q_out = sem("q_out")
        last_t_ready = sem("last_t_ready")
        last_pd_ready = sem("last_pd_ready")
        out_ready = sem("out_ready")
        out_added = sem("out_added")

        scores = m.scores
        pt_bank = m.bank[4:6]
        mixed_bank = m.bank[6]
        q_bank = m.bank[7]

        UN = 8
        LOOPS = (B - UN) // UN
        TAIL = range(B - UN + 1, B)

        block = ctx.enter_context(nc.Block())

        @block.sync
        def _(sp):
            def load_context(n, slot):
                sp.dma_start(cx[:, slot, :], ctx_pack[n, :, :]).then_inc(cx_loaded[slot], 16)

            def load_last(g, slot):
                for a in range(NT):
                    sp.dma_start(v_last[GB * a:GB * (a + 1), slot, :],
                                 m.v_scratch[bass.ds(g * GB, GB), HT * E * a:HT * E * (a + 1)]).then_inc(v_loaded[slot], 16)

            for s in range(GB):
                load_context(s, s)
            load_last(0, 0)
            load_last(1, 1)

            def load_group(g):
                for s in range(GB):
                    sp.wait_ge(mixed_ready, g * GB + (s - GB + 1))
                    load_context(g * GB + s, s)

            load_group(1)
            with sp.Fori(1, NG // 2) as k:
                for s in range(2):
                    load_group(k * 2 + s)
                    sp.wait_ge(out_ready, k * 2 + (s - 1))
                    load_last(k * 2 + s, s)

        @block.tensor
        def _(pe):
            def score_tiles(n, par, slot, group):
                pe.wait_ge(cx_loaded[slot], group * 16 + 16)
                if slot == 0:
                    pe.wait_ge(q_out, group * 4 + 4)
                for pair in range(2):
                    if not early(n, 1):
                        pe.wait_ge(exp_done, n * NT - NT + 2 * pair + 2)
                    for g in (2 * pair, 2 * pair + 1):
                        nc.tensor.matmul(scores[:, g, 0:S2], q[:, par, slot, HT * g:HT * (g + 1), :],
                                         cx[:, slot, CH * P:PACK], start=True, stop=False)
                        last = nc.tensor.matmul(scores[:, g, 0:S2], m.spread[:, slot, :],
                                                m.mask_add[:, group, :], start=False, stop=True)
                    last.then_inc(scores_ready, 1)

            def queries(group, hb):
                for j in range(4):
                    last = nc.tensor.matmul(q_bank[:, j * P:(j + 1) * P], m.w_qk[:, 4 * hb + j, :],
                                            m.xT[:, bass.ts(group, P)], start=True, stop=True)
                last.then_inc(q_ready, 1)

            def transposes(n, par):
                pe.wait_ge(probs_ready, n + 1)
                for c in range(CH):
                    if not early(n, 1):
                        pe.wait_ge((probsT_out0, probsT_out1)[c], n)
                    for g in range(NT):
                        last = nc.tensor.transpose(pt_bank[c][:, g * P:(g + 1) * P], probs[:, par, g, c * P:(c + 1) * P],
                                                   m.ident)
                    last.then_inc(probsT_ready, 1)

            def product(n, par, slot):
                pe.wait_ge(probsT_out0, n + 1)
                pe.wait_ge(probsT_out1, n + 1)
                if not early(n, 1):
                    pe.wait_ge(mixed_out, n)
                for c in range(CH):
                    last = nc.tensor.matmul(mixed_bank[:], cx[:, slot, c * P:(c + 1) * P], probsT[:, par, c, :],
                                            start=(c == 0), stop=(c == CH - 1))
                last.then_inc(mixed_ready, 1)

            def last_transpose(group, par):
                pe.wait_ge(last_p_ready, group * GB + GB)
                nc.tensor.transpose(q_bank[0:NT * GB, 0:P], last_p[:, par, :, :], m.ident).then_inc(last_t_ready, 1)

            def output(group, par):
                pe.wait_ge(mixed_out, group * GB + GB)
                pe.wait_ge(last_pd_ready, group + 1)
                pe.wait_ge(v_loaded[par], group * 32 + (64 - 32 * par))
                for h in range(H):
                    nc.tensor.matmul(q_bank[:, 0:E], mixed[:, par, h, :, :], m.w_vo[:, h, :], start=(h == 0), stop=False)
                for j in range(HT):
                    last = nc.tensor.matmul(q_bank[:, 0:E], last_pd[:, j, :, :], v_last[:, par, j * E:(j + 1) * E],
                                            start=False, stop=(j == HT - 1))
                last.then_inc(out_ready, 1)

            def step(n, u, group, tail):
                s = (1 + u) % UN
                gpar = s // GB % 2
                if not tail or n + 1 < B:
                    nslot = (s + 1) % GB
                    score_tiles(n + 1, (s + 1) // GB % 2, nslot, group + (1 if nslot == 0 else 0))
                product(n - 1, (s - 1) % 2, (s - 1) % GB)
                j = s % GB
                made = group * 4 + (5 + j)
                more = not tail or made < 4 * NG
                if j == 0:
                    pe.wait_ge(q_out, made if more else 4 * NG)
                    last_transpose(group - 1, 1 - gpar)
                if more:
                    if j == 0:
                        pe.wait_ge(last_pd_ready, group)
                    if j == 1 and not early(group, 1):
                        pe.wait_ge(out_added, group)
                    pe.wait_ge(q_out, made)
                    queries(group + (2 if j == 3 else 1), (j + 1) % 4)
                transposes(n, s % 2)
                if j == 0:
                    if more:
                        pe.wait_ge(q_out, made + 1)
                    output(group - 1, 1 - gpar)

            for hb in range(4):
                if hb:
                    pe.wait_ge(q_out, hb)
                queries(0, hb)
            score_tiles(0, 0, 0, 0)
            score_tiles(1, 0, 1, 0)
            for hb in range(2):
                pe.wait_ge(q_out, 4 + hb)
                queries(1, hb)
            transposes(0, 0)
            for n in range(1, UN + 1):
                step(n, n - 1, n // GB, False)
            with pe.Fori(1, LOOPS) as i:
                for u in range(UN):
                    step(i * UN + (1 + u), u, i * (UN // GB) + (1 + u) // GB, False)
            for n in TAIL:
                step(n, (n - 1) % UN, n // GB, True)
            product(B - 1, 1, GB - 1)
            pe.wait_ge(out_added, NG - 1)
            last_transpose(NG - 1, 1)
            output(NG - 1, 1)

        @block.scalar
        def _(act):
            def queries_out(gpar, hb, count):
                act.wait_ge(q_ready, count)
                nc.scalar.copy(q[:, gpar, :, 4 * hb:4 * hb + 4, :].rearrange("p b h t -> p h b t"),
                               q_bank[:].rearrange("p (h b t) -> p h b t", h=4, b=GB)).then_inc(q_out, 1)

            def exponentials(n, par):
                act.wait_ge(max_ready, n + 1)
                if not early(n, 2):
                    act.wait_ge(probsT_ready, (n - 1) * 2)
                    act.wait_ge(last_p_ready, n - 1)
                for g in range(NT):
                    nc.scalar.activation(probs[:, par, g, :], scores[:, g, 0:S2], ACT.Exp, bias=row_max[:, par, g:g + 1],
                                         scale=XSCALE, accum_out=row_sum[:, par, g:g + 1]).then_inc(exp_done, 1)

            def chunk_out(n, par):
                act.wait_ge(probsT_ready, n * 2 + 1)
                if not early(n, 2):
                    act.wait_ge(mixed_ready, n - 1)
                nc.scalar.copy(probsT[:, par, 0, :], pt_bank[0][:]).then_inc(probsT_out0, 1)

            def step(n, u, group, tail):
                s = (1 + u) % UN
                if not tail or n + 1 < B:
                    exponentials(n + 1, (s + 1) % 2)
                j = s % GB
                made = group * 4 + (5 + j)
                if not tail or made < 4 * NG:
                    queries_out((s // GB + (2 if j == 3 else 1)) % 2, (j + 1) % 4, made + 1)
                chunk_out(n, s % 2)

            for hb in range(4):
                queries_out(0, hb, hb + 1)
            exponentials(0, 0)
            exponentials(1, 1)
            queries_out(1, 0, 5)
            queries_out(1, 1, 6)
            chunk_out(0, 0)
            for n in range(1, UN + 1):
                step(n, n - 1, n // GB, False)
            with act.Fori(1, LOOPS) as i:
                for u in range(UN):
                    step(i * UN + (1 + u), u, i * (UN // GB) + (1 + u) // GB, False)
            for n in TAIL:
                step(n, (n - 1) % UN, n // GB, True)

        @block.vector
        def _(dve):
            def maxima(n, par):
                for pair in range(2):
                    dve.wait_ge(scores_ready, n * 2 + (pair + 1))
                    nc.vector.tensor_reduce(row_top[:, par, 2 * pair:2 * pair + 2], scores[:, 2 * pair:2 * pair + 2, 0:S2],
                                            AX.X, ALU.max).then_inc(max_step, 1)
                dve.wait_ge(max_step, n * 2 + 2)
                nc.vector.tensor_scalar(row_max[:, par, :], row_top[:, par, :], -XSCALE, None, ALU.mult).then_inc(max_ready, 1)

            def inverses(n, par):
                dve.wait_ge(exp_done, n * NT + NT)
                nc.vector.reciprocal(row_inv[:, par, :], row_sum[:, par, :]).then_inc(inv_ready, 1)

            def chunk_out(n, par):
                dve.wait_ge(probsT_ready, n * 2 + 2)
                if not early(n, 2):
                    dve.wait_ge(mixed_ready, n - 1)
                nc.vector.tensor_copy(probsT[:, par, 1, :], pt_bank[1][:]).then_inc(probsT_out1, 1)

            def product_out(n, gpar, slot):
                dve.wait_ge(mixed_ready, n + 1)
                nc.vector.tensor_copy(mixed[:, gpar, :, slot, :], mixed_bank[:].rearrange("p (h t) -> p h t", h=H)).then_inc(mixed_out, 1)

            def spread_last(group):
                dve.wait_ge(last_t_ready, group + 1)
                nc.vector.tensor_tensor(last_pd[:],
                                        q_bank[0:NT * GB, 0:P].rearrange("p (h t) -> p h t", h=HT).unsqueeze(2).to_broadcast([NT * GB, HT, GB, T]),
                                        m.own_entry[:].unsqueeze(1).unsqueeze(3).to_broadcast([NT * GB, HT, GB, T]),
                                        ALU.mult).then_inc(last_pd_ready, 1)

            def add_output(group):
                dve.wait_ge(out_ready, group + 1)
                nc.vector.tensor_tensor(m.x[:, group, :], m.x[:, group, :], q_bank[:, 0:E], ALU.add).then_inc(out_added, 1)

            def step(n, u, group, tail):
                s = (1 + u) % UN
                if not tail or n + 1 < B:
                    maxima(n + 1, (s + 1) % 2)
                product_out(n - 1, (s - 1) % UN // GB, (s - 1) % GB)
                if s % GB == 0:
                    spread_last(group - 1)
                if not tail or n + 1 < B:
                    inverses(n + 1, (s + 1) % 2)
                chunk_out(n, s % 2)
                if s % GB == 0:
                    add_output(group - 1)

            maxima(0, 0)
            inverses(0, 0)
            maxima(1, 1)
            inverses(1, 1)
            chunk_out(0, 0)
            for n in range(1, UN + 1):
                step(n, n - 1, n // GB, False)
            with dve.Fori(1, LOOPS) as i:
                for u in range(UN):
                    step(i * UN + (1 + u), u, i * (UN // GB) + (1 + u) // GB, False)
            for n in TAIL:
                step(n, (n - 1) % UN, n // GB, True)
            product_out(B - 1, 1, GB - 1)
            spread_last(NG - 1)
            add_output(NG - 1)

        @block.gpsimd
        def _(pool):
            def normalise(n, par, group, gpar, slot):
                pool.wait_ge(inv_ready, n + 1)
                if not early(n, 2 * GB):
                    pool.wait_ge(last_t_ready, group - 1)
                pool.tensor_tensor(last_p[:, gpar, :, slot], probs[:, par, :, S2 - 1], row_inv[:, par, :],
                                   ALU.mult).then_inc(last_p_ready, 1)
                pool.tensor_tensor(probs[:, par, :, 0:S2 - 1], probs[:, par, :, 0:S2 - 1],
                                   row_inv[:, par, :].unsqueeze(2).to_broadcast([P, NT, S2 - 1]), ALU.mult).then_inc(probs_ready, 1)

            for n in range(UN):
                normalise(n, n % 2, n // GB, n // GB, n % GB)
            with pool.Fori(1, B // UN) as i:
                for u in range(UN):
                    normalise(i * UN + u, u % 2, i * (UN // GB) + u // GB, u // GB, u % GB)


def differential_attention(nc, m):
    with ExitStack() as ctx:
        def sb(name, shape, dt=F32):
            return ctx.enter_context(nc.sbuf_tensor(name, shape, dt))

        def sem(name):
            return ctx.enter_context(nc.semaphore(name))

        xg = sb("d_xg", [P, 2, P])
        q = sb("d_q", [P, GB, NC, T])
        v = sb("d_v", [P, 2, DE])
        e = sb("d_e", [P, 2, GB * 4, T])
        diff = sb("d_diff", [P, 2, 2, GB, T])
        wT = sb("d_wT", [P, 2, DH, GB, T])
        mx = sb("d_mx", [P, 2, GB * 4])
        sm = sb("d_sm", [P, 2, GB * 4])
        rc = sb("d_rc", [P, 2, GB * 4])
        rf = sb("d_rf", [P, 2, GB * 4])

        xg_ready = sem("d_xg_ready")
        q_ready = sem("d_q_ready")
        q_out = sem("d_q_out")
        q_out2 = sem("d_q_out2")
        v_ready = sem("d_v_ready")
        v_out = sem("d_v_out")
        scores_ready = sem("d_scores_ready")
        max_ready = sem("d_max_ready")
        shifted = sem("d_shifted")
        exp_done = sem("d_exp_done")
        summed = sem("d_summed")
        scaled = sem("d_scaled")
        diff_ready = sem("d_diff_ready")
        diffT_ready = sem("d_diffT_ready")
        wT_zero = sem("d_wT_zero")
        wT_out = sem("d_wT_out")
        att_ready = sem("d_att_ready")
        att_out = sem("d_att_out")

        qb = [m.bank[0], m.bank[1]]
        vb, sb_, tb, ab = m.bank[2], m.bank[3], m.bank[4], m.bank[5]
        block = ctx.enter_context(nc.Block())

        @block.gpsimd
        def _(pool):
            for k in range(2):
                pool.memset(wT[:, k], 0.0).then_inc(wT_zero, 1)

            def stage(g, par):
                pool.tensor_copy(xg[:, par, :], m.xT[:, bass.ts(g, P)]).then_inc(xg_ready, 1)

            def difference(g, par):
                pool.wait_ge(summed, g * 3 + 3)
                pool.tensor_tensor(e[:, par], e[:, par], rf[:, par].unsqueeze(2).to_broadcast([P, GB * 4, T]),
                                   ALU.mult).then_inc(scaled, 1)
                pool.wait_ge(scaled, g + 1)
                if not early(g, 2):
                    pool.wait_ge(diffT_ready, g - 1)
                ev = e[:, par].rearrange("p (b c u) k -> p c u b k", b=GB, c=2)
                pool.tensor_tensor(diff[:, par], ev[:, 0], ev[:, 1], ALU.add).then_inc(diff_ready, 1)

            stage(0, 0)
            stage(1, 1)
            difference(0, 0)
            pool.wait_ge(scores_ready, 1)
            stage(2, 0)
            difference(1, 1)

            def step(g, par):
                pool.wait_ge(scores_ready, g)
                stage(g + 1, 1 - par)
                difference(g, par)

            with pool.Fori(1, NG // 2 - 1) as k:
                for par in range(2):
                    step(k * 2 + par, par)
            step(NG - 2, 0)
            difference(NG - 1, 1)

        @block.tensor
        def _(pe):
            def front(g, par):
                pe.wait_ge(xg_ready, g + 1)
                for hb in range(4):
                    if not (early(g, 1) and hb < 2):
                        pe.wait_ge((q_out, q_out2)[hb % 2], g * 2 + hb // 2)
                    for j in range(4):
                        last = nc.tensor.matmul(qb[hb % 2][:, j * P:(j + 1) * P], m.w_dd[:, 4 * hb + j, :], xg[:, par, :],
                                                start=True, stop=True)
                    last.then_inc(q_ready, 1)
                if not early(g, 1):
                    pe.wait_ge(v_out, g)
                nc.tensor.matmul(vb[:], xg[:, par, :], m.w_v[:], start=True, stop=True).then_inc(v_ready, 1)

            def scores(g, par):
                pe.wait_ge(q_out, g * 2 + 2)
                pe.wait_ge(q_out2, g * 2 + 2)
                if not early(g, 1):
                    pe.wait_ge(shifted, g)
                for b in range(GB):
                    for cu in range(4):
                        col = (b * 4 + cu) * T
                        last = nc.tensor.matmul(sb_[:, col:col + T], q[:, b, 4 * cu:4 * cu + 4, :],
                                                xg[:, par, b * T:(b + 1) * T], start=True, stop=True)
                last.then_inc(scores_ready, 1)

            def back(g, par):
                pe.wait_ge(diff_ready, g + 1)
                if not early(g, 1):
                    pe.wait_ge(wT_out, g)
                for u in range(2):
                    last = nc.tensor.transpose(tb[:, u * P:(u + 1) * P], diff[:, par, u].rearrange("p b k -> p (b k)"), m.ident)
                last.then_inc(diffT_ready, 1)

            def products(g, par):
                pe.wait_ge(wT_out, g + 1)
                pe.wait_ge(v_out, g + 1)
                if not early(g, 1):
                    pe.wait_ge(att_out, g)
                for h in range(DH):
                    last = nc.tensor.matmul(ab[:, 2 * DD * h:2 * DD * (h + 1)], wT[:, par, h], v[:, par, 2 * DD * h:2 * DD * (h + 1)],
                                            start=True, stop=True)
                last.then_inc(att_ready, 1)

            front(0, 0)
            scores(0, 0)
            front(1, 1)
            back(0, 0)
            scores(1, 1)
            products(0, 0)
            with pe.Fori(1, NG // 2) as k:
                for par in range(2):
                    g = k * 2 + par
                    front(g, par)
                    back(g - 1, 1 - par)
                    scores(g, par)
                    products(g - 1, 1 - par)
            back(NG - 1, 1)
            products(NG - 1, 1)

        def query_copy(copy, par, hb):
            return copy(q[:, :, 4 * hb:4 * hb + 4, :].rearrange("p b h t -> p h b t"),
                        qb[hb % 2][:].rearrange("p (h b t) -> p h b t", h=4, b=GB))

        @block.scalar
        def _(act):
            def front(g, par):
                for hb in (0, 2):
                    act.wait_ge(q_ready, g * 4 + hb + 1)
                    if not early(g, 1):
                        act.wait_ge(scores_ready, g)
                    query_copy(nc.scalar.copy, par, hb).then_inc(q_out, 1)
                act.wait_ge(v_ready, g + 1)
                if not early(g, 2):
                    act.wait_ge(att_ready, g - 1)
                nc.scalar.copy(v[:, par, :], vb[:]).then_inc(v_out, 1)

            def exponentials(g, par):
                act.wait_ge(shifted, g + 1)
                nc.scalar.activation(e[:, par], e[:, par], ACT.Exp, scale=DD ** -0.5).then_inc(exp_done, 1)

            def result_out(g):
                act.wait_ge(att_ready, g + 1)
                nc.scalar.copy(m.att[:, g, :], ab[:]).then_inc(att_out, 1)

            front(0, 0)
            exponentials(0, 0)
            front(1, 1)
            exponentials(1, 1)
            result_out(0)
            with act.Fori(1, NG // 2) as k:
                for par in range(2):
                    g = k * 2 + par
                    front(g, par)
                    exponentials(g, par)
                    result_out(g - 1)
            result_out(NG - 1)

        @block.vector
        def _(dve):
            dve.wait_ge(wT_zero, 2)

            def front(g, par):
                for hb in (1, 3):
                    dve.wait_ge(q_ready, g * 4 + hb + 1)
                    if not early(g, 1):
                        dve.wait_ge(scores_ready, g)
                    query_copy(nc.vector.tensor_copy, par, hb).then_inc(q_out2, 1)

            def softmax_front(g, par):
                dve.wait_ge(scores_ready, g + 1)
                if not early(g, 2):
                    dve.wait_ge(diff_ready, g - 1)
                bank = sb_[:].rearrange("p (a k) -> p a k", k=T)
                nc.vector.tensor_reduce(mx[:, par], bank, AX.X, ALU.max).then_inc(max_ready, 1)
                dve.wait_ge(max_ready, g + 1)
                nc.vector.tensor_tensor(e[:, par], bank, mx[:, par].unsqueeze(2).to_broadcast([P, GB * 4, T]),
                                        ALU.subtract).then_inc(shifted, 1)

            def softmax_back(g, par):
                dve.wait_ge(exp_done, g + 1)
                nc.vector.tensor_reduce(sm[:, par], e[:, par], AX.X, ALU.add).then_inc(summed, 1)
                dve.wait_ge(summed, g * 3 + 1)
                nc.vector.reciprocal(rc[:, par], sm[:, par]).then_inc(summed, 1)
                dve.wait_ge(summed, g * 3 + 2)
                nc.vector.tensor_tensor(rf[:, par].rearrange("p (b c u) -> p b c u", b=GB, c=2),
                                        rc[:, par].rearrange("p (b c u) -> p b c u", b=GB, c=2),
                                        m.pair_factor[:].unsqueeze(1).unsqueeze(3).to_broadcast([P, GB, 2, 2]),
                                        ALU.mult).then_inc(summed, 1)

            def blocks_out(g, par):
                dve.wait_ge(diffT_ready, g + 1)
                if not early(g, 2):
                    dve.wait_ge(att_ready, g - 1)
                for b in range(GB):
                    rows = slice(T * b, T * (b + 1))
                    last = nc.vector.tensor_copy(wT[rows, par, :, b, :], tb[rows, 0:2 * P].rearrange("p (h t) -> p h t", h=DH))
                last.then_inc(wT_out, 1)

            front(0, 0)
            softmax_front(0, 0)
            softmax_back(0, 0)
            front(1, 1)
            blocks_out(0, 0)
            softmax_front(1, 1)
            softmax_back(1, 1)
            with dve.Fori(1, NG // 2) as k:
                for par in range(2):
                    g = k * 2 + par
                    front(g, par)
                    blocks_out(g - 1, 1 - par)
                    softmax_front(g, par)
                    softmax_back(g, par)
            blocks_out(NG - 1, 1)


def attention_output(nc, m):
    W = 2 * DD
    with ExitStack() as ctx:
        def sem(name):
            return ctx.enter_context(nc.semaphore(name))

        an = ctx.enter_context(nc.sbuf_tensor("o_an", [P, 2, DE], F32))
        anT = ctx.enter_context(nc.sbuf_tensor("o_anT", [P, 2, DE], F32))
        ss = ctx.enter_context(nc.sbuf_tensor("o_ss", [P, 4, NG * DH], F32))
        sq = ctx.enter_context(nc.sbuf_tensor("o_sq", [P, 2, 4, DE], F32))
        squared = sem("o_squared")
        summed = sem("o_summed")
        root = sem("o_root")
        inv = sem("o_inv")
        an_ready = sem("o_an_ready")
        anT_ready = sem("o_anT_ready")
        anT_out = sem("o_anT_out")
        out_ready = sem("o_out_ready")
        added = sem("o_added")
        tb = m.bank[0:2]
        ob = m.bank[2:4]
        block = ctx.enter_context(nc.Block())

        @block.scalar
        def _(act):
            for k in range(NG // 4):
                if k >= 2:
                    act.wait_ge(summed, k - 1)
                nc.scalar.activation(sq[:, k % 2], m.att[:, 4 * k:4 * k + 4, :], ACT.Square).then_inc(squared, 1)
            act.wait_ge(summed, NG // 4 + 1)
            nc.scalar.activation(ss[:, 2], ss[:, 1], ACT.Sqrt).then_inc(root, 1)

            def turned_out(g, par):
                act.wait_ge(anT_ready, g + 1)
                if not early(g, 2):
                    act.wait_ge(out_ready, g - 1)
                nc.scalar.copy(anT[:, par, :], tb[par][:]).then_inc(anT_out, 1)

            turned_out(0, 0)
            turned_out(1, 1)
            with act.Fori(1, NG // 2) as k:
                for par in range(2):
                    turned_out(k * 2 + par, par)

        @block.vector
        def _(dve):
            for k in range(NG // 4):
                dve.wait_ge(squared, k + 1)
                nc.vector.tensor_reduce(ss[:, 0, 4 * DH * k:4 * DH * (k + 1)], sq[:, k % 2].rearrange("p a (h w) -> p (a h) w", w=W),
                                        AX.X, ALU.add).then_inc(summed, 1)
            dve.wait_ge(summed, NG // 4)
            nc.vector.tensor_scalar(ss[:, 1], ss[:, 0], 1.0 / W, None, ALU.mult).then_inc(summed, 1)
            dve.wait_ge(root, 1)
            nc.vector.tensor_scalar(ss[:, 3], ss[:, 2], RMS_EPS, None, ALU.add).then_inc(inv, 1)
            dve.wait_ge(inv, 1)
            nc.vector.reciprocal(ss[:, 0], ss[:, 3]).then_inc(inv, 1)

            def add(g, par):
                dve.wait_ge(out_ready, g + 1)
                nc.vector.tensor_tensor(m.x[:, g, :], m.x[:, g, :], ob[par][:, 0:E], ALU.add).then_inc(added, 1)

            add(0, 0)
            add(1, 1)
            with dve.Fori(1, NG // 2) as k:
                for par in range(2):
                    add(k * 2 + par, par)

        @block.gpsimd
        def _(pool):
            pool.wait_ge(inv, 2)

            def normalise(g, par):
                if not early(g, 2):
                    pool.wait_ge(anT_ready, g - 1)
                pool.tensor_tensor(an[:, par, :].rearrange("p (h w) -> p h w", w=W),
                                   m.att[:, g, :].rearrange("p (h w) -> p h w", w=W),
                                   ss[:, 0, bass.ts(g, DH)].unsqueeze(2).to_broadcast([P, DH, W]), ALU.mult).then_inc(an_ready, 1)

            normalise(0, 0)
            normalise(1, 1)
            with pool.Fori(1, NG // 2) as k:
                for par in range(2):
                    normalise(k * 2 + par, par)

        @block.tensor
        def _(pe):
            def turn(g, par):
                pe.wait_ge(an_ready, g + 1)
                if not early(g, 2):
                    pe.wait_ge(anT_out, g - 1)
                for j in range(4):
                    last = nc.tensor.transpose(tb[par][:, j * P:(j + 1) * P], an[:, par, j * P:(j + 1) * P], m.ident)
                last.then_inc(anT_ready, 1)

            def out(g, par):
                pe.wait_ge(anT_out, g + 1)
                if not early(g, 2):
                    pe.wait_ge(added, g - 1)
                for j in range(4):
                    last = nc.tensor.matmul(ob[par][:, 0:E], anT[:, par, j * P:(j + 1) * P], m.w_out[:, j, :],
                                            start=(j == 0), stop=(j == 3))
                last.then_inc(out_ready, 1)

            turn(0, 0)
            turn(1, 1)
            out(0, 0)
            with pe.Fori(1, NG // 2) as k:
                for par in range(2):
                    g = k * 2 + par
                    turn(g, par)
                    out(g - 1, 1 - par)
            out(NG - 1, 1)


def route(nc, m):
    with ExitStack() as ctx:
        def sb(name, shape, dt=F32):
            return ctx.enter_context(nc.sbuf_tensor(name, shape, dt))

        lg = sb("r_lg", [P, NG, NR])
        oh = sb("r_oh", [P, 2, NG, NR])
        tmp = sb("r_tmp", [P, 2, NG, NR])
        top = sb("r_top", [P, 8, NG])
        logits_ready = ctx.enter_context(nc.semaphore("r_logits_ready"))
        chain = ctx.enter_context(nc.semaphore("r_chain"))
        gap_ready = ctx.enter_context(nc.semaphore("r_gap_ready"))
        exp_ready = ctx.enter_context(nc.semaphore("r_exp_ready"))
        block = ctx.enter_context(nc.Block())

        @block.tensor
        def _(pe):
            for g in range(NG):
                last = nc.tensor.matmul(m.bank[4][:, 8 * g:8 * g + NR], m.xT[:, g * P:(g + 1) * P], m.router[:],
                                        start=True, stop=True)
            last.then_inc(logits_ready, 1)

        @block.scalar
        def _(act):
            act.wait_ge(gap_ready, 1)
            nc.scalar.activation(top[:, 3], top[:, 2], ACT.Exp).then_inc(exp_ready, 1)

        @block.vector
        def _(dve):
            def wide(a):
                return a.unsqueeze(2).to_broadcast([P, NG, NR])

            preference = m.preference[:].unsqueeze(1).to_broadcast([P, NG, NR])
            dve.wait_ge(logits_ready, 1)
            nc.vector.tensor_copy(lg[:], m.bank[4][:, 0:8 * NG].rearrange("p (g e) -> p g e", e=8)[:, :, 0:NR]).then_inc(chain, 1)
            n = 1
            for k in range(2):
                dve.wait_ge(chain, n)
                nc.vector.tensor_reduce(top[:, k], lg[:], AX.X, ALU.max).then_inc(chain, 1)
                dve.wait_ge(chain, n + 1)
                nc.vector.tensor_tensor(tmp[:, 0], lg[:], wide(top[:, k]), ALU.is_equal).then_inc(chain, 1)
                dve.wait_ge(chain, n + 2)
                nc.vector.tensor_tensor(tmp[:, 1], tmp[:, 0], preference, ALU.mult).then_inc(chain, 1)
                dve.wait_ge(chain, n + 3)
                nc.vector.tensor_reduce(top[:, 7], tmp[:, 1], AX.X, ALU.max).then_inc(chain, 1)
                dve.wait_ge(chain, n + 4)
                nc.vector.tensor_tensor(oh[:, k], tmp[:, 1], wide(top[:, 7]), ALU.is_equal).then_inc(chain, 1)
                n += 5
                if k == 0:
                    dve.wait_ge(chain, n)
                    nc.vector.scalar_tensor_tensor(lg[:], oh[:, 0], LOW, lg[:], ALU.mult, ALU.add).then_inc(chain, 1)
                    n += 1
            dve.wait_ge(chain, n)
            nc.vector.tensor_tensor(top[:, 2], top[:, 1], top[:, 0], ALU.subtract).then_inc(gap_ready, 1)
            dve.wait_ge(exp_ready, 1)
            nc.vector.tensor_scalar(top[:, 4], top[:, 3], 1.0, None, ALU.add).then_inc(chain, 1)
            dve.wait_ge(chain, n + 1)
            nc.vector.reciprocal(top[:, 5], top[:, 4]).then_inc(chain, 1)
            dve.wait_ge(chain, n + 2)
            nc.vector.tensor_tensor(top[:, 6], top[:, 5], top[:, 3], ALU.mult).then_inc(chain, 1)
            dve.wait_ge(chain, n + 3)
            nc.vector.tensor_tensor(tmp[:, 0], oh[:, 0], wide(top[:, 5]), ALU.mult).then_inc(chain, 1)
            nc.vector.tensor_tensor(tmp[:, 1], oh[:, 1], wide(top[:, 6]), ALU.mult).then_inc(chain, 1)
            nc.vector.memset(m.share[:, :, NR:NE], 1.0).then_inc(chain, 1)
            dve.wait_ge(chain, n + 6)
            nc.vector.tensor_tensor(m.share[:, :, 0:NR], tmp[:, 0], tmp[:, 1], ALU.add)


def experts(nc, m, out):
    with ExitStack() as ctx:
        def sb(name, shape, dt=F32):
            return ctx.enter_context(nc.sbuf_tensor(name, shape, dt))

        def sem(name):
            return ctx.enter_context(nc.semaphore(name))

        xg = sb("f_xg", [P, 2, P])
        gate = sb("f_gate", [P, 2, HID])
        h = sb("f_h", [P, 2, HID])
        hT = sb("f_hT", [P, 2, HID])
        xg_ready = sem("f_xg_ready")
        g_ready = sem("f_g_ready")
        u_ready = sem("f_u_ready")
        gate_ready = sem("f_gate_ready")
        h_ready = sem("f_h_ready")
        hT_ready = sem("f_hT_ready")
        hT_out = sem("f_hT_out")
        y_ready = sem("f_y_ready")
        y_added = sem("f_y_added")
        stored = sem("f_stored")
        gb, ub, tb, yb = m.bank[0:2], m.bank[2:4], m.bank[4:6], m.bank[6:8]
        block = ctx.enter_context(nc.Block())

        def over_jobs(eng, head, body, tail):
            for e in range(NE):
                body(0, e, e)
            with eng.Fori(1, NG) as g:
                for e in range(NE):
                    body(g, e, g * NE + e)
            tail()

        @block.gpsimd
        def _(pool):
            def stage(g, par):
                if not early(g, 2):
                    pool.wait_ge(u_ready, g * NE - NE)
                pool.tensor_copy(xg[:, par, :], m.xT[:, bass.ts(g, P)]).then_inc(xg_ready, 1)

            stage(0, 0)
            stage(1, 1)
            with pool.Fori(1, NG // 2) as k:
                for par in range(2):
                    stage(k * 2 + par, par)

        @block.tensor
        def _(pe):
            def up(g, gpar, e, n):
                if e == 0:
                    pe.wait_ge(xg_ready, g + 1)
                if not early(n, 2):
                    pe.wait_ge(gate_ready, n - 1)
                nc.tensor.matmul(gb[e % 2][:], xg[:, gpar, :], m.w_gate[:, e, :], start=True, stop=True).then_inc(g_ready, 1)
                if not early(n, 2):
                    pe.wait_ge(h_ready, n - 1)
                nc.tensor.matmul(ub[e % 2][:], xg[:, gpar, :], m.w_up[:, e, :], start=True, stop=True).then_inc(u_ready, 1)

            def turn(e, n):
                pe.wait_ge(h_ready, n + 1)
                if not early(n, 2):
                    pe.wait_ge(hT_out, n - 1)
                for j in range(KT):
                    last = nc.tensor.transpose(tb[e % 2][:, j * P:(j + 1) * P], h[:, e % 2, j * P:(j + 1) * P], m.ident)
                last.then_inc(hT_ready, 1)

            def down(e, n):
                pe.wait_ge(hT_out, n + 1)
                if not early(n, 2):
                    pe.wait_ge(y_added, n - 1)
                for j in range(KT):
                    last = nc.tensor.matmul(yb[e % 2][:, 0:E], hT[:, e % 2, j * P:(j + 1) * P], m.w_down[:, e, j, :],
                                            start=(j == 0), stop=(j == KT - 1))
                last.then_inc(y_ready, 1)

            def group(g, gpar, n0):
                for e in range(NE):
                    up(g, gpar, e, n0 + e)
                    if not early(n0 + e, 1):
                        turn((e - 1) % NE, n0 + (e - 1))
                    if not early(n0 + e, 2):
                        down((e - 2) % NE, n0 + (e - 2))

            pe.wait_ge(m.ew_loaded, 16 * 6)
            group(0, 0, 0)
            group(1, 1, NE)
            with pe.Fori(1, NG // 2) as k:
                for gpar in range(2):
                    g = k * 2 + gpar
                    group(g, gpar, g * NE)
            turn(NE - 1, NG * NE - 1)
            down(NE - 2, NG * NE - 2)
            down(NE - 1, NG * NE - 1)

        @block.scalar
        def _(act):
            def body(g, e, n):
                act.wait_ge(g_ready, n + 1)
                if not early(n, 2):
                    act.wait_ge(h_ready, n - 1)
                nc.scalar.activation(gate[:, e % 2, :], gb[e % 2][:], ACT.Silu).then_inc(gate_ready, 1)
                if not early(n, 1):
                    turned(1 - e % 2, n - 1)

            def turned(par, n):
                act.wait_ge(hT_ready, n + 1)
                if not early(n, 2):
                    act.wait_ge(y_ready, n - 1)
                nc.scalar.copy(hT[:, par, :], tb[par][:]).then_inc(hT_out, 1)

            over_jobs(act, None, body, lambda: turned(1, NG * NE - 1))

        @block.vector
        def _(dve):
            def body(g, e, n):
                dve.wait_ge(gate_ready, n + 1)
                dve.wait_ge(u_ready, n + 1)
                if not early(n, 2):
                    dve.wait_ge(hT_ready, n - 1)
                nc.vector.tensor_tensor(h[:, e % 2, :], gate[:, e % 2, :], ub[e % 2][:], ALU.mult).then_inc(h_ready, 1)
                if not early(n, 2):
                    add(g if e >= 2 else g - 1, (e - 2) % NE, n - 2)

            def add(g, e, n):
                dve.wait_ge(y_ready, n + 1)
                if not early(n, 1):
                    dve.wait_ge(y_added, n)
                nc.vector.scalar_tensor_tensor(m.x[:, g, :], yb[e % 2][:, 0:E], m.share[:, g, e:e + 1], m.x[:, g, :],
                                               ALU.mult, ALU.add).then_inc(y_added, 1)

            def tail():
                add(NG - 1, NE - 2, NG * NE - 2)
                add(NG - 1, NE - 1, NG * NE - 1)

            over_jobs(dve, None, body, tail)

        @block.sync
        def _(sp):
            ov = out.rearrange("(g p) d -> p g d", p=P)
            for k in range(NG // 4):
                sp.wait_ge(y_added, 4 * NE * (k + 1))
                sp.dma_start(ov[:, 4 * k:4 * k + 4, :], m.x[:, 4 * k:4 * k + 4, :]).then_inc(stored, 16)
            sp.wait_ge(stored, 16 * (NG // 4))


def perceiver_layer(nc, ins, out):
    with ExitStack() as ctx:
        m = Shared()

        def sb(name, shape, dt=F32):
            return ctx.enter_context(nc.sbuf_tensor(name, shape, dt))

        def sem(name):
            return ctx.enter_context(nc.semaphore(name))

        psum = ctx.enter_context(nc.psum_tensor("banks", [P, 8, 512], F32))
        m.bank = [psum[:, k, :] for k in range(8)]
        m.scores = psum[:, 0:NT, :]
        m.x = sb("x", [P, NG, E])
        m.xn = sb("xn", [P, NG, E])
        m.xT = sb("xT", [P, TOK])
        m.stat = sb("stat", [P, 4, NG])
        m.consts = sb("consts", [P, P + NR])
        m.ident = m.consts[:, 0:P]
        m.preference = m.consts[:, P:P + NR]
        m.own_entry = sb("own_entry", [NT * GB, GB])
        m.spread = sb("spread", [P, GB, P], BF16)
        m.w_qk = sb("w_qk", [P, H, P])
        m.w_vo = sb("w_vo", [P, H, P])
        m.w_dd = sb("w_dd", [P, NC, P])
        m.w_v = sb("w_v", [P, DE])
        m.w_out = sb("w_out", [P, DE // P, E])
        m.router = sb("router", [P, NR])
        m.gamma_in = sb("gamma_in", [P, 1])
        m.gamma = sb("gamma", [P, 1])
        m.lam_in = sb("lam_in", [P, 4, DD])
        m.lam_prod = sb("lam_prod", [P, 2, DD])
        m.lam = sb("lam", [P, 5])
        m.pair_factor = sb("pair_factor", [P, 2])
        m.share = sb("share", [P, NG, NE])
        m.v_scratch = nc.dram_tensor("v_scratch", [B, H * E], F32, kind="Internal").ap()

        m.x_loaded = sem("x_loaded")
        m.consts_loaded = sem("consts_loaded")
        m.aw_loaded = sem("aw_loaded")
        m.mask_loaded = sem("mask_loaded")
        m.misc_loaded = sem("misc_loaded")
        m.ew_loaded = sem("ew_loaded")
        m.v_stored = sem("v_stored")

        with ExitStack() as front:
            m.mask_add = front.enter_context(nc.sbuf_tensor("mask_add", [P, NG, S2], BF16))
            with ExitStack() as early:
                def eb(name, shape, dt=F32):
                    return early.enter_context(nc.sbuf_tensor(name, shape, dt))

                m.sq = eb("sq1", [P, NG, E])
                m.aw = eb("aw", [DK, 4, H, P])
                m.dw = eb("dw", [DD, 2, NC, P])
                m.last_row = eb("last_row", [P, B])
                m.v_rows = eb("v_rows", [B, 4, 512])
                m.mask_in = eb("mask_in", [P, NG, S2], U8)
                with nc.Block() as block:
                    @block.sync
                    def _(sp):
                        sp.dma_start(m.x[:], ins["x"].rearrange("(g p) d -> p g d", p=P)).then_inc(m.x_loaded, 16)
                        sp.dma_start(m.consts[:], ins["consts"]).then_inc(m.consts_loaded, 16)
                        sp.dma_start(m.aw[:], ins["aw"]).then_inc(m.aw_loaded, 16)
                        sp.dma_start(m.dw[:], ins["dw"]).then_inc(m.aw_loaded, 16)
                        sp.dma_start(m.mask_in[:], ins["mask"].rearrange("(g p) t -> p g t", p=P)).then_inc(m.mask_loaded, 16)

                    @block.scalar
                    def _(act):
                        for dst, name in ((m.last_row, "last_row"), (m.own_entry, "own_entry"), (m.spread, "spread"),
                                          (m.w_v, "w_v"), (m.w_out, "w_out"), (m.router, "router"),
                                          (m.gamma_in, "gamma"), (m.lam_in, "lam")):
                            act.dma_start(dst[:], ins[name]).then_inc(m.misc_loaded, 16)
                        act.wait_ge(m.misc_loaded, 16 * 8)
                layer_norm(nc, m, "ln1")
                fold_weights(nc, m)
            cross_attention(nc, m, ins["ctx_pack"])
        m.w_gate = sb("w_gate", [P, NE, HID])
        m.w_up = sb("w_up", [P, NE, HID])
        m.w_down = sb("w_down", [P, NE, KT, E])
        with nc.Block() as block:
            @block.sync
            def _(sp):
                for dst, name in ((m.w_gate, "gate"), (m.w_up, "up")):
                    sp.dma_start(dst[:, 0:NR, :], ins["w_" + name].rearrange("e d h -> d e h")).then_inc(m.ew_loaded, 16)
                    sp.dma_start(dst[:, NR, :], ins["sw_" + name][0]).then_inc(m.ew_loaded, 16)
                sp.dma_start(m.w_down[:, 0:NR], ins["w_down"].rearrange("e (k p) d -> p e k d", p=P)).then_inc(m.ew_loaded, 16)
                sp.dma_start(m.w_down[:, NR], ins["sw_down"][0].rearrange("(k p) d -> p k d", p=P)).then_inc(m.ew_loaded, 16)
        with ExitStack() as mid:
            m.sq = mid.enter_context(nc.sbuf_tensor("sq2", [P, NG, E], F32))
            layer_norm(nc, m, "ln2")
        with ExitStack() as mid:
            m.att = mid.enter_context(nc.sbuf_tensor("att", [P, NG, DE], F32))
            differential_attention(nc, m)
            attention_output(nc, m)
        with ExitStack() as mid:
            m.sq = mid.enter_context(nc.sbuf_tensor("sq3", [P, NG, E], F32))
            layer_norm(nc, m, "ln3")
            route(nc, m)
        experts(nc, m, out)


def kernel(**inputs):
    from concourse import bacc
    from concourse.bass_utils import run_bass_kernel_spmd

    a = {k: np.ascontiguousarray(v) for k, v in inputs.items()}
    f32 = np.float32
    ctx = a["ctx_1024"]
    nat = ctx[:, :CH * P, :].reshape(B, CH, P, E).transpose(0, 2, 1, 3).reshape(B, P, CH * E)
    consts = np.concatenate([np.eye(P, dtype=f32), np.tile(np.arange(NR, 0, -1, dtype=f32), (P, 1))], 1)
    spread = np.zeros((P, GB, P), f32)
    for b in range(GB):
        for t in range(T):
            spread[b * T + t, b, t::T] = 1.0
    import ml_dtypes

    def heads_first(w):
        return w.reshape(E, DH, 2, DD).transpose(3, 2, 1, 0).reshape(DD, NC, E)

    arrays = {
        "x": a["x"].reshape(TOK, E),
        "ctx_pack": np.concatenate([nat, ctx.transpose(0, 2, 1)], 2),
        "last_row": ctx[:, S2 - 1, :].T,
        "mask": a["mask_Bx1xSxS2_bf1"].reshape(TOK, S2).view(np.uint8),
        "aw": np.stack([a["L0_xattn_w_q"].transpose(2, 0, 1), a["L0_xattn_w_k"].transpose(2, 0, 1),
                        a["L0_xattn_w_v"].transpose(2, 0, 1), a["L0_xattn_w_o"].transpose(1, 0, 2)], 1),
        "dw": np.stack([heads_first(a["L0_attn_Wq"]), heads_first(a["L0_attn_Wkv"][:, :DE])], 1),
        "w_v": a["L0_attn_Wkv"][:, DE:],
        "w_out": a["L0_attn_Wout"].reshape(DE // P, P, E).transpose(1, 0, 2),
        "gamma": np.tile(a["L0_attn_gamma"], P // (2 * DD)).reshape(P, 1),
        "lam": np.tile(np.stack([a["L0_attn_lambda_q1"], a["L0_attn_lambda_q2"], a["L0_attn_lambda_k1"],
                                 a["L0_attn_lambda_k2"]])[None], (P, 1, 1)),
        "router": a["L0_ffn_router_w"].T,
        "w_gate": a["L0_ffn_w_gate"], "w_up": a["L0_ffn_w_up"], "w_down": a["L0_ffn_w_down"],
        "sw_gate": a["L0_ffn_sw_gate"], "sw_up": a["L0_ffn_sw_up"], "sw_down": a["L0_ffn_sw_down"],
        "consts": consts,
        "own_entry": np.tile(np.eye(GB, dtype=f32), (NT, 1)),
        "spread": spread.astype(ml_dtypes.bfloat16),
    }
    arrays = {f"in_{k}": np.ascontiguousarray(v) for k, v in arrays.items()}
    nc = bacc.Bacc("TRN2", target_bir_lowering=False, num_devices=1)
    ins = {k[3:]: nc.dram_tensor(k, v.shape, mybir.dt.from_np(v.dtype), kind="ExternalInput").ap()
           for k, v in arrays.items()}
    out = nc.dram_tensor("out", (TOK, E), F32, kind="ExternalOutput").ap()
    perceiver_layer(nc, ins, out)
    r = run_bass_kernel_spmd(nc, [arrays], core_ids=[0])
    return r.results[0]["out"].reshape(B, T, E)
```

```python
import math
from contextlib import ExitStack

import numpy as np

import concourse.bass as bass
from concourse import mybir

F32 = mybir.dt.float32
F32R = mybir.dt.float32r
BF16 = mybir.dt.bfloat16
U8 = mybir.dt.uint8
ALU = mybir.AluOpType
ACT = mybir.ActivationFunctionType
AX = mybir.AxisListType

P = 128
B, T, E = 64, 32, 128
S2 = 257
H, DK = 16, 64
TOK = B * T
NG = TOK // P
GB = P // T
NT = H * T // P
HT = H // NT
CH = (S2 - 1) // P
PACK = CH * P + S2 + 1
XSCALE = 1.0 / math.sqrt(DK)
MASKED = -8e30

DH, DD = 8, 32
NC = 2 * DH
DE = 2 * DH * DD
LAMBDA_INIT = 0.8 - 0.6 * math.exp(-0.3 * 1)

NE, HID = 8, 512
NR = NE - 1
KT = HID // P
EW = 2 * HID + KT * E
NTILE = (2 * TOK + NR * (P - 1)) // P
NTILE += NTILE % 2
LN_EPS = 1e-5
RMS_EPS = 1e-8
SE = E + 2
LOW = -3.0e38


class Shared:
    pass


def early(n, k):
    return isinstance(n, int) and n < k


def product3(nc, out, stationary, moving, start, stop):
    nc.tensor.matmul(out, stationary[0], moving[0], start=start, stop=False)
    nc.tensor.matmul(out, stationary[0], moving[1], start=False, stop=False)
    return nc.tensor.matmul(out, stationary[1], moving[0], start=False, stop=stop)


def layer_norm(nc, m, tag):
    with ExitStack() as ctx:
        mean_ready = ctx.enter_context(nc.semaphore(f"{tag}_mean_ready"))
        centred = ctx.enter_context(nc.semaphore(f"{tag}_centred"))
        squared = ctx.enter_context(nc.semaphore(f"{tag}_squared"))
        var_ready = ctx.enter_context(nc.semaphore(f"{tag}_var_ready"))
        std_ready = ctx.enter_context(nc.semaphore(f"{tag}_std_ready"))
        normed = ctx.enter_context(nc.semaphore(f"{tag}_normed"))
        turned = ctx.enter_context(nc.semaphore(f"{tag}_turned"))
        turned_high = ctx.enter_context(nc.semaphore(f"{tag}_turned_high"))
        turned_out = ctx.enter_context(nc.semaphore(f"{tag}_turned_out"))
        block = ctx.enter_context(nc.Block())

        @block.vector
        def _(dve):
            if tag == "ln1":
                dve.wait_ge(m.x_loaded, 32)
            nc.vector.tensor_reduce(m.stat[:, 0, :], m.x[:], AX.X, ALU.add).then_inc(mean_ready, 1)
            dve.wait_ge(mean_ready, 1)
            nc.vector.tensor_scalar(m.stat[:, 1, :], m.stat[:, 0, :], 1.0 / E, None, ALU.mult).then_inc(mean_ready, 1)
            dve.wait_ge(mean_ready, 2)
            nc.vector.tensor_tensor(m.xn[:], m.x[:], m.stat[:, 1, :].unsqueeze(2).to_broadcast([P, NG, E]),
                                    ALU.subtract).then_inc(centred, 1)
            if tag == "ln1":
                for n in range(4):
                    fold_low(nc, m, dve, n)
            dve.wait_ge(squared, 1)
            nc.vector.tensor_reduce(m.stat[:, 0, :], m.sq[:], AX.X, ALU.add).then_inc(var_ready, 1)
            dve.wait_ge(var_ready, 1)
            nc.vector.tensor_scalar(m.stat[:, 1, :], m.stat[:, 0, :], 1.0 / E, LN_EPS, ALU.mult,
                                    ALU.add).then_inc(var_ready, 1)
            dve.wait_ge(std_ready, 1)
            nc.vector.reciprocal(m.stat[:, 3, :], m.stat[:, 2, :]).then_inc(std_ready, 1)
            dve.wait_ge(std_ready, 2)
            for k in range(NG // 4):
                part = slice(4 * k, 4 * k + 4)
                nc.vector.tensor_tensor(m.xn[:, part, :], m.xn[:, part, :],
                                        m.stat[:, 3, part].unsqueeze(2).to_broadcast([P, 4, E]),
                                        ALU.mult).then_inc(normed, 1)
            if tag == "ln1":
                dve.wait_ge(m.row_high, 1)
                nc.vector.tensor_tensor(m.row_parts[1][:], m.last_row[:], m.row_parts[0][:].bitcast(F32), ALU.subtract)
                for n in range(4, FOLDS):
                    fold_low(nc, m, dve, n)
            for k in range(NG // 4):
                part = slice(4 * P * k, 4 * P * (k + 1))
                dve.wait_ge(turned_high, k + 1)
                nc.vector.tensor_tensor(m.xT[1][:, part], m.bank[k % 2][:], m.xT[0][:, part].bitcast(F32),
                                        ALU.subtract).then_inc(turned_out, 1)

        @block.scalar
        def _(act):
            if tag == "ln3":
                weights_high(nc, m, act, 0)
            act.wait_ge(centred, 1)
            nc.scalar.activation(m.sq[:], m.xn[:], ACT.Square).then_inc(squared, 1)
            if tag == "ln3":
                weights_high(nc, m, act, 1)
            if tag == "ln1":
                for n in range(4):
                    fold_high(nc, m, act, n)
            act.wait_ge(var_ready, 2)
            nc.scalar.activation(m.stat[:, 2, :], m.stat[:, 1, :], ACT.Sqrt).then_inc(std_ready, 1)
            if tag == "ln1":
                act.wait_ge(m.misc_loaded, 16 * 7)
                nc.scalar.copy(m.row_parts[0][:], m.last_row[:]).then_inc(m.row_high, 1)
                for n in range(4, FOLDS):
                    fold_high(nc, m, act, n)
            for k in range(NG // 4):
                act.wait_ge(turned, k + 1)
                nc.scalar.copy(m.xT[0][:, 4 * P * k:4 * P * (k + 1)], m.bank[k % 2][:]).then_inc(turned_high, 1)
            if tag == "ln3":
                weights_high(nc, m, act, 2)
                weights_high(nc, m, act, 3)

        if tag == "ln1":
            @block.gpsimd
            def _(pool):
                pool.memset(m.pair_factor[:, 0:1], 1.0)
                pool.wait_ge(m.mask_loaded, 16)
                for k in range(4):
                    part = slice(NG // 4 * k, NG // 4 * (k + 1))
                    pool.tensor_scalar(m.mask_add[:, part, :], m.mask_in[:, part, :], -MASKED, MASKED, ALU.mult, ALU.add)

        if tag == "ln3":
            @block.sync
            def _(sp):
                load_weights(m, sp, range(NE // 2))

            @block.gpsimd
            def _(pool):
                weights_low(m, pool, range(NE // 2))

        @block.tensor
        def _(pe):
            if tag == "ln1":
                pe.wait_ge(m.aw_loaded, 16)
                for n in range(FOLDS):
                    fold(nc, m, pe, n)
                pe.wait_ge(m.consts_loaded, 16)
            for k in range(NG // 4):
                pe.wait_ge(normed, k + 1)
                if k >= 2:
                    pe.wait_ge(turned_out, k - 1)
                for j in range(4):
                    last = nc.tensor.transpose(m.bank[k % 2][:, j * P:(j + 1) * P], m.xn[:, 4 * k + j, :],
                                               m.ident)
                last.then_inc(turned, 1)


def load_weights(m, sp, experts):
    for e in experts:
        if e >= 2:
            sp.wait_ge(m.raw_low, e - 1)
        gate, up, down = m.expert_sources[e]
        sp.dma_start(m.raw[:, e % 2, 0:HID], gate).then_inc(m.raw_loaded[e % 2], 16)
        sp.dma_start(m.raw[:, e % 2, HID:2 * HID], up).then_inc(m.raw_loaded[e % 2], 16)
        sp.dma_start(m.raw[:, e % 2, 2 * HID:].rearrange("p (k d) -> p k d", d=E),
                     down.rearrange("(k p) d -> p k d", p=P)).then_inc(m.raw_loaded[e % 2], 16)


def weights_high(nc, m, act, e):
    act.wait_ge(m.raw_loaded[e % 2], 48 * (e // 2 + 1))
    nc.scalar.copy(m.w_exp[0][:, e, :], m.raw[:, e % 2, :]).then_inc(m.raw_high, 1)


def weights_low(m, pool, experts):
    for e in experts:
        pool.wait_ge(m.raw_high, e + 1)
        pool.tensor_tensor(m.w_exp[1][:, e, :], m.raw[:, e % 2, :], m.w_exp[0][:, e, :].bitcast(F32),
                           ALU.subtract).then_inc(m.raw_low, 1)


FOLDS = 8


def fold_parts(m, n):
    parts = (m.w_qk, m.w_vo)[n // 4]
    return m.bank[2 + n % 4], [a[:, 4 * (n % 4):4 * (n % 4) + 4, :] for a in parts]


def fold(nc, m, pe, n):
    if n >= 4:
        pe.wait_ge(m.folded_out, n - 3)
    for j in range(4):
        h = 4 * (n % 4) + j
        last = nc.tensor.matmul(fold_parts(m, n)[0][:, j * P:(j + 1) * P], m.aw[:, n // 4 * 2, h, :],
                                m.aw[:, n // 4 * 2 + 1, h, :], start=True, stop=True)
    last.then_inc(m.folded, 1)


def fold_high(nc, m, act, n):
    act.wait_ge(m.folded, n + 1)
    bank, parts = fold_parts(m, n)
    nc.scalar.copy(parts[0], bank[:]).then_inc(m.folded_high, 1)


def fold_low(nc, m, dve, n):
    dve.wait_ge(m.folded_high, n + 1)
    bank, parts = fold_parts(m, n)
    high, low = (a.rearrange("p a n -> p (a n)") for a in parts)
    nc.vector.tensor_tensor(low, bank[:], high.bitcast(F32), ALU.subtract).then_inc(m.folded_out, 1)


def finish_folding(nc, m):
    with ExitStack() as ctx:
        v_row = ctx.enter_context(nc.semaphore("v_row"))
        v_row_out = ctx.enter_context(nc.semaphore("v_row_out"))
        lam_step = ctx.enter_context(nc.semaphore("lam_step"))
        lam_exp = ctx.enter_context(nc.semaphore("lam_exp"))
        block = ctx.enter_context(nc.Block())

        @block.tensor
        def _(pe):
            for hb in range(4):
                product3(nc, m.bank[4 + hb][:], [a[:] for a in m.row_parts], [a[:, 4 * hb:4 * hb + 4, :] for a in m.w_vo],
                         True, True).then_inc(v_row, 1)

        @block.scalar
        def _(act):
            for hb in range(1, 4, 2):
                act.wait_ge(v_row, hb + 1)
                nc.scalar.copy(m.v_rows[:, hb, :], m.bank[4 + hb][0:B, :]).then_inc(v_row_out, 1)
            act.wait_ge(lam_step, 2)
            nc.scalar.activation(m.lam[:, 2:4], m.lam[:, 0:2], ACT.Exp).then_inc(lam_exp, 1)

        @block.vector
        def _(dve):
            nc.vector.tensor_tensor(m.lam_prod[:], m.lam_in[:, 0:2, :], m.lam_in[:, 2:4, :], ALU.mult).then_inc(lam_step, 1)
            dve.wait_ge(lam_step, 1)
            nc.vector.tensor_reduce(m.lam[:, 0:2], m.lam_prod[:], AX.X, ALU.add).then_inc(lam_step, 1)
            for hb in range(0, 4, 2):
                dve.wait_ge(v_row, hb + 1)
                nc.vector.tensor_copy(m.v_rows[:, hb, :], m.bank[4 + hb][0:B, :]).then_inc(v_row_out, 1)
            dve.wait_ge(lam_exp, 1)
            nc.vector.tensor_tensor(m.lam[:, 4:5], m.lam[:, 3:4], m.lam[:, 2:3], ALU.subtract).then_inc(lam_step, 1)
            dve.wait_ge(lam_step, 3)
            nc.vector.tensor_scalar(m.pair_factor[:, 1:2], m.lam[:, 4:5], -LAMBDA_INIT, None, ALU.add).then_inc(lam_step, 1)
            nc.vector.tensor_scalar(m.gamma[:], m.gamma_in[:], 1.0 - LAMBDA_INIT, None, ALU.mult).then_inc(lam_step, 1)
            dve.wait_ge(lam_step, 5)
            nc.vector.tensor_scalar(m.w_out[:], m.w_out[:], m.gamma[:, 0:1], None, ALU.mult)

        @block.sync
        def _(sp):
            sp.wait_ge(v_row_out, 4)
            sp.dma_start(m.v_scratch[:, :], m.v_rows[:].rearrange("b a n -> b (a n)")).then_inc(m.v_stored, 16)
            sp.wait_ge(m.v_stored, 16)


def fold_self_weights(nc, m):
    with ExitStack() as ctx:
        folded = ctx.enter_context(nc.semaphore("s_folded"))
        folded_high = ctx.enter_context(nc.semaphore("s_folded_high"))
        other_high = ctx.enter_context(nc.semaphore("s_other_high"))
        block = ctx.enter_context(nc.Block())

        @block.tensor
        def _(pe):
            pe.wait_ge(m.self_loaded, 32)
            for hb in range(4):
                for j in range(4):
                    h = 4 * hb + j
                    last = nc.tensor.matmul(m.bank[4 + hb][:, j * P:(j + 1) * P], m.dw[:, 0, h, :], m.dw[:, 1, h, :],
                                            start=True, stop=True)
                last.then_inc(folded, 1)

        @block.scalar
        def _(act):
            act.wait_ge(m.self_loaded, 32)
            nc.scalar.copy(m.w_v[0][:], m.w_v_in[:]).then_inc(other_high, 1)
            nc.scalar.copy(m.router[0][:], m.router_in[:]).then_inc(other_high, 1)
            for hb in range(4):
                act.wait_ge(folded, hb + 1)
                nc.scalar.copy(m.w_dd[0][:, 4 * hb:4 * hb + 4, :], m.bank[4 + hb][:]).then_inc(folded_high, 1)

        @block.vector
        def _(dve):
            for n, (parts, whole) in enumerate(((m.w_v, m.w_v_in), (m.router, m.router_in))):
                dve.wait_ge(other_high, n + 1)
                nc.vector.tensor_tensor(parts[1][:], whole[:], parts[0][:].bitcast(F32), ALU.subtract)
            for hb in range(4):
                dve.wait_ge(folded_high, hb + 1)
                nc.vector.tensor_tensor(m.w_dd[1][:, 4 * hb:4 * hb + 4, :].rearrange("p a n -> p (a n)"), m.bank[4 + hb][:],
                                        m.w_dd[0][:, 4 * hb:4 * hb + 4, :].rearrange("p a n -> p (a n)").bitcast(F32),
                                        ALU.subtract)


def cross_attention(nc, m, ctx_pack):
    with ExitStack() as ctx:
        def sb(name, shape, dt=F32):
            return ctx.enter_context(nc.sbuf_tensor(name, shape, dt))

        def sem(name):
            return ctx.enter_context(nc.semaphore(name))

        raw = sb("raw", [P, GB, PACK])
        cx = [sb(f"cx{k}", [P, GB, PACK], F32R) for k in range(2)]
        q = [sb(f"q{k}", [P, 2, GB, H, T], F32R) for k in range(2)]
        probs = sb("probs", [P, 2, NT, S2])
        probsT = [sb(f"probsT{k}", [P, 2, CH, H * T], F32R) for k in range(2)]
        mixed = [sb(f"mixed{k}", [P, H, 2 * GB, T], F32R) for k in range(2)]
        outT = sb("outT", [P, 2 * P])
        row_top = sb("row_top", [P, 2, NT])
        row_max = sb("row_max", [P, 2, NT])
        row_sum = sb("row_sum", [P, 2, NT])
        row_inv = sb("row_inv", [P, 2, NT])
        last_p = sb("last_p", [P, 2, NT, GB])
        last_pd = sb("last_pd", [NT * GB, 2, HT, GB, T])
        v_last = sb("v_last", [NT * GB, 2, HT * E])

        cx_high = sem("cx_high")
        cx_low = sem("cx_low")
        cx_loaded = [sem(f"cx_loaded{s}") for s in range(GB)]
        v_loaded = [sem(f"v_loaded{s}") for s in range(2)]
        scores_ready = sem("scores_ready")
        max_ready = sem("max_ready")
        max_step = sem("max_step")
        exp_done = sem("exp_done")
        inv_ready = sem("inv_ready")
        probs_ready = sem("probs_ready")
        last_p_ready = sem("last_p_ready")
        probsT_ready = sem("probsT_ready")
        probsT_high = sem("probsT_high")
        probsT_out = sem("probsT_out")
        mixed_ready = sem("mixed_ready")
        mixed_high = sem("mixed_high")
        mixed_out = sem("mixed_out")
        q_ready = sem("q_ready")
        q_high = sem("q_high")
        q_out = sem("q_out")
        last_t_ready = sem("last_t_ready")
        last_pd_ready = sem("last_pd_ready")
        out_ready = sem("out_ready")
        outT_ready = sem("outT_ready")
        out_turned = sem("out_turned")
        out_added = sem("out_added")

        scores = m.scores
        pt_bank = m.bank[4:6]
        mixed_bank = m.bank[6]
        q_bank = m.bank[7]

        UN = 8
        LOOPS = (B - UN) // UN
        TAIL = range(B - UN + 1, B)

        block = ctx.enter_context(nc.Block())

        @block.sync
        def _(sp):
            def load_context(n, slot):
                sp.dma_start(raw[:, slot, :], ctx_pack[n, :, :]).then_inc(cx_loaded[slot], 16)

            def load_last(g, slot):
                for a in range(NT):
                    sp.dma_start(v_last[GB * a:GB * (a + 1), slot, :],
                                 m.v_scratch[bass.ds(g * GB, GB), HT * E * a:HT * E * (a + 1)]).then_inc(v_loaded[slot], 16)

            for s in range(GB):
                load_context(s, s)
            load_last(0, 0)
            load_last(1, 1)

            def load_group(g):
                for s in range(GB):
                    sp.wait_ge(cx_low, g * GB + (s - GB + 1))
                    load_context(g * GB + s, s)

            load_group(1)
            with sp.Fori(1, NG // 2) as k:
                for s in range(2):
                    load_group(k * 2 + s)
                sp.wait_ge(out_ready, k)
                for s in range(2):
                    load_last(k * 2 + s, s)

        @block.tensor
        def _(pe):
            def score_tiles(n, par, slot, group):
                pe.wait_ge(cx_low, n + 1)
                if slot == 0:
                    pe.wait_ge(q_out, group * 4 + 4)
                for pair in range(2):
                    if not early(n, 1):
                        pe.wait_ge(exp_done, n * NT - NT + 2 * pair + 2)
                    for g in (2 * pair, 2 * pair + 1):
                        product3(nc, scores[:, g, 0:S2 + 1], [a[:, par, slot, HT * g:HT * (g + 1), :] for a in q],
                                 [a[:, slot, CH * P:PACK] for a in cx], True, False)
                        last = nc.tensor.matmul(scores[:, g, 0:S2], m.spread[:, slot, :],
                                                m.mask_add[:, group, :], start=False, stop=True)
                    last.then_inc(scores_ready, 1)

            def queries(group, hb):
                for j in range(4):
                    last = product3(nc, q_bank[:, j * P:(j + 1) * P], [a[:, 4 * hb + j, :] for a in m.w_qk],
                                    [a[:, bass.ts(group, P)] for a in m.xT], True, True)
                last.then_inc(q_ready, 1)

            def transposes(n, par):
                pe.wait_ge(probs_ready, n + 1)
                for c in range(CH):
                    if not early(n, 1):
                        pe.wait_ge(probsT_out, n * 2 + (c - 1))
                    for g in range(NT):
                        last = nc.tensor.transpose(pt_bank[c][:, g * P:(g + 1) * P], probs[:, par, g, c * P:(c + 1) * P],
                                                   m.ident)
                    last.then_inc(probsT_ready, 1)

            def product(n, par, slot):
                pe.wait_ge(probsT_out, n * 2 + 2)
                if not early(n, 1):
                    pe.wait_ge(mixed_out, n)
                for c in range(CH):
                    last = product3(nc, mixed_bank[:], [a[:, slot, c * P:(c + 1) * P] for a in cx],
                                    [a[:, par, c, :] for a in probsT], c == 0, c == CH - 1)
                last.then_inc(mixed_ready, 1)

            def last_transpose(group, par):
                pe.wait_ge(last_p_ready, group * GB + GB)
                pe.wait_ge(mixed_out, group * GB + GB - 1)
                nc.tensor.transpose(mixed_bank[0:NT * GB, 0:P], last_p[:, par, :, :], m.ident).then_inc(last_t_ready, 1)

            def output(pair):
                pe.wait_ge(mixed_out, pair * (2 * GB) + 2 * GB)
                pe.wait_ge(last_pd_ready, pair * 2 + 2)
                for par in range(2):
                    pe.wait_ge(v_loaded[par], pair * 64 + 64)
                for h in range(H):
                    last = product3(nc, mixed_bank[:, 0:2 * P], [a[:, h, :] for a in m.w_vo], [a[:, h, :, :] for a in mixed],
                                    h == 0, h == H - 1)
                    if h % 2 == 0:
                        par, j = h // 2 // HT, h // 2 % HT
                        nc.tensor.matmul(mixed_bank[:, par * P:(par + 1) * P], v_last[:, par, j * E:(j + 1) * E],
                                         last_pd[:, par, j, :, :], start=False, stop=False)
                last.then_inc(out_ready, 1)

            def turn_back(pair):
                pe.wait_ge(outT_ready, pair + 1)
                for par in range(2):
                    last = nc.tensor.transpose(mixed_bank[:, par * P:(par + 1) * P], outT[:, par * P:(par + 1) * P], m.ident)
                last.then_inc(out_turned, 1)

            def step(n, u, group, pair, tail):
                s = (1 + u) % UN
                gpar = s // GB % 2
                if s % GB == 0:
                    last_transpose(group - 1, 1 - gpar)
                if not tail or n + 1 < B:
                    nslot = (s + 1) % GB
                    score_tiles(n + 1, (s + 1) // GB % 2, nslot, group + (1 if nslot == 0 else 0))
                j = s % GB
                made = group * 4 + (5 + j)
                more = not tail or made < 4 * NG
                if s == 1 and not early(pair, 1):
                    output(pair - 1)
                if s == 2 and not early(pair, 1):
                    pe.wait_ge(mixed_out, n - 1)
                    turn_back(pair - 1)
                if more:
                    pe.wait_ge(q_out, made)
                    queries(group + (2 if j == 3 else 1), (j + 1) % 4)
                if j == 0:
                    pe.wait_ge(last_pd_ready, group)
                if s == 1 and not early(pair, 1):
                    pe.wait_ge(outT_ready, pair)
                if s == 2 and not early(pair, 1):
                    pe.wait_ge(out_added, pair)
                product(n - 1, (s - 1) % 2, (s - 1) % GB)
                transposes(n, s % 2)

            for hb in range(4):
                if hb:
                    pe.wait_ge(q_out, hb)
                queries(0, hb)
            score_tiles(0, 0, 0, 0)
            score_tiles(1, 0, 1, 0)
            for hb in range(2):
                pe.wait_ge(q_out, 4 + hb)
                queries(1, hb)
            transposes(0, 0)
            for n in range(1, UN + 1):
                step(n, n - 1, n // GB, n // UN, False)
            with pe.Fori(1, LOOPS) as i:
                for u in range(UN):
                    step(i * UN + (1 + u), u, i * (UN // GB) + (1 + u) // GB, i + (1 + u) // UN, False)
            for n in TAIL:
                step(n, (n - 1) % UN, n // GB, n // UN, True)
            product(B - 1, 1, GB - 1)
            pe.wait_ge(mixed_out, B)
            last_transpose(NG - 1, 1)
            output(B // UN - 1)
            turn_back(B // UN - 1)

        @block.scalar
        def _(act):
            def context_high(n, slot, group):
                act.wait_ge(cx_loaded[slot], group * 16 + 16)
                if not early(n, GB):
                    act.wait_ge(mixed_ready, n - (GB - 1))
                nc.scalar.copy(cx[0][:, slot, :], raw[:, slot, :]).then_inc(cx_high, 1)

            def queries_high(gpar, hb, count):
                act.wait_ge(q_ready, count)
                nc.scalar.copy(q[0][:, gpar, :, 4 * hb:4 * hb + 4, :].rearrange("p b h t -> p h b t"),
                               q_bank[:].rearrange("p (h b t) -> p h b t", h=4, b=GB)).then_inc(q_high, 1)

            def exponentials(n, par):
                if not early(n, 2):
                    act.wait_ge(probsT_ready, (n - 1) * 2)
                    act.wait_ge(last_p_ready, n - 1)
                for g in range(NT):
                    if g % 2 == 0:
                        act.wait_ge(max_ready, n * 2 + (g // 2 + 1))
                    nc.scalar.activation(probs[:, par, g, :], scores[:, g, 0:S2], ACT.Exp, bias=row_max[:, par, g:g + 1],
                                         scale=XSCALE, accum_out=row_sum[:, par, g:g + 1]).then_inc(exp_done, 1)

            def chunks_high(n, par):
                for c in range(CH):
                    act.wait_ge(probsT_ready, n * 2 + (1 + c))
                    if not early(n, 2):
                        act.wait_ge(mixed_ready, n - 1)
                    nc.scalar.copy(probsT[0][:, par, c, :], pt_bank[c][:]).then_inc(probsT_high, 1)

            def product_high(n, slot):
                act.wait_ge(mixed_ready, n + 1)
                nc.scalar.copy(mixed[0][:, :, slot, :], mixed_bank[:].rearrange("p (h t) -> p h t", h=H)).then_inc(mixed_high, 1)

            def step(n, u, group, pair, tail):
                s = (1 + u) % UN
                if not tail or n + 1 < B:
                    exponentials(n + 1, (s + 1) % 2)
                if s == 1 and not early(pair, 1):
                    outT_copy(pair - 1)
                j = s % GB
                made = group * 4 + (5 + j)
                if not tail or made < 4 * NG:
                    queries_high((s // GB + (2 if j == 3 else 1)) % 2, (j + 1) % 4, made + 1)
                product_high(n - 1, (s - 1) % UN)
                chunks_high(n, s % 2)
                if not tail or n + 3 < B:
                    context_high(n + 3, (s + 3) % GB, group + (1 if j else 0))

            def outT_copy(pair):
                act.wait_ge(out_ready, pair + 1)
                if not early(pair, 1):
                    act.wait_ge(out_turned, pair)
                nc.scalar.copy(outT[:], mixed_bank[:, 0:2 * P]).then_inc(outT_ready, 1)

            for n in range(3):
                context_high(n, n, 0)
            for hb in range(4):
                queries_high(0, hb, hb + 1)
            exponentials(0, 0)
            exponentials(1, 1)
            queries_high(1, 0, 5)
            queries_high(1, 1, 6)
            chunks_high(0, 0)
            context_high(3, 3, 0)
            for n in range(1, UN + 1):
                step(n, n - 1, n // GB, n // UN, False)
            with act.Fori(1, LOOPS) as i:
                for u in range(UN):
                    step(i * UN + (1 + u), u, i * (UN // GB) + (1 + u) // GB, i + (1 + u) // UN, False)
            for n in TAIL:
                step(n, (n - 1) % UN, n // GB, n // UN, True)
            product_high(B - 1, UN - 1)
            outT_copy(B // UN - 1)

        @block.vector
        def _(dve):
            def maxima(n, par, pair):
                tiles = slice(2 * pair, 2 * pair + 2)
                dve.wait_ge(scores_ready, n * 2 + (pair + 1))
                nc.vector.tensor_reduce(row_top[:, par, tiles], scores[:, tiles, 0:S2], AX.X, ALU.max).then_inc(max_step, 1)
                dve.wait_ge(max_step, n * 2 + (pair + 1))
                nc.vector.tensor_scalar(row_max[:, par, tiles], row_top[:, par, tiles], -XSCALE, None, ALU.mult).then_inc(max_ready, 1)

            def inverses(n, par):
                dve.wait_ge(exp_done, n * NT + NT)
                nc.vector.reciprocal(row_inv[:, par, :], row_sum[:, par, :]).then_inc(inv_ready, 1)

            def chunk_low(n, par, c):
                dve.wait_ge(probsT_high, n * 2 + (1 + c))
                if not early(n, 2):
                    dve.wait_ge(mixed_ready, n - 1)
                nc.vector.tensor_tensor(probsT[1][:, par, c, :], pt_bank[c][:], probsT[0][:, par, c, :].bitcast(F32),
                                        ALU.subtract).then_inc(probsT_out, 1)

            def product_low(n, slot):
                dve.wait_ge(mixed_high, n + 1)
                nc.vector.tensor_tensor(mixed[1][:, :, slot, :], mixed_bank[:].rearrange("p (h t) -> p h t", h=H),
                                        mixed[0][:, :, slot, :].bitcast(F32), ALU.subtract).then_inc(mixed_out, 1)

            def queries_low(gpar, hb, count):
                dve.wait_ge(q_high, count)
                nc.vector.tensor_tensor(q[1][:, gpar, :, 4 * hb:4 * hb + 4, :].rearrange("p b h t -> p h b t"),
                                        q_bank[:].rearrange("p (h b t) -> p h b t", h=4, b=GB),
                                        q[0][:, gpar, :, 4 * hb:4 * hb + 4, :].rearrange("p b h t -> p h b t").bitcast(F32),
                                        ALU.subtract).then_inc(q_out, 1)

            def spread_last(group, par, pair):
                dve.wait_ge(last_t_ready, group + 1)
                if not early(pair, 1 + par):
                    dve.wait_ge(out_ready, pair - par)
                nc.vector.tensor_tensor(last_pd[:, par],
                                        mixed_bank[0:NT * GB, 0:P].rearrange("p (h t) -> p h t", h=HT).unsqueeze(2).to_broadcast([NT * GB, HT, GB, T]),
                                        m.own_entry[:].unsqueeze(1).unsqueeze(3).to_broadcast([NT * GB, HT, GB, T]),
                                        ALU.mult).then_inc(last_pd_ready, 1)

            def add_output(pair):
                dve.wait_ge(out_turned, pair + 1)
                both = m.x[:, bass.ds(pair * 2, 2), :]
                nc.vector.tensor_tensor(both, both, mixed_bank[:, 0:2 * P].rearrange("p (g e) -> p g e", g=2),
                                        ALU.add).then_inc(out_added, 1)

            def step(n, u, group, pair, tail):
                s = (1 + u) % UN
                j = s % GB
                for c in range(CH):
                    chunk_low(n - 1, (s - 1) % 2, c)
                    if c == 0 and j == 0:
                        spread_last(group - 1, 1 - s // GB, pair)
                    if not tail or n + 1 < B:
                        maxima(n + 1, (s + 1) % 2, c)
                if s == 2 and not early(pair, 1):
                    add_output(pair - 1)
                if not tail or n + 1 < B:
                    inverses(n + 1, (s + 1) % 2)
                made = group * 4 + (5 + j)
                if not tail or made < 4 * NG:
                    queries_low((s // GB + (2 if j == 3 else 1)) % 2, (j + 1) % 4, made + 1)
                product_low(n - 1, (s - 1) % UN)

            for hb in range(4):
                queries_low(0, hb, hb + 1)
            for n in range(2):
                for pair in range(2):
                    maxima(n, n, pair)
                inverses(n, n)
            queries_low(1, 0, 5)
            queries_low(1, 1, 6)
            for n in range(1, UN + 1):
                step(n, n - 1, n // GB, n // UN, False)
            with dve.Fori(1, LOOPS) as i:
                for u in range(UN):
                    step(i * UN + (1 + u), u, i * (UN // GB) + (1 + u) // GB, i + (1 + u) // UN, False)
            for n in TAIL:
                step(n, (n - 1) % UN, n // GB, n // UN, True)
            for c in range(CH):
                chunk_low(B - 1, 1, c)
            product_low(B - 1, UN - 1)
            spread_last(NG - 1, 1, B // UN)
            add_output(B // UN - 1)

        @block.gpsimd
        def _(pool):
            def normalise(n, par, group, gpar, slot):
                pool.wait_ge(inv_ready, n + 1)
                if not early(n, 2 * GB):
                    pool.wait_ge(last_t_ready, group - 1)
                pool.tensor_tensor(last_p[:, gpar, :, slot], probs[:, par, :, S2 - 1], row_inv[:, par, :],
                                   ALU.mult).then_inc(last_p_ready, 1)
                pool.tensor_tensor(probs[:, par, :, 0:S2 - 1], probs[:, par, :, 0:S2 - 1],
                                   row_inv[:, par, :].unsqueeze(2).to_broadcast([P, NT, S2 - 1]), ALU.mult).then_inc(probs_ready, 1)

            def context_low(n, slot):
                pool.wait_ge(cx_high, n + 1)
                pool.tensor_tensor(cx[1][:, slot, :], raw[:, slot, :], cx[0][:, slot, :].bitcast(F32),
                                   ALU.subtract).then_inc(cx_low, 1)

            for n in range(3):
                context_low(n, n)
            for n in range(UN):
                normalise(n, n % 2, n // GB, n // GB, n % GB)
                context_low(n + 3, (n + 3) % GB)
            with pool.Fori(1, B // UN - 1) as i:
                for u in range(UN):
                    normalise(i * UN + u, u % 2, i * (UN // GB) + u // GB, u // GB, u % GB)
                    context_low(i * UN + (u + 3), (u + 3) % GB)
            for n in range(B - UN, B):
                normalise(n, n % 2, n // GB, n // GB % 2, n % GB)
                if n + 3 < B:
                    context_low(n + 3, (n + 3) % GB)


def differential_attention(nc, m):
    with ExitStack() as ctx:
        def sb(name, shape, dt=F32):
            return ctx.enter_context(nc.sbuf_tensor(name, shape, dt))

        def sem(name):
            return ctx.enter_context(nc.semaphore(name))

        xg = [sb(f"d_xg{k}", [P, 2, P], F32R) for k in range(2)]
        xw = sb("d_xw", [P, 2, P])
        q = sb("d_q", [P, 2, 2, GB, NC, T])
        v = sb("d_v", [P, 2, DE])
        e = sb("d_e", [P, 2, GB * 4, T])
        diff = sb("d_diff", [P, 2, 2, GB, T])
        wT = sb("d_wT", [P, 2, DH, GB, T])
        sq = sb("d_sq", [P, 2, DE])
        empty = sb("d_empty", [P, NTILE, SE])
        mx = sb("d_mx", [P, 2, GB * 4])
        sm = sb("d_sm", [P, 2, GB * 4])
        rc = sb("d_rc", [P, 2, GB * 4])
        rf = sb("d_rf", [P, 2, GB * 4])

        xg_ready = sem("d_xg_ready")
        q_ready = sem("d_q_ready")
        q_out = sem("d_q_out")
        v_ready = sem("d_v_ready")
        v_out = sem("d_v_out")
        scores_ready = sem("d_scores_ready")
        max_ready = sem("d_max_ready")
        shifted = sem("d_shifted")
        exp_done = sem("d_exp_done")
        summed = sem("d_summed")
        scaled = sem("d_scaled")
        diff_ready = sem("d_diff_ready")
        diffT_ready = sem("d_diffT_ready")
        wT_zero = sem("d_wT_zero")
        wT_out = sem("d_wT_out")
        att_ready = sem("d_att_ready")
        att_out = sem("d_att_out")
        squares_summed = sem("d_squares_summed")

        qb = [m.bank[4], m.bank[5]]
        FIRST, LAST = 4, NG - 4
        tb = m.bank[6]
        vb = ab = m.bank[7]
        block = ctx.enter_context(nc.Block())

        @block.gpsimd
        def _(pool):
            for k in range(2):
                pool.memset(wT[:, k], 0.0).then_inc(wT_zero, 1)

            def stage(g, par):
                for a in range(2):
                    pool.tensor_copy(xg[a][:, par, :], m.xT[a][:, bass.ts(g, P)].bitcast(F32))
                pool.tensor_tensor(xw[:, par, :], m.xT[0][:, bass.ts(g, P)].bitcast(F32),
                                   m.xT[1][:, bass.ts(g, P)].bitcast(F32), ALU.add).then_inc(xg_ready, 1)

            def difference(g, par):
                pool.wait_ge(summed, g * 3 + 3)
                pool.tensor_tensor(e[:, par], e[:, par], rf[:, par].unsqueeze(2).to_broadcast([P, GB * 4, T]),
                                   ALU.mult).then_inc(scaled, 1)
                pool.wait_ge(scaled, g + 1)
                if not early(g, 2):
                    pool.wait_ge(diffT_ready, g - 1)
                ev = e[:, par].rearrange("p (b c u) k -> p c u b k", b=GB, c=2)
                pool.tensor_tensor(diff[:, par], ev[:, 0], ev[:, 1], ALU.add).then_inc(diff_ready, 1)

            def step(g, s):
                if not early(g, 1):
                    pool.wait_ge(v_ready, g)
                if not isinstance(g, int) or g + 1 < NG:
                    stage(g + 1, (s + 1) % 2)
                difference(g, s % 2)

            stage(0, 0)
            for g in range(2):
                step(g, g)
            pool.memset(empty[:], 0.0).then_inc(m.zeros_ready, 1)
            pool.wait_ge(m.zeros_ready, 1)
            pool.tensor_copy(empty[:, :, E], m.empty_rows).then_inc(m.zeros_ready, 1)
            pool.wait_ge(m.zeros_ready, 2)
            pool.dma_start(m.slot_rows.rearrange("(j p) d -> p j d", p=P), empty[:]).then_inc(m.slots_zeroed, 16)
            for g in range(2, FIRST):
                step(g, g)
            with pool.Fori(FIRST // 4, LAST // 4) as i:
                for s in range(4):
                    step(i * 4 + s, s)
            for g in range(LAST, NG):
                step(g, g - LAST)
            pool.wait_ge(m.slots_zeroed, 16)

        @block.tensor
        def _(pe):
            def queries(pair, half, k):
                for j in range(2):
                    last = product3(nc, qb[k % 2][:, j * 2 * P:(j + 1) * 2 * P], [a[:, 8 * half + 2 * k + j, :] for a in m.w_dd],
                                    [a[:, bass.ts(pair, 2 * P)] for a in m.xT], True, True)
                last.then_inc(q_ready, 1)

            def values(g, par):
                if not early(g, 2):
                    pe.wait_ge(att_out, g - 1)
                pe.wait_ge(xg_ready, g + 1)
                product3(nc, vb[:], [a[:, par, :] for a in xg], [a[:] for a in m.w_v], True, True).then_inc(v_ready, 1)

            def scores(g, s):
                pe.wait_ge(xg_ready, g + 1)
                if not early(g, 1):
                    pe.wait_ge(shifted, g)
                if s % 2 == 0:
                    pe.wait_ge(q_out, g * 4 + 8)
                for b in range(GB):
                    for cu in range(4):
                        last = nc.tensor.matmul(m.bank[b][:, cu * P:(cu + 1) * P], q[:, s // 2, s % 2, b, 4 * cu:4 * cu + 4, :],
                                                xw[:, s % 2, :], start=True, stop=True)
                last.then_inc(scores_ready, 1)

            def back(g, par):
                pe.wait_ge(diff_ready, g + 1)
                if not early(g, 1):
                    pe.wait_ge(wT_out, g)
                for u in range(2):
                    last = nc.tensor.transpose(tb[:, u * P:(u + 1) * P], diff[:, par, u].rearrange("p b k -> p (b k)"), m.ident)
                last.then_inc(diffT_ready, 1)

            def products(g, par):
                pe.wait_ge(wT_out, g + 1)
                pe.wait_ge(v_out, g + 2 if not isinstance(g, int) or g + 1 < NG else g + 1)
                if isinstance(g, int) and g == NG - 1:
                    pe.wait_ge(att_out, g)
                for h in range(DH):
                    last = nc.tensor.matmul(ab[:, 2 * DD * h:2 * DD * (h + 1)], wT[:, par, h], v[:, par, 2 * DD * h:2 * DD * (h + 1)],
                                            start=True, stop=True)
                last.then_inc(att_ready, 1)

            def step(g, s, pair):
                more = not isinstance(g, int) or g < NG - 2
                for k in range(4):
                    if more:
                        pe.wait_ge(q_out, g * 4 + (7 + k))
                        queries(pair, s % 2, k)
                    if k == 0 and not early(g, 1):
                        back(g - 1, (s - 1) % 2)
                    if k == 1:
                        values(g, s % 2)
                if not early(g, 1):
                    products(g - 1, (s - 1) % 2)
                if not isinstance(g, int) or g + 1 < NG:
                    scores(g + 1, (s + 1) % 4)

            for half in range(2):
                for k in range(4):
                    if half or k >= 2:
                        pe.wait_ge(q_out, 4 * half + k - 1)
                    queries(0, half, k)
            scores(0, 0)
            for g in range(FIRST):
                step(g, g, g // 2 + 1)
            with pe.Fori(FIRST // 4, LAST // 4) as i:
                for s in range(4):
                    step(i * 4 + s, s, i * 2 + (s // 2 + 1))
            for g in range(LAST, NG):
                step(g, g - LAST, g // 2 + 1)
            back(NG - 1, 1)
            products(NG - 1, 1)

        @block.scalar
        def _(act):
            def queries_out(n, pair_par, half, k):
                act.wait_ge(q_ready, n + 1)
                nc.scalar.copy(q[:, pair_par, :, :, 8 * half + 2 * k:8 * half + 2 * k + 2, :].rearrange("p g b h t -> p h (g b) t"),
                               qb[k % 2][:].rearrange("p (h a t) -> p h a t", h=2, t=T)).then_inc(q_out, 1)

            def values_out(g, par):
                act.wait_ge(v_ready, g + 1)
                if not early(g, 2):
                    act.wait_ge(att_ready, g - 1)
                nc.scalar.copy(v[:, par, :], vb[:]).then_inc(v_out, 1)

            def exponentials(g, par):
                act.wait_ge(shifted, g + 1)
                nc.scalar.activation(e[:, par], e[:, par], ACT.Exp, scale=DD ** -0.5).then_inc(exp_done, 1)

            def result_out(g, par):
                act.wait_ge(att_ready, g + 1)
                nc.scalar.copy(m.att[:, g, :], ab[:])
                if not early(g, 2):
                    act.wait_ge(squares_summed, g - 1)
                nc.scalar.activation(sq[:, par, :], ab[:], ACT.Square).then_inc(att_out, 1)

            def step(g, s):
                for k in range(4):
                    if not isinstance(g, int) or g < NG - 2:
                        if k == 0 and not early(g, 1):
                            act.wait_ge(scores_ready, g)
                        queries_out(g * 4 + (8 + k), (s // 2 + 1) % 2, s % 2, k)
                    if k == 0:
                        exponentials(g, s % 2)
                    if k == 1:
                        values_out(g, s % 2)
                if not early(g, 1):
                    result_out(g - 1, (s - 1) % 2)

            for half in range(2):
                for k in range(4):
                    queries_out(4 * half + k, 0, half, k)
            for g in range(FIRST):
                step(g, g)
            with act.Fori(FIRST // 4, LAST // 4) as i:
                for s in range(4):
                    step(i * 4 + s, s)
            for g in range(LAST, NG):
                step(g, g - LAST)
            result_out(NG - 1, 1)

        @block.vector
        def _(dve):
            dve.wait_ge(wT_zero, 2)
            own = m.own_scores

            def softmax_front(g, par):
                dve.wait_ge(scores_ready, g + 1)
                if not early(g, 2):
                    dve.wait_ge(diff_ready, g - 1)
                nc.vector.tensor_reduce(mx[:, par].rearrange("p (b c) -> p b c", b=GB), own, AX.X, ALU.max).then_inc(max_ready, 1)
                dve.wait_ge(max_ready, g + 1)
                nc.vector.tensor_tensor(e[:, par].rearrange("p (b c) k -> p b c k", b=GB), own,
                                        mx[:, par].rearrange("p (b c) -> p b c", b=GB).unsqueeze(3).to_broadcast([P, GB, 4, T]),
                                        ALU.subtract).then_inc(shifted, 1)

            def softmax_back(g, par):
                dve.wait_ge(exp_done, g + 1)
                nc.vector.tensor_reduce(sm[:, par], e[:, par], AX.X, ALU.add).then_inc(summed, 1)
                dve.wait_ge(summed, g * 3 + 1)
                nc.vector.reciprocal(rc[:, par], sm[:, par]).then_inc(summed, 1)
                dve.wait_ge(summed, g * 3 + 2)
                nc.vector.tensor_tensor(rf[:, par].rearrange("p (b c u) -> p b c u", b=GB, c=2),
                                        rc[:, par].rearrange("p (b c u) -> p b c u", b=GB, c=2),
                                        m.pair_factor[:].unsqueeze(1).unsqueeze(3).to_broadcast([P, GB, 2, 2]),
                                        ALU.mult).then_inc(summed, 1)

            def blocks_out(g, par):
                dve.wait_ge(diffT_ready, g + 1)
                if not early(g, 2):
                    dve.wait_ge(att_ready, g - 1)
                for b in range(GB):
                    rows = slice(T * b, T * (b + 1))
                    last = nc.vector.tensor_copy(wT[rows, par, :, b, :], tb[rows, 0:2 * P].rearrange("p (h t) -> p h t", h=DH))
                last.then_inc(wT_out, 1)

            def sum_squares(g, par):
                dve.wait_ge(att_out, g + 1)
                nc.vector.tensor_reduce(m.att_squares[:, bass.ts(g, DH)], sq[:, par, :].rearrange("p (h w) -> p h w", w=2 * DD),
                                        AX.X, ALU.add).then_inc(squares_summed, 1)

            def step(g, s):
                softmax_front(g, s % 2)
                if not early(g, 2):
                    sum_squares(g - 2, s % 2)
                if not early(g, 1):
                    blocks_out(g - 1, (s - 1) % 2)
                softmax_back(g, s % 2)

            for g in range(FIRST):
                step(g, g)
            with dve.Fori(FIRST // 4, LAST // 4) as i:
                for s in range(4):
                    step(i * 4 + s, s)
            for g in range(LAST, NG):
                step(g, g - LAST)
            blocks_out(NG - 1, 1)
            sum_squares(NG - 2, 0)
            sum_squares(NG - 1, 1)


def attention_output(nc, m):
    W = 2 * DD
    with ExitStack() as ctx:
        def sem(name):
            return ctx.enter_context(nc.semaphore(name))

        an = ctx.enter_context(nc.sbuf_tensor("o_an", [P, 2, DE], F32))
        anT = ctx.enter_context(nc.sbuf_tensor("o_anT", [P, 2, DE], F32))
        ss = ctx.enter_context(nc.sbuf_tensor("o_ss", [P, 4, NG * DH], F32))
        summed = sem("o_summed")
        root = sem("o_root")
        inv = sem("o_inv")
        an_ready = sem("o_an_ready")
        anT_ready = sem("o_anT_ready")
        anT_out = sem("o_anT_out")
        out_ready = sem("o_out_ready")
        added = sem("o_added")
        tb = m.bank[0:2]
        ob = m.bank[2:4]
        block = ctx.enter_context(nc.Block())

        @block.scalar
        def _(act):
            act.wait_ge(summed, 1)
            nc.scalar.activation(ss[:, 2], ss[:, 1], ACT.Sqrt).then_inc(root, 1)

            def turned_out(g, par):
                act.wait_ge(anT_ready, g + 1)
                if not early(g, 2):
                    act.wait_ge(out_ready, g - 1)
                nc.scalar.copy(anT[:, par, :], tb[par][:]).then_inc(anT_out, 1)

            for g in range(NG):
                turned_out(g, g % 2)

        @block.vector
        def _(dve):
            nc.vector.tensor_scalar(ss[:, 1], m.att_squares[:], 1.0 / W, None, ALU.mult).then_inc(summed, 1)
            dve.wait_ge(root, 1)
            nc.vector.tensor_scalar(ss[:, 3], ss[:, 2], RMS_EPS, None, ALU.add).then_inc(inv, 1)
            dve.wait_ge(inv, 1)
            nc.vector.reciprocal(ss[:, 0], ss[:, 3]).then_inc(inv, 1)

            def add(g, par):
                dve.wait_ge(out_ready, g + 1)
                nc.vector.tensor_tensor(m.x[:, g, :], m.x[:, g, :], ob[par][:, 0:E], ALU.add).then_inc(added, 1)

            for g in range(NG):
                add(g, g % 2)

        @block.gpsimd
        def _(pool):
            pool.wait_ge(inv, 2)

            def normalise(g, par):
                if not early(g, 2):
                    pool.wait_ge(anT_ready, g - 1)
                pool.tensor_tensor(an[:, par, :].rearrange("p (h w) -> p h w", w=W),
                                   m.att[:, g, :].rearrange("p (h w) -> p h w", w=W),
                                   ss[:, 0, bass.ts(g, DH)].unsqueeze(2).to_broadcast([P, DH, W]), ALU.mult).then_inc(an_ready, 1)

            normalise(0, 0)
            normalise(1, 1)
            with pool.Fori(1, NG // 2) as k:
                for par in range(2):
                    normalise(k * 2 + par, par)

        @block.tensor
        def _(pe):
            def turn(g, par):
                pe.wait_ge(an_ready, g + 1)
                if not early(g, 2):
                    pe.wait_ge(anT_out, g - 1)
                for j in range(4):
                    last = nc.tensor.transpose(tb[par][:, j * P:(j + 1) * P], an[:, par, j * P:(j + 1) * P], m.ident)
                last.then_inc(anT_ready, 1)

            def out(g, par):
                pe.wait_ge(anT_out, g + 1)
                if not early(g, 2):
                    pe.wait_ge(added, g - 1)
                for j in range(4):
                    last = nc.tensor.matmul(ob[par][:, 0:E], anT[:, par, j * P:(j + 1) * P], m.w_out[:, j, :],
                                            start=(j == 0), stop=(j == 3))
                last.then_inc(out_ready, 1)

            turn(0, 0)
            turn(1, 1)
            out(0, 0)
            with pe.Fori(1, NG // 2) as k:
                for par in range(2):
                    g = k * 2 + par
                    turn(g, par)
                    out(g - 1, 1 - par)
            out(NG - 1, 1)


def route(nc, m):
    with ExitStack() as ctx:
        def sb(name, shape, dt=F32):
            return ctx.enter_context(nc.sbuf_tensor(name, shape, dt))

        lg = sb("r_lg", [P, NG, NR])
        oh = sb("r_oh", [P, 2, NG, NR])
        tmp = sb("r_tmp", [P, 2, NG, NR])
        top = sb("r_top", [P, 8, NG])
        chosen = sb("r_chosen", [P, NG + 1, NR])
        place = sb("r_place", [P, NG, NR])
        full = sb("r_full", [P, NR, NG])
        tiles = sb("r_tiles", [P, NR])
        ends = sb("r_ends", [P, NR])
        starts = sb("r_starts", [P, NR])
        passed = sb("r_passed", [P, NTILE, NR])
        slot_f = sb("r_slot_f", [P, 2, NG])
        owner = sb("r_owner", [P, 2, NTILE])
        chosen_zero = ctx.enter_context(nc.semaphore("r_chosen_zero"))
        chosen_ready = ctx.enter_context(nc.semaphore("r_chosen_ready"))
        rank_ready = ctx.enter_context(nc.semaphore("r_rank_ready"))
        logits_ready = ctx.enter_context(nc.semaphore("r_logits_ready"))
        chain = ctx.enter_context(nc.semaphore("r_chain"))
        gap_ready = ctx.enter_context(nc.semaphore("r_gap_ready"))
        exp_ready = ctx.enter_context(nc.semaphore("r_exp_ready"))
        block = ctx.enter_context(nc.Block())

        @block.tensor
        def _(pe):
            for g in range(NG):
                last = product3(nc, m.bank[4][:, 8 * g:8 * g + 8], [a[:, g * P:(g + 1) * P] for a in m.xT],
                                [a[:] for a in m.router], True, True)
            last.then_inc(logits_ready, 1)
            pe.wait_ge(chosen_ready, 1)
            rank = m.bank[5][:, 0:(NG + 1) * NR].rearrange("p (g e) -> p g e", e=NR)
            nc.tensor.matmul(rank, m.ahead, chosen[:], start=True, stop=False)
            for g in range(NG):
                last = nc.tensor.matmul(rank[:, g + 1:NG + 1, :], m.ones,
                                        chosen[:, g:g + 1, :].to_broadcast([P, NG - g, NR]),
                                        start=False, stop=(g == NG - 1))
            last.then_inc(rank_ready, 1)

        @block.scalar
        def _(act):
            for k in range(2):
                nc.scalar.copy(m.slot_source[:, k, :, 0:E], m.xn[:])
            weights_high(nc, m, act, NE // 2)
            weights_high(nc, m, act, NE // 2 + 1)
            act.wait_ge(gap_ready, 1)
            nc.scalar.activation(top[:, 3], top[:, 2], ACT.Exp).then_inc(exp_ready, 1)
            weights_high(nc, m, act, NE // 2 + 2)
            weights_high(nc, m, act, NE // 2 + 3)

        @block.sync
        def _(sp):
            load_weights(m, sp, range(NE // 2, NE))

        @block.vector
        def _(dve):
            def wide(a):
                return a.unsqueeze(2).to_broadcast([P, NG, NR])

            nc.vector.tensor_copy(m.slot_source[:, :, :, E], m.token_rows.rearrange("p (k g) -> p k g", k=2))
            preference = m.preference[:].unsqueeze(1).to_broadcast([P, NG, NR])
            dve.wait_ge(logits_ready, 1)
            nc.vector.tensor_copy(lg[:], m.bank[4][:, 0:8 * NG].rearrange("p (g e) -> p g e", e=8)[:, :, 0:NR]).then_inc(chain, 1)
            n = 1
            for k in range(2):
                dve.wait_ge(chain, n)
                nc.vector.tensor_reduce(top[:, k], lg[:], AX.X, ALU.max).then_inc(chain, 1)
                dve.wait_ge(chain, n + 1)
                nc.vector.tensor_tensor(tmp[:, 0], lg[:], wide(top[:, k]), ALU.is_equal).then_inc(chain, 1)
                dve.wait_ge(chain, n + 2)
                nc.vector.tensor_tensor(tmp[:, 1], tmp[:, 0], preference, ALU.mult).then_inc(chain, 1)
                dve.wait_ge(chain, n + 3)
                nc.vector.tensor_reduce(top[:, 7], tmp[:, 1], AX.X, ALU.max).then_inc(chain, 1)
                dve.wait_ge(chain, n + 4)
                nc.vector.tensor_tensor(oh[:, k], tmp[:, 1], wide(top[:, 7]), ALU.is_equal).then_inc(chain, 1)
                n += 5
                if k == 0:
                    dve.wait_ge(chain, n)
                    nc.vector.scalar_tensor_tensor(lg[:], oh[:, 0], LOW, lg[:], ALU.mult, ALU.add).then_inc(chain, 1)
                    n += 1
            dve.wait_ge(chain, n)
            nc.vector.tensor_tensor(top[:, 2], top[:, 1], top[:, 0], ALU.subtract).then_inc(gap_ready, 1)
            dve.wait_ge(chosen_zero, 1)
            nc.vector.tensor_tensor(chosen[:, 0:NG, :], oh[:, 0], oh[:, 1], ALU.add).then_inc(chosen_ready, 1)
            dve.wait_ge(exp_ready, 1)
            nc.vector.tensor_scalar(top[:, 4], top[:, 3], 1.0, None, ALU.add).then_inc(chain, 1)
            dve.wait_ge(chain, n + 1)
            nc.vector.reciprocal(top[:, 5], top[:, 4]).then_inc(chain, 1)
            dve.wait_ge(chain, n + 2)
            nc.vector.tensor_tensor(top[:, 6], top[:, 5], top[:, 3], ALU.mult).then_inc(chain, 1)
            dve.wait_ge(chain, n + 3)
            nc.vector.tensor_copy(m.slot_source[:, :, :, E + 1], top[:, 5:7]).then_inc(chain, 1)
            n += 4

            def then(make):
                nonlocal n
                dve.wait_ge(chain, n)
                make().then_inc(chain, 1)
                n += 1

            rank = m.bank[5][:, 0:(NG + 1) * NR].rearrange("p (g e) -> p g e", e=NR)
            dve.wait_ge(rank_ready, 1)
            then(lambda: nc.vector.tensor_copy(starts[:], rank[:, NG, :]))
            then(lambda: nc.vector.tensor_tensor(full[:], starts[:].unsqueeze(2).to_broadcast([P, NR, NG]),
                                                 m.multiples.unsqueeze(1).to_broadcast([P, NR, NG]), ALU.is_gt))
            then(lambda: nc.vector.tensor_reduce(tiles[:], full[:], AX.X, ALU.add))
            then(lambda: nc.vector.tensor_tensor_scan(ends[:], m.ones[:, 0:NR], tiles[:], 0.0, ALU.mult, ALU.add))
            then(lambda: nc.vector.tensor_tensor(starts[:], ends[:], tiles[:], ALU.subtract))
            then(lambda: nc.vector.tensor_scalar(starts[:], starts[:], float(P), None, ALU.mult))
            then(lambda: nc.vector.tensor_tensor(place[:], rank[:, 0:NG, :], starts[:].unsqueeze(1).to_broadcast([P, NG, NR]),
                                                 ALU.add))
            for k in range(2):
                then(lambda: nc.vector.tensor_tensor(tmp[:, k], place[:], oh[:, k], ALU.mult))
                then(lambda: nc.vector.tensor_reduce(slot_f[:, k], tmp[:, k], AX.X, ALU.add))
            then(lambda: nc.vector.tensor_copy(m.slot[:], slot_f[:]))
            then(lambda: nc.vector.tensor_tensor(passed[:], ends[:].unsqueeze(1).to_broadcast([P, NTILE, NR]),
                                                 m.tile_numbers.unsqueeze(2).to_broadcast([P, NTILE, NR]), ALU.is_le))
            then(lambda: nc.vector.tensor_reduce(owner[:, 0], passed[:], AX.X, ALU.add))
            then(lambda: nc.vector.tensor_scalar(owner[:, 1], owner[:, 0], float(NR - 1), None, ALU.min))
            then(lambda: nc.vector.tensor_copy(m.tile_expert[:], owner[:, 1]))

        @block.gpsimd
        def _(pool):
            pool.memset(chosen[:, NG, :], 0.0).then_inc(chosen_zero, 1)
            weights_low(m, pool, range(NE // 2, NE))


def experts(nc, m, out):
    with ExitStack() as ctx:
        def sb(name, shape, dt=F32):
            return ctx.enter_context(nc.sbuf_tensor(name, shape, dt))

        def sem(name):
            return ctx.enter_context(nc.semaphore(name))

        rows = sb("f_rows", [P, 4, SE])
        meta = sb("f_meta", [P, 4, 2])
        place = sb("f_place", [P, 4], mybir.dt.uint32)
        xg = [sb(f"f_xg{k}", [P, 2, P], F32R) for k in range(2)]
        gate = sb("f_gate", [P, 2, HID])
        h = sb("f_h", [P, 2, HID])
        hT = [sb(f"f_hT{k}", [P, 2, HID], F32R) for k in range(2)]
        ysb = sb("f_ysb", [P, 4, E])
        back = sb("f_back", [P, 2, NG, E])
        scattered = sem("f_scattered")
        rows_loaded = [sem(f"f_rows_loaded{s}") for s in range(4)]
        rowsT_ready = sem("f_rowsT_ready")
        xg_high = sem("f_xg_high")
        xg_ready = sem("f_xg_ready")
        g_ready = sem("f_g_ready")
        u_ready = sem("f_u_ready")
        gate_ready = sem("f_gate_ready")
        h_ready = sem("f_h_ready")
        hT_ready = sem("f_hT_ready")
        hT_high = sem("f_hT_high")
        hT_out = sem("f_hT_out")
        y_ready = sem("f_y_ready")
        y_out = sem("f_y_out")
        y_stored = [sem(f"f_y_stored{s}") for s in range(4)]
        back_loaded = [sem(f"f_back_loaded{k}") for k in range(NG // 4)]
        mixed = sem("f_mixed")
        y_part = sem("f_y_part")
        stored = sem("f_stored")
        gb, ub, tb, yb, rb = m.bank[0:2], m.bank[2:4], m.bank[4:6], m.bank[6], m.bank[7]
        JOBS = NG + NTILE
        block = ctx.enter_context(nc.Block())

        @block.gpsimd
        def _(pool):
            for g in range(NG):
                for k in range(2):
                    pool.indirect_dma_start(m.slot_rows[:, :], bass.IndirectOffsetOnAxis(m.slot[:, k, g:g + 1], 0),
                                            m.slot_source[:, k, g, :], None).then_inc(scattered, 16)

            for j in range(NTILE):
                s = j % 4
                pool.wait_ge(y_out, j + NG + 1)
                pool.indirect_dma_start(m.results[:, :], bass.IndirectOffsetOnAxis(place[:, s:s + 1], 0),
                                        ysb[:, s, :], None).then_inc(y_stored[s], 16)

        @block.sync
        def _(sp):
            def load(j, s):
                if not early(j, 4):
                    sp.wait_ge(xg_ready, j + (NG - 3))
                sp.dma_start(rows[:, s, :], m.slot_rows[bass.ts(j, P), :]).then_inc(rows_loaded[s], 16)

            sp.wait_ge(scattered, 16 * 2 * NG)
            for j in range(4):
                load(j, j)
            with sp.Fori(1, NTILE // 4) as i:
                for s in range(4):
                    load(i * 4 + s, s)
            for j in range(NTILE // 4 * 4, NTILE):
                load(j, j % 4)
            for s in range(4):
                sp.wait_ge(y_stored[s], 16 * len(range(s, NTILE, 4)))
            rv = m.results[0:2 * TOK, :].rearrange("(k g p) e -> p k g e", k=2, p=P)
            for q in range(NG // 4):
                part = slice(4 * q, 4 * q + 4)
                for k in range(2):
                    sp.dma_start(back[:, k, part, :], rv[:, k, part, :]).then_inc(back_loaded[q], 16)
            ov = out.rearrange("(g p) d -> p g d", p=P)
            for k in range(NG // 4):
                sp.wait_ge(mixed, 2 * (k + 1))
                sp.dma_start(ov[:, 4 * k:4 * k + 4, :], m.x[:, 4 * k:4 * k + 4, :]).then_inc(stored, 16)
            sp.wait_ge(stored, 16 * (NG // 4))

        @block.tensor
        def _(pe):
            def expert_of(n):
                if isinstance(n, int) and n < NG:
                    return NR
                return pe.value_load(m.tile_expert[0:1, bass.ds(n - NG, 1)], min_val=0, max_val=NR - 1)

            def turn_rows(n, s):
                pe.wait_ge(rows_loaded[s], (n - NG - s) * 4 + 16)
                if not early(n, NG + 1):
                    pe.wait_ge(xg_ready, n)
                nc.tensor.transpose(rb[:, 0:P], rows[:, s, 0:E], m.ident).then_inc(rowsT_ready, 1)

            def up(n, par, e):
                pe.wait_ge(xg_ready, n + 1)
                if not early(n, 2):
                    pe.wait_ge(gate_ready, n - 1)
                product3(nc, gb[par][:], [a[:, par, :] for a in xg], [a[:, e, 0:HID] for a in m.w_exp], True, True).then_inc(g_ready, 1)
                if not early(n, 2):
                    pe.wait_ge(h_ready, n - 1)
                product3(nc, ub[par][:], [a[:, par, :] for a in xg], [a[:, e, HID:2 * HID] for a in m.w_exp], True, True).then_inc(u_ready, 1)

            def turn(n, par):
                pe.wait_ge(h_ready, n + 1)
                if not early(n, 2):
                    pe.wait_ge(hT_out, n - 1)
                for j in range(KT):
                    last = nc.tensor.transpose(tb[par][:, j * P:(j + 1) * P], h[:, par, j * P:(j + 1) * P], m.ident)
                last.then_inc(hT_ready, 1)

            def down(n, par, e):
                pe.wait_ge(hT_out, n + 1)
                if not early(n, 1):
                    pe.wait_ge(y_out, n)
                def high(j):
                    return nc.tensor.matmul(yb[:, 0:2 * E], hT[0][:, par, j * P:(j + 1) * P],
                                            m.w_exp_parts[:, :, e, 2 * HID + j * E:2 * HID + (j + 1) * E],
                                            start=(j == 0), stop=(j == KT - 1))

                high(0)
                for j in range(KT):
                    nc.tensor.matmul(yb[:, E:2 * E], hT[1][:, par, j * P:(j + 1) * P],
                                     m.w_exp[0][:, e, 2 * HID + j * E:2 * HID + (j + 1) * E], start=False, stop=False)
                for j in range(1, KT):
                    last = high(j)
                last.then_inc(y_ready, 1)

            def step(n, par, shared, shared_before, rows_next):
                if rows_next is not None:
                    turn_rows(n + 1, rows_next)
                up(n, par, NR if shared else expert_of(n))
                if not early(n, 1):
                    turn(n - 1, 1 - par)
                if not early(n, 2):
                    down(n - 2, par, NR if shared_before else expert_of(n - 2))

            for n in range(2):
                step(n, n, True, True, None)
            with pe.Fori(1, NG // 2 - 1) as k:
                for par in range(2):
                    step(k * 2 + par, par, True, True, None)
            for n in range(NG - 2, NG + 4):
                step(n, n % 2, n < NG, n - 2 < NG, (n + 1 - NG) % 4 if n + 1 >= NG else None)
            with pe.Fori(NG // 4 + 1, JOBS // 4) as i:
                for s in range(4):
                    step(i * 4 + s, s % 2, False, False, (s + 1) % 4)
            for n in range(JOBS // 4 * 4, JOBS):
                step(n, n % 2, False, False, (n + 1) % 4 if n + 1 < JOBS else None)
            turn(JOBS - 1, 1)
            down(JOBS - 2, 0, expert_of(JOBS - 2))
            down(JOBS - 1, 1, expert_of(JOBS - 1))

        @block.scalar
        def _(act):
            def slot_rows_out(n, par):
                act.wait_ge(rowsT_ready, n - (NG - 1))
                act.wait_ge(u_ready, n - 1)
                nc.scalar.copy(xg[0][:, par, :], rb[:, 0:P]).then_inc(xg_high, 1)

            def group_rows(n, par):
                if not early(n, 2):
                    act.wait_ge(u_ready, n - 1)
                nc.scalar.copy(xg[0][:, par, :], m.xT[0][:, bass.ts(n, P)].bitcast(F32)).then_inc(xg_high, 1)

            def turned(n, par):
                act.wait_ge(hT_ready, n + 1)
                if not early(n, 2):
                    act.wait_ge(y_ready, n - 1)
                nc.scalar.copy(hT[0][:, par, :], tb[par][:]).then_inc(hT_high, 1)

            def step(n, par, from_group):
                if from_group is True:
                    group_rows(n + 1, 1 - par)
                elif from_group is False:
                    slot_rows_out(n + 1, 1 - par)
                act.wait_ge(g_ready, n + 1)
                if not early(n, 2):
                    act.wait_ge(h_ready, n - 1)
                nc.scalar.activation(gate[:, par, :], gb[par][:], ACT.Silu).then_inc(gate_ready, 1)
                if not early(n, 1):
                    turned(n - 1, 1 - par)

            group_rows(0, 0)
            for n in range(2):
                step(n, n, True)
            with act.Fori(1, NG // 2 - 1) as k:
                for par in range(2):
                    step(k * 2 + par, par, True)
            for n in range(NG - 2, NG + 4):
                step(n, n % 2, n + 1 < NG)
            with act.Fori(NG // 2 + 2, JOBS // 2 - 1) as k:
                for par in range(2):
                    step(k * 2 + par, par, False)
            step(JOBS - 2, 0, False)
            step(JOBS - 1, 1, None)
            turned(JOBS - 1, 1)

        @block.vector
        def _(dve):
            def result_out(n, slot):
                dve.wait_ge(y_ready, n + 1)
                if slot is None:
                    nc.vector.tensor_tensor(m.x[:, n, :], m.x[:, n, :], yb[:, 0:E], ALU.add).then_inc(y_part, 1)
                    dve.wait_ge(y_part, n + 1)
                    nc.vector.tensor_tensor(m.x[:, n, :], m.x[:, n, :], yb[:, E:2 * E], ALU.add).then_inc(y_out, 1)
                else:
                    if not early(n, NG + 4):
                        dve.wait_ge(y_stored[slot], (n - NG - slot) * 4)
                    nc.vector.tensor_copy(place[:, slot:slot + 1], meta[:, slot, 0:1])
                    nc.vector.tensor_scalar(ysb[:, slot, :], yb[:, 0:E], meta[:, slot, 1:2], None, ALU.mult).then_inc(y_part, 1)
                    dve.wait_ge(y_part, n + 1)
                    nc.vector.scalar_tensor_tensor(ysb[:, slot, :], yb[:, E:2 * E], meta[:, slot, 1:2], ysb[:, slot, :],
                                                   ALU.mult, ALU.add).then_inc(y_out, 1)

            def rows_low(n, par, from_group, slot):
                dve.wait_ge(xg_high, n + 1)
                if from_group:
                    nc.vector.tensor_copy(xg[1][:, par, :], m.xT[1][:, bass.ts(n, P)].bitcast(F32)).then_inc(xg_ready, 1)
                else:
                    if not early(n, NG + 4):
                        dve.wait_ge(y_out, n - 3)
                    nc.vector.tensor_copy(meta[:, slot, :], rows[:, slot, E:SE])
                    nc.vector.tensor_tensor(xg[1][:, par, :], rb[:, 0:P], xg[0][:, par, :].bitcast(F32),
                                            ALU.subtract).then_inc(xg_ready, 1)

            def turned_low(n, par):
                dve.wait_ge(hT_high, n + 1)
                nc.vector.tensor_tensor(hT[1][:, par, :], tb[par][:], hT[0][:, par, :].bitcast(F32),
                                        ALU.subtract).then_inc(hT_out, 1)

            def step(n, par, slot, from_group, next_slot=None):
                if from_group is not None:
                    rows_low(n + 1, 1 - par, from_group, next_slot)
                dve.wait_ge(gate_ready, n + 1)
                dve.wait_ge(u_ready, n + 1)
                if not early(n, 2):
                    dve.wait_ge(hT_ready, n - 1)
                nc.vector.tensor_tensor(h[:, par, :], gate[:, par, :], ub[par][:], ALU.mult).then_inc(h_ready, 1)
                if not early(n, 1):
                    turned_low(n - 1, 1 - par)
                if not early(n, 2):
                    result_out(n - 2, slot)

            rows_low(0, 0, True, None)
            for n in range(2):
                step(n, n, None, True)
            with dve.Fori(1, NG // 2 - 1) as k:
                for par in range(2):
                    step(k * 2 + par, par, None, True)
            for n in range(NG - 2, NG + 8):
                step(n, n % 2, None if n - 2 < NG else (n - 2) % 4, n + 1 < NG, (n + 1) % 4)
            with dve.Fori(NG // 4 + 2, JOBS // 4) as i:
                for s in range(4):
                    step(i * 4 + s, s % 2, (s + 2) % 4, False, (s + 1) % 4)
            for n in range(JOBS // 4 * 4, JOBS):
                step(n, n % 2, (n - 2) % 4, False if n + 1 < JOBS else None, (n + 1) % 4)
            turned_low(JOBS - 1, 1)
            for n in range(JOBS - 2, JOBS):
                result_out(n, n % 4)
            for q in range(NG // 4):
                dve.wait_ge(back_loaded[q], 32)
                part = slice(4 * q, 4 * q + 4)
                for k in range(2):
                    if k:
                        dve.wait_ge(mixed, 2 * q + 1)
                    nc.vector.tensor_tensor(m.x[:, part, :], m.x[:, part, :], back[:, k, part, :], ALU.add).then_inc(mixed, 1)


def perceiver_layer(nc, ins, out):
    with ExitStack() as ctx:
        m = Shared()

        def buffers(stack):
            def sb(name, shape, dt=F32):
                return stack.enter_context(nc.sbuf_tensor(name, shape, dt))
            return sb

        sb = buffers(ctx)

        def pair(make, name, shape):
            return [make(f"{name}{k}", shape, F32R) for k in range(2)]

        def sem(name):
            return ctx.enter_context(nc.semaphore(name))

        psum = ctx.enter_context(nc.psum_tensor("banks", [P, 8, 512], F32))
        m.bank = [psum[:, k, :] for k in range(8)]
        m.scores = psum[:, 0:NT, :]
        step = 512 + T
        m.own_scores = bass.AP(psum, 0, [[8 * 512, P], [step, GB], [P, 4], [1, T]])
        m.x = sb("x", [P, NG, E])
        m.xn = sb("xn", [P, NG, E])
        m.xT = pair(sb, "xT", [P, TOK])
        m.stat = sb("stat", [P, 4, NG])
        m.consts = sb("consts", [P, 3 * P + NR + 3 * NG + 2 * NTILE])
        m.ident, m.ahead, m.ones = (m.consts[:, k * P:(k + 1) * P] for k in range(3))
        m.preference = m.consts[:, 3 * P:3 * P + NR]
        m.multiples = m.consts[:, 3 * P + NR:3 * P + NR + NG]
        at = 3 * P + NR + NG
        m.tile_numbers = m.consts[:, at:at + NTILE]
        at += NTILE
        m.token_rows = m.consts[:, at:at + 2 * NG]
        m.empty_rows = m.consts[:, at + 2 * NG:]
        m.own_entry = sb("own_entry", [NT * GB, GB])
        m.w_out = sb("w_out", [P, DE // P, E])
        m.router_in = sb("router_in", [P, NE])
        m.router = pair(sb, "router", [P, NE])
        m.gamma_in = sb("gamma_in", [P, 1])
        m.gamma = sb("gamma", [P, 1])
        m.lam_in = sb("lam_in", [P, 4, DD])
        m.lam_prod = sb("lam_prod", [P, 2, DD])
        m.lam = sb("lam", [P, 5])
        m.pair_factor = sb("pair_factor", [P, 2])
        m.slot = sb("slot", [P, 2, NG], mybir.dt.uint32)
        m.tile_expert = sb("tile_expert", [P, NTILE], mybir.dt.int32)
        m.slot_rows = nc.dram_tensor("slot_rows", [NTILE * P, SE], F32, kind="Internal").ap()
        m.results = nc.dram_tensor("results", [2 * TOK + NTILE * P, E], F32, kind="Internal").ap()
        m.v_scratch = nc.dram_tensor("v_scratch", [B, H * E], F32, kind="Internal").ap()
        m.expert_sources = [(ins["w_gate"][e], ins["w_up"][e], ins["w_down"][e]) for e in range(NR)]
        m.expert_sources.append((ins["sw_gate"][0], ins["sw_up"][0], ins["sw_down"][0]))

        m.x_loaded = sem("x_loaded")
        m.consts_loaded = sem("consts_loaded")
        m.aw_loaded = sem("aw_loaded")
        m.mask_loaded = sem("mask_loaded")
        m.misc_loaded = sem("misc_loaded")
        m.self_loaded = sem("self_loaded")
        m.v_stored = sem("v_stored")
        m.folded = sem("folded")
        m.folded_high = sem("folded_high")
        m.folded_out = sem("folded_out")
        m.row_high = sem("row_high")
        m.raw_loaded = [sem(f"raw_loaded{k}") for k in range(2)]
        m.raw_high = sem("raw_high")
        m.raw_low = sem("raw_low")
        m.zeros_ready = sem("zeros_ready")
        m.slots_zeroed = sem("slots_zeroed")

        with ExitStack() as cross:
            cb = buffers(cross)
            m.mask_add = cb("mask_add", [P, NG, S2], BF16)
            m.spread = cb("spread", [P, GB, P], BF16)
            m.w_qk = pair(cb, "w_qk", [P, H, P])
            m.w_vo = pair(cb, "w_vo", [P, H, P])
            with ExitStack() as early:
                eb = buffers(early)
                m.sq = eb("sq1", [P, NG, E])
                m.aw = eb("aw", [DK, 4, H, P])
                m.last_row = eb("last_row", [P, P])
                m.row_parts = pair(eb, "row_parts", [P, P])
                m.v_rows = eb("v_rows", [B, 4, 512])
                m.mask_in = eb("mask_in", [P, NG, S2], U8)
                with nc.Block() as block:
                    @block.sync
                    def _(sp):
                        xs = ins["x"].rearrange("(g p) d -> p g d", p=P)
                        for k in range(2):
                            half = slice(NG // 2 * k, NG // 2 * (k + 1))
                            sp.dma_start(m.x[:, half, :], xs[:, half, :]).then_inc(m.x_loaded, 16)
                        sp.dma_start(m.aw[:], ins["aw"]).then_inc(m.aw_loaded, 16)
                        sp.dma_start(m.consts[:], ins["consts"]).then_inc(m.consts_loaded, 16)
                        sp.dma_start(m.mask_in[:], ins["mask"].rearrange("(g p) t -> p g t", p=P)).then_inc(m.mask_loaded, 16)

                    @block.scalar
                    def _(act):
                        for dst, name in ((m.last_row, "last_row"), (m.own_entry, "own_entry"), (m.spread, "spread"),
                                          (m.w_out, "w_out"), (m.router_in, "router"),
                                          (m.gamma_in, "gamma"), (m.lam_in, "lam")):
                            act.dma_start(dst[:], ins[name]).then_inc(m.misc_loaded, 16)
                layer_norm(nc, m, "ln1")
                finish_folding(nc, m)
            cross_attention(nc, m, ins["ctx_pack"])
        result = ctx.enter_context(ExitStack())
        m.att = buffers(result)("att", [P, NG, DE])
        m.att_squares = buffers(result)("att_squares", [P, NG * DH])
        with ExitStack() as attention:
            ab = buffers(attention)
            with ExitStack() as early:
                m.w_dd = pair(ab, "w_dd", [P, NC, P])
                m.w_v = pair(ab, "w_v", [P, DE])
                eb = buffers(early)
                m.sq = m.att[:, 0:NG * E // DE, :].rearrange("p a (b e) -> p (a b) e", e=E)
                m.dw = eb("dw", [DD, 2, NC, P])
                m.w_v_in = eb("w_v_in", [P, DE])
                with nc.Block() as block:
                    @block.sync
                    def _(sp):
                        sp.dma_start(m.dw[:], ins["dw"]).then_inc(m.self_loaded, 16)
                        sp.dma_start(m.w_v_in[:], ins["w_v"]).then_inc(m.self_loaded, 16)
                layer_norm(nc, m, "ln2")
                fold_self_weights(nc, m)
            differential_attention(nc, m)
        attention_output(nc, m)
        result.close()
        m.w_exp_parts = sb("w_exp", [P, 2, NE, EW], F32R)
        m.w_exp = [m.w_exp_parts[:, k] for k in range(2)]
        m.slot_source = sb("slot_source", [P, 2, NG, SE])
        with ExitStack() as mid:
            m.sq = buffers(mid)("sq3", [P, NG, E])
            m.raw = buffers(mid)("raw_weights", [P, 2, EW])
            layer_norm(nc, m, "ln3")
            route(nc, m)
        experts(nc, m, out)


def kernel(**inputs):
    from concourse import bacc
    from concourse.bass_utils import run_bass_kernel_spmd

    a = {k: np.ascontiguousarray(v) for k, v in inputs.items()}
    f32 = np.float32
    ctx = a["ctx_1024"]
    nat = ctx[:, :CH * P, :].reshape(B, CH, P, E).transpose(0, 2, 1, 3).reshape(B, P, CH * E)
    row = np.concatenate([np.arange(NR, 0, -1), P * np.arange(NG), np.arange(NTILE)]).astype(f32)
    rows = P * np.arange(2 * NG + NTILE) + np.arange(P)[:, None]
    consts = np.concatenate([np.eye(P, dtype=f32), np.triu(np.ones((P, P), f32), 1), np.ones((P, P), f32),
                             np.tile(row, (P, 1)), rows.astype(f32)], 1)
    spread = np.zeros((P, GB, P), f32)
    for b in range(GB):
        for t in range(T):
            spread[b * T + t, b, t::T] = 1.0
    import ml_dtypes

    def heads_first(w):
        return w.reshape(E, DH, 2, DD).transpose(3, 2, 1, 0).reshape(DD, NC, E)

    arrays = {
        "x": a["x"].reshape(TOK, E),
        "ctx_pack": np.concatenate([nat, ctx.transpose(0, 2, 1), np.zeros((B, P, 1), f32)], 2),
        "last_row": np.concatenate([ctx[:, S2 - 1, :].T, np.zeros((P, P - B), f32)], 1),
        "mask": a["mask_Bx1xSxS2_bf1"].reshape(TOK, S2).view(np.uint8),
        "aw": np.stack([a["L0_xattn_w_q"].transpose(2, 0, 1), a["L0_xattn_w_k"].transpose(2, 0, 1),
                        a["L0_xattn_w_v"].transpose(2, 0, 1), a["L0_xattn_w_o"].transpose(1, 0, 2)], 1),
        "dw": np.stack([heads_first(a["L0_attn_Wq"]), heads_first(a["L0_attn_Wkv"][:, :DE])], 1),
        "w_v": a["L0_attn_Wkv"][:, DE:],
        "w_out": a["L0_attn_Wout"].reshape(DE // P, P, E).transpose(1, 0, 2),
        "gamma": np.tile(a["L0_attn_gamma"], P // (2 * DD)).reshape(P, 1),
        "lam": np.tile(np.stack([a["L0_attn_lambda_q1"], a["L0_attn_lambda_q2"], a["L0_attn_lambda_k1"],
                                 a["L0_attn_lambda_k2"]])[None], (P, 1, 1)),
        "router": np.concatenate([a["L0_ffn_router_w"].T, np.zeros((E, 1), f32)], 1),
        "w_gate": a["L0_ffn_w_gate"], "w_up": a["L0_ffn_w_up"], "w_down": a["L0_ffn_w_down"],
        "sw_gate": a["L0_ffn_sw_gate"], "sw_up": a["L0_ffn_sw_up"], "sw_down": a["L0_ffn_sw_down"],
        "consts": consts,
        "own_entry": np.tile(np.eye(GB, dtype=f32), (NT, 1)),
        "spread": spread.astype(ml_dtypes.bfloat16),
    }
    arrays = {f"in_{k}": np.ascontiguousarray(v) for k, v in arrays.items()}
    nc = bacc.Bacc("TRN2", target_bir_lowering=False, num_devices=1)
    ins = {k[3:]: nc.dram_tensor(k, v.shape, mybir.dt.from_np(v.dtype), kind="ExternalInput").ap()
           for k, v in arrays.items()}
    out = nc.dram_tensor("out", (TOK, E), F32, kind="ExternalOutput").ap()
    perceiver_layer(nc, ins, out)
    r = run_bass_kernel_spmd(nc, [arrays], core_ids=[0])
    return r.results[0]["out"].reshape(B, T, E)
```

```python
import math
from contextlib import ExitStack

import numpy as np

import concourse.bass as bass
from concourse import mybir

F32 = mybir.dt.float32
F32R = mybir.dt.float32r
BF16 = mybir.dt.bfloat16
U8 = mybir.dt.uint8
ALU = mybir.AluOpType
ACT = mybir.ActivationFunctionType
AX = mybir.AxisListType

P = 128
B, T, E = 64, 32, 128
S2 = 257
H, DK = 16, 64
TOK = B * T
NG = TOK // P
GB = P // T
NT = H * T // P
HT = H // NT
CH = (S2 - 1) // P
PACK = CH * P + S2 + 1
XSCALE = 1.0 / math.sqrt(DK)
MASKED = -8e30

DH, DD = 8, 32
NC = 2 * DH
DE = 2 * DH * DD
LAMBDA_INIT = 0.8 - 0.6 * math.exp(-0.3 * 1)

NE, HID = 8, 512
NR = NE - 1
KT = HID // P
EW = 2 * HID + KT * E
NTILE = (2 * TOK + NR * (P - 1)) // P
NTILE += NTILE % 2
LN_EPS = 1e-5
RMS_EPS = 1e-8
SE = E + 2
LOW = -3.0e38


class Shared:
    pass


def early(n, k):
    return isinstance(n, int) and n < k


def product3(nc, out, stationary, moving, start, stop):
    nc.tensor.matmul(out, stationary[0], moving[0], start=start, stop=False)
    nc.tensor.matmul(out, stationary[0], moving[1], start=False, stop=False)
    return nc.tensor.matmul(out, stationary[1], moving[0], start=False, stop=stop)


BY_SCALAR = (1, 4, 7, 10, 12, 15)
BY_VECTOR = [g for g in range(NG) if g not in BY_SCALAR]


def layer_norm(nc, m, tag):
    with ExitStack() as ctx:
        moments_ready = ctx.enter_context(nc.semaphore(f"{tag}_moments_ready"))
        var_ready = ctx.enter_context(nc.semaphore(f"{tag}_var_ready"))
        std_ready = ctx.enter_context(nc.semaphore(f"{tag}_std_ready"))
        normed = ctx.enter_context(nc.semaphore(f"{tag}_normed"))
        normed_too = ctx.enter_context(nc.semaphore(f"{tag}_normed_too"))
        turned = ctx.enter_context(nc.semaphore(f"{tag}_turned"))
        turned_high = ctx.enter_context(nc.semaphore(f"{tag}_turned_high"))
        turned_out = ctx.enter_context(nc.semaphore(f"{tag}_turned_out"))
        banks = [m.bank[k] for k in ((0, 1, 6, 7) if tag == "ln1" else (0, 1, 2, 3))]
        block = ctx.enter_context(nc.Block())

        if tag == "ln1":
            @block.sync
            def _(sp):
                first_loads(m, sp)

        if tag == "ln2":
            @block.sync
            def _(sp):
                sp.dma_start(m.dw[:], m.ins["dw"]).then_inc(m.self_loaded, 16)
                sp.dma_start(m.w_v_in[:], m.ins["w_v"]).then_inc(m.self_loaded, 16)
                load_weights(m, sp, range(RAW))

        @block.vector
        def _(dve):
            if tag != "ln3":
                for g in range(NG):
                    if tag == "ln1" and g % (NG // 2) == 0:
                        dve.wait_ge(m.x_loaded[g // (NG // 2)], 16)
                    nc.vector.bn_stats(m.moments[:, g, :], m.x[:, g, :]).then_inc(moments_ready, 1)
                for g in range(NG):
                    dve.wait_ge(moments_ready, g + 1)
                    last = nc.vector.bn_aggr(m.mean_var[:, g, :], m.moments[:, g, :])
                last.then_inc(moments_ready, 1)
                dve.wait_ge(moments_ready, NG + 1)
            nc.vector.tensor_scalar(m.stat[:, 1, :], m.mean_var[:, :, 1], LN_EPS, None, ALU.add).then_inc(var_ready, 1)
            dve.wait_ge(std_ready, 1)
            nc.vector.reciprocal(m.stat[:, 3, :], m.stat[:, 2, :]).then_inc(std_ready, 1)
            dve.wait_ge(std_ready, 2)
            nc.vector.scalar_tensor_tensor(m.stat[:, 0, :], m.mean_var[:, :, 0], -1.0, m.stat[:, 3, :], ALU.mult,
                                           ALU.mult).then_inc(std_ready, 1)
            for g in BY_VECTOR:
                nc.vector.tensor_scalar(m.xn[:, g, :], m.x[:, g, :], m.mean_var[:, g, 0:1], m.stat[:, 3, g:g + 1],
                                        ALU.subtract, ALU.mult).then_inc(normed, 1)
            if tag == "ln2":
                split_self_low(nc, m, dve)
            if tag == "ln1":
                dve.wait_ge(m.row_high, 1)
                nc.vector.tensor_tensor(m.row_parts[1][:], m.last_row[:], m.row_parts[0][:].bitcast(F32), ALU.subtract)
                fold_low(nc, m, dve, 0)
            for k in range(NG // 4):
                part = slice(4 * P * k, 4 * P * (k + 1))
                dve.wait_ge(turned_high, k + 1)
                nc.vector.tensor_tensor(m.xT[1][:, part], banks[k][:], m.xT[0][:, part].bitcast(F32),
                                        ALU.subtract).then_inc(turned_out, 1)
                if tag == "ln1" and k == 0:
                    fold_low(nc, m, dve, 1)
            if tag == "ln1":
                for n in range(2, FOLDS):
                    fold_low(nc, m, dve, n)

        @block.scalar
        def _(act):
            if tag == "ln1":
                act.dma_start(m.consts[:], m.ins["consts"]).then_inc(m.consts_loaded, 16)
                act.dma_start(m.last_row[:], m.ins["last_row"]).then_inc(m.row_loaded, 16)
                for dst, name in ((m.own_entry, "own_entry"), (m.spread, "spread"),
                                  (m.w_out, "w_out"), (m.router_in, "router"),
                                  (m.gamma_in, "gamma"), (m.lam_in, "lam")):
                    act.dma_start(dst[:], m.ins[name]).then_inc(m.misc_loaded, 16)
            act.wait_ge(var_ready, 1)
            nc.scalar.activation(m.stat[:, 2, :], m.stat[:, 1, :], ACT.Sqrt).then_inc(std_ready, 1)
            act.wait_ge(std_ready, 3)
            for g in BY_SCALAR:
                nc.scalar.activation(m.xn[:, g, :], m.x[:, g, :], ACT.Identity, bias=m.stat[:, 0, g:g + 1],
                                     scale=m.stat[:, 3, g:g + 1]).then_inc(normed_too, 1)
            if tag == "ln2":
                split_self_high(nc, m, act)
            if tag == "ln1":
                act.wait_ge(m.row_loaded, 16)
                nc.scalar.copy(m.row_parts[0][:], m.last_row[:]).then_inc(m.row_high, 1)
                fold_high(nc, m, act, 0)
            for k in range(NG // 4):
                act.wait_ge(turned, k + 1)
                nc.scalar.copy(m.xT[0][:, 4 * P * k:4 * P * (k + 1)], banks[k][:]).then_inc(turned_high, 1)
                if tag == "ln1" and k == 0:
                    fold_high(nc, m, act, 1)
            if tag == "ln1":
                for n in range(2, FOLDS):
                    fold_high(nc, m, act, n)
                for n in range(3):
                    act.wait_ge(m.cx_loaded[n], 16)
                    nc.scalar.copy(m.cx[0][:, n, :], m.cx_raw[:, n, :]).then_inc(m.cx_high, 1)
                act.wait_ge(m.misc_loaded, 16 * 6)

        if tag == "ln1":
            @block.gpsimd
            def _(pool):
                pool.memset(m.pair_factor[:, 0:1], 1.0)
                pool.wait_ge(m.mask_loaded, 16)
                for k in range(4):
                    part = slice(NG // 4 * k, NG // 4 * (k + 1))
                    pool.tensor_scalar(m.mask_add[:, part, :], m.mask_in[:, part, :], -MASKED, MASKED, ALU.mult, ALU.add)

        @block.tensor
        def _(pe):
            if tag == "ln1":
                for n in range(2):
                    fold(nc, m, pe, n)
                pe.wait_ge(m.consts_loaded, 16)
            if tag == "ln2":
                fold_self(nc, m, pe)
            for k in range(NG // 4):
                pe.wait_ge(normed, sum(g < 4 * k + 4 for g in BY_VECTOR))
                pe.wait_ge(normed_too, sum(g < 4 * k + 4 for g in BY_SCALAR))
                for j in range(4):
                    last = nc.tensor.transpose(banks[k][:, j * P:(j + 1) * P], m.xn[:, 4 * k + j, :],
                                               m.ident)
                last.then_inc(turned, 1)
            if tag == "ln1":
                for n in range(2, FOLDS):
                    fold(nc, m, pe, n)
            if tag == "ln3":
                for k in range(NG // 4):
                    router_logits(nc, m, pe, k, turned_out)


def first_loads(m, sp):
    xs = m.ins["x"].rearrange("(g p) d -> p g d", p=P)
    for k in range(2):
        half = slice(NG // 2 * k, NG // 2 * (k + 1))
        sp.dma_start(m.x[:, half, :], xs[:, half, :]).then_inc(m.x_loaded[k], 16)
    for n in range(FOLDS):
        heads, which = slice(4 * (n % 4), 4 * (n % 4) + 4), slice(n // 4 * 2, n // 4 * 2 + 2)
        sp.dma_start(m.aw[:, which, heads, :], m.ins["aw"][:, which, heads, :]).then_inc(m.aw_loaded[n], 16)
    sp.dma_start(m.mask_in[:], m.ins["mask"].rearrange("(g p) t -> p g t", p=P)).then_inc(m.mask_loaded, 16)
    for s in range(GB):
        sp.dma_start(m.cx_raw[:, s, :], m.ins["ctx_pack"][s, :, :]).then_inc(m.cx_loaded[s], 16)


def router_logits(nc, m, pe, k, turned_out):
    pe.wait_ge(turned_out, k + 1)
    for g in range(4 * k, 4 * k + 4):
        both, side = m.bank[4][:, 2 * NE * g:2 * NE * (g + 1)], m.bank[4][:, 2 * NE * g + NE:2 * NE * (g + 1)]
        nc.tensor.matmul(both, m.xT[0][:, g * P:(g + 1) * P], m.router_parts[:], start=True, stop=False)
        nc.tensor.matmul(side, m.xT[1][:, g * P:(g + 1) * P], m.router[0][:], start=False, stop=True)


RAW = 3


def load_weights(m, sp, experts):
    for e in experts:
        if e >= RAW:
            sp.wait_ge(m.raw_low, e - RAW + 1)
        gate, up, down = m.expert_sources[e]
        k = e % RAW
        sp.dma_start(m.raw[:, k, 0:HID], gate).then_inc(m.raw_loaded[k], 16)
        sp.dma_start(m.raw[:, k, HID:2 * HID], up).then_inc(m.raw_loaded[k], 16)
        sp.dma_start(m.raw[:, k, 2 * HID:].rearrange("p (k d) -> p k d", d=E),
                     down.rearrange("(k p) d -> p k d", p=P)).then_inc(m.raw_loaded[k], 16)


def weights_high(nc, m, act, e):
    act.wait_ge(m.raw_loaded[e % RAW], 48 * (e // RAW + 1))
    nc.scalar.copy(m.w_exp[0][:, e, :], m.raw[:, e % RAW, :]).then_inc(m.raw_high, 1)


def weights_low(nc, m, dve, e):
    dve.wait_ge(m.raw_high, e + 1)
    nc.vector.tensor_tensor(m.w_exp[1][:, e, :], m.raw[:, e % RAW, :], m.w_exp[0][:, e, :].bitcast(F32),
                            ALU.subtract).then_inc(m.raw_low, 1)


FOLDS = 8


def fold_parts(m, n):
    parts = (m.w_qk, m.w_vo)[n // 4]
    return m.bank[2 + n % 4], [a[:, 4 * (n % 4):4 * (n % 4) + 4, :] for a in parts]


def fold(nc, m, pe, n):
    pe.wait_ge(m.aw_loaded[n], 16)
    if n >= 4:
        pe.wait_ge(m.folded_out, n - 3)
    for j in range(4):
        h = 4 * (n % 4) + j
        last = nc.tensor.matmul(fold_parts(m, n)[0][:, j * P:(j + 1) * P], m.aw[:, n // 4 * 2, h, :],
                                m.aw[:, n // 4 * 2 + 1, h, :], start=True, stop=True)
    last.then_inc(m.folded, 1)


def fold_high(nc, m, act, n):
    act.wait_ge(m.folded, n + 1)
    bank, parts = fold_parts(m, n)
    nc.scalar.copy(parts[0], bank[:]).then_inc(m.folded_high, 1)


def fold_low(nc, m, dve, n):
    dve.wait_ge(m.folded_high, n + 1)
    bank, parts = fold_parts(m, n)
    high, low = (a.rearrange("p a n -> p (a n)") for a in parts)
    nc.vector.tensor_tensor(low, bank[:], high.bitcast(F32), ALU.subtract).then_inc(m.folded_out, 1)


def last_row_products(nc, m, pe):
    for hb in range(4):
        product3(nc, m.bank[hb][:], [a[:] for a in m.row_parts], [a[:, 4 * hb:4 * hb + 4, :] for a in m.w_vo],
                 True, True).then_inc(m.v_row, 1)


def last_row_out(nc, m, dve):
    for hb in range(4):
        dve.wait_ge(m.v_row, hb + 1)
        nc.vector.tensor_copy(m.v_rows[:, hb, :], m.bank[hb][0:B, :]).then_inc(m.v_row_out, 1)


def lambda_exp(nc, m, act):
    act.wait_ge(m.lam_step, 2)
    nc.scalar.activation(m.lam[:, 2:4], m.lam[:, 0:2], ACT.Exp).then_inc(m.lam_exp, 1)


def lambda_sums(nc, m, dve):
    nc.vector.tensor_tensor(m.lam_prod[:], m.lam_in[:, 0:2, :], m.lam_in[:, 2:4, :], ALU.mult).then_inc(m.lam_step, 1)
    dve.wait_ge(m.lam_step, 1)
    nc.vector.tensor_reduce(m.lam[:, 0:2], m.lam_prod[:], AX.X, ALU.add).then_inc(m.lam_step, 1)


def lambda_factor(nc, m, dve):
    dve.wait_ge(m.lam_exp, 1)
    nc.vector.tensor_tensor(m.lam[:, 4:5], m.lam[:, 3:4], m.lam[:, 2:3], ALU.subtract).then_inc(m.lam_step, 1)
    dve.wait_ge(m.lam_step, 3)
    nc.vector.tensor_scalar(m.pair_factor[:, 1:2], m.lam[:, 4:5], -LAMBDA_INIT, None, ALU.add).then_inc(m.lam_step, 1)
    nc.vector.tensor_scalar(m.gamma[:], m.gamma_in[:], 1.0 - LAMBDA_INIT, None, ALU.mult).then_inc(m.lam_step, 1)
    dve.wait_ge(m.lam_step, 5)
    nc.vector.tensor_scalar(m.w_out[:], m.w_out[:], m.gamma[:, 0:1], None, ALU.mult)


def fold_self(nc, m, pe):
    pe.wait_ge(m.self_loaded, 32)
    for hb in range(4):
        for j in range(4):
            h = 4 * hb + j
            last = nc.tensor.matmul(m.bank[4 + hb][:, j * P:(j + 1) * P], m.dw[:, 0, h, :], m.dw[:, 1, h, :],
                                    start=True, stop=True)
        last.then_inc(m.self_folded, 1)


def split_self_high(nc, m, act):
    act.wait_ge(m.self_loaded, 32)
    nc.scalar.copy(m.w_v[0][:], m.w_v_in[:]).then_inc(m.other_high, 1)
    nc.scalar.copy(m.router[0][:], m.router_in[:]).then_inc(m.other_high, 1)
    for hb in range(4):
        act.wait_ge(m.self_folded, hb + 1)
        nc.scalar.copy(m.w_dd[0][:, 4 * hb:4 * hb + 4, :], m.bank[4 + hb][:]).then_inc(m.self_folded_high, 1)


def split_self_low(nc, m, dve):
    for n, (parts, whole) in enumerate(((m.w_v, m.w_v_in), (m.router, m.router_in))):
        dve.wait_ge(m.other_high, n + 1)
        nc.vector.tensor_tensor(parts[1][:], whole[:], parts[0][:].bitcast(F32), ALU.subtract)
    for hb in range(4):
        dve.wait_ge(m.self_folded_high, hb + 1)
        nc.vector.tensor_tensor(m.w_dd[1][:, 4 * hb:4 * hb + 4, :].rearrange("p a n -> p (a n)"), m.bank[4 + hb][:],
                                m.w_dd[0][:, 4 * hb:4 * hb + 4, :].rearrange("p a n -> p (a n)").bitcast(F32),
                                ALU.subtract)


def cross_attention(nc, m, ctx_pack):
    with ExitStack() as ctx:
        def sb(name, shape, dt=F32):
            return ctx.enter_context(nc.sbuf_tensor(name, shape, dt))

        def sem(name):
            return ctx.enter_context(nc.semaphore(name))

        raw, cx = m.cx_raw, m.cx
        q = [sb(f"q{k}", [P, 2, GB, H, T], F32R) for k in range(2)]
        probs = sb("probs", [P, 2, NT, S2])
        probsT = [sb(f"probsT{k}", [P, 2, CH, H * T], F32R) for k in range(2)]
        mixed = [sb(f"mixed{k}", [P, H, 2 * GB, T], F32R) for k in range(2)]
        outT = sb("outT", [P, 2 * P])
        row_top = sb("row_top", [P, 2, NT])
        row_max = sb("row_max", [P, 2, NT])
        row_sum = sb("row_sum", [P, 2, NT])
        row_inv = sb("row_inv", [P, 2, NT])
        last_p = sb("last_p", [P, 2, NT, GB])
        last_pd = sb("last_pd", [NT * GB, 2, HT, GB, T])
        v_last = sb("v_last", [NT * GB, 2, HT * E])

        cx_high, cx_low, cx_loaded = m.cx_high, m.cx_low, m.cx_loaded
        v_loaded = [sem(f"v_loaded{s}") for s in range(2)]
        scores_ready = sem("scores_ready")
        max_ready = sem("max_ready")
        max_step = sem("max_step")
        exp_done = sem("exp_done")
        inv_ready = sem("inv_ready")
        probs_ready = sem("probs_ready")
        last_p_ready = sem("last_p_ready")
        probsT_ready = sem("probsT_ready")
        probsT_high = sem("probsT_high")
        probsT_out = sem("probsT_out")
        mixed_ready = sem("mixed_ready")
        mixed_high = sem("mixed_high")
        mixed_out = sem("mixed_out")
        q_ready = sem("q_ready")
        q_high = sem("q_high")
        q_out = sem("q_out")
        last_t_ready = sem("last_t_ready")
        last_pd_ready = sem("last_pd_ready")
        out_ready = sem("out_ready")
        outT_ready = sem("outT_ready")
        out_turned = sem("out_turned")
        out_added = sem("out_added")

        scores = m.scores
        pt_bank = m.bank[4:6]
        mixed_bank = m.bank[6]
        q_bank = m.bank[7]

        UN = 8
        LOOPS = (B - UN) // UN
        TAIL = range(B - UN + 1, B)

        block = ctx.enter_context(nc.Block())

        @block.sync
        def _(sp):
            def load_context(n, slot):
                sp.dma_start(raw[:, slot, :], ctx_pack[n, :, :]).then_inc(cx_loaded[slot], 16)

            def load_last(g, slot):
                for a in range(NT):
                    sp.dma_start(v_last[GB * a:GB * (a + 1), slot, :],
                                 m.v_scratch[bass.ds(g * GB, GB), HT * E * a:HT * E * (a + 1)]).then_inc(v_loaded[slot], 16)

            sp.wait_ge(m.v_row_out, 4)
            sp.dma_start(m.v_scratch[:, :], m.v_rows.rearrange("b a n -> b (a n)")).then_inc(m.v_stored, 16)
            sp.wait_ge(m.v_stored, 16)
            load_last(0, 0)
            load_last(1, 1)

            def load_group(g):
                for s in range(GB):
                    sp.wait_ge(cx_low, g * GB + (s - GB + 1))
                    load_context(g * GB + s, s)

            load_group(1)
            with sp.Fori(1, NG // 2) as k:
                for s in range(2):
                    load_group(k * 2 + s)
                sp.wait_ge(out_ready, k)
                for s in range(2):
                    load_last(k * 2 + s, s)

        @block.tensor
        def _(pe):
            def score_tiles(n, par, slot, group, ended_group=None, ended_pair=None):
                pe.wait_ge(cx_low, n + 1)
                if slot == 0:
                    pe.wait_ge(q_out, group * 4 + 4)
                for pair in range(2):
                    if pair and ended_group is not None:
                        last_transpose(ended_group, 1 - par)
                    if pair and ended_pair is not None:
                        pe.wait_ge(mixed_out, n - 2)
                        turn_back(ended_pair)
                    if not early(n, 1):
                        pe.wait_ge(exp_done, n * NT - NT + 2 * pair + 2)
                    for g in (2 * pair, 2 * pair + 1):
                        product3(nc, scores[:, g, 0:S2 + 1], [a[:, par, slot, HT * g:HT * (g + 1), :] for a in q],
                                 [a[:, slot, CH * P:PACK] for a in cx], True, False)
                        last = nc.tensor.matmul(scores[:, g, 0:S2], m.spread[:, slot, :],
                                                m.mask_add[:, group, :], start=False, stop=True)
                    last.then_inc(scores_ready, 1)

            def queries(group, hb, bank=q_bank):
                for j in range(4):
                    last = product3(nc, bank[:, j * P:(j + 1) * P], [a[:, 4 * hb + j, :] for a in m.w_qk],
                                    [a[:, bass.ts(group, P)] for a in m.xT], True, True)
                last.then_inc(q_ready, 1)

            def transposes(n, par):
                pe.wait_ge(probs_ready, n + 1)
                for c in range(CH):
                    if not early(n, 1):
                        pe.wait_ge(probsT_out, n * 2 + (c - 1))
                    for g in range(NT):
                        last = nc.tensor.transpose(pt_bank[c][:, g * P:(g + 1) * P], probs[:, par, g, c * P:(c + 1) * P],
                                                   m.ident)
                    last.then_inc(probsT_ready, 1)

            def product(n, par, slot):
                pe.wait_ge(probsT_out, n * 2 + 2)
                if not early(n, 1):
                    pe.wait_ge(mixed_out, n)
                for c in range(CH):
                    last = product3(nc, mixed_bank[:], [a[:, slot, c * P:(c + 1) * P] for a in cx],
                                    [a[:, par, c, :] for a in probsT], c == 0, c == CH - 1)
                last.then_inc(mixed_ready, 1)

            def last_transpose(group, par):
                pe.wait_ge(last_p_ready, group * GB + GB)
                pe.wait_ge(mixed_out, group * GB + GB - 1)
                nc.tensor.transpose(mixed_bank[0:NT * GB, 0:P], last_p[:, par, :, :], m.ident).then_inc(last_t_ready, 1)

            def output(pair):
                pe.wait_ge(mixed_out, pair * (2 * GB) + 2 * GB)
                pe.wait_ge(last_pd_ready, pair * 2 + 2)
                for par in range(2):
                    pe.wait_ge(v_loaded[par], pair * 64 + 64)
                for h in range(H):
                    last = product3(nc, mixed_bank[:, 0:2 * P], [a[:, h, :] for a in m.w_vo], [a[:, h, :, :] for a in mixed],
                                    h == 0, h == H - 1)
                    if h % 2 == 0:
                        par, j = h // 2 // HT, h // 2 % HT
                        nc.tensor.matmul(mixed_bank[:, par * P:(par + 1) * P], v_last[:, par, j * E:(j + 1) * E],
                                         last_pd[:, par, j, :, :], start=False, stop=False)
                last.then_inc(out_ready, 1)

            def turn_back(pair):
                pe.wait_ge(outT_ready, pair + 1)
                for par in range(2):
                    last = nc.tensor.transpose(mixed_bank[:, par * P:(par + 1) * P], outT[:, par * P:(par + 1) * P], m.ident)
                last.then_inc(out_turned, 1)

            def step(n, u, group, pair, tail):
                s = (1 + u) % UN
                if not tail or n + 1 < B:
                    nslot = (s + 1) % GB
                    score_tiles(n + 1, (s + 1) // GB % 2, nslot, group + (1 if nslot == 0 else 0),
                                group - 1 if s % GB == 0 else None,
                                pair - 1 if s == 2 and not early(pair, 1) else None)
                j = s % GB
                made = group * 4 + (5 + j)
                more = not tail or made < 4 * NG
                if s == 1 and not early(pair, 1):
                    output(pair - 1)
                if more:
                    pe.wait_ge(q_out, made)
                    queries(group + (2 if j == 3 else 1), (j + 1) % 4)
                if j == 0:
                    pe.wait_ge(last_pd_ready, group)
                if s == 1 and not early(pair, 1):
                    pe.wait_ge(outT_ready, pair)
                if s == 2 and not early(pair, 1):
                    pe.wait_ge(out_added, pair)
                product(n - 1, (s - 1) % 2, (s - 1) % GB)
                transposes(n, s % 2)

            last_row_products(nc, m, pe)
            for hb in range(4):
                queries(0, hb, m.bank[4 + hb])
            pe.wait_ge(m.v_row_out, 4)
            score_tiles(0, 0, 0, 0)
            score_tiles(1, 0, 1, 0)
            for hb in range(2):
                pe.wait_ge(q_out, 4 + hb)
                queries(1, hb)
            transposes(0, 0)
            for n in range(1, UN + 1):
                step(n, n - 1, n // GB, n // UN, False)
            with pe.Fori(1, LOOPS) as i:
                for u in range(UN):
                    step(i * UN + (1 + u), u, i * (UN // GB) + (1 + u) // GB, i + (1 + u) // UN, False)
            for n in TAIL:
                step(n, (n - 1) % UN, n // GB, n // UN, True)
            product(B - 1, 1, GB - 1)
            pe.wait_ge(mixed_out, B)
            last_transpose(NG - 1, 1)
            output(B // UN - 1)
            turn_back(B // UN - 1)

        @block.scalar
        def _(act):
            def context_high(n, slot, group):
                act.wait_ge(cx_loaded[slot], group * 16 + 16)
                if not early(n, GB):
                    act.wait_ge(mixed_ready, n - (GB - 1))
                nc.scalar.copy(cx[0][:, slot, :], raw[:, slot, :]).then_inc(cx_high, 1)

            def queries_high(gpar, hb, count, bank=q_bank):
                act.wait_ge(q_ready, count)
                nc.scalar.copy(q[0][:, gpar, :, 4 * hb:4 * hb + 4, :].rearrange("p b h t -> p h b t"),
                               bank[:].rearrange("p (h b t) -> p h b t", h=4, b=GB)).then_inc(q_high, 1)

            def exponentials(n, par, pairs=(0, 1)):
                if not early(n, 2) and 0 in pairs:
                    act.wait_ge(probsT_ready, (n - 1) * 2)
                    act.wait_ge(last_p_ready, n - 1)
                for g in range(2 * pairs[0], 2 * pairs[-1] + 2):
                    if g % 2 == 0:
                        act.wait_ge(max_ready, n * 2 + (g // 2 + 1))
                    nc.scalar.activation(probs[:, par, g, :], scores[:, g, 0:S2], ACT.Exp, bias=row_max[:, par, g:g + 1],
                                         scale=XSCALE, accum_out=row_sum[:, par, g:g + 1]).then_inc(exp_done, 1)

            def chunks_high(n, par):
                for c in range(CH):
                    act.wait_ge(probsT_ready, n * 2 + (1 + c))
                    if not early(n, 2):
                        act.wait_ge(mixed_ready, n - 1)
                    nc.scalar.copy(probsT[0][:, par, c, :], pt_bank[c][:]).then_inc(probsT_high, 1)

            def product_high(n, slot):
                act.wait_ge(mixed_ready, n + 1)
                nc.scalar.copy(mixed[0][:, :, slot, :], mixed_bank[:].rearrange("p (h t) -> p h t", h=H)).then_inc(mixed_high, 1)

            def step(n, u, group, pair, tail):
                s = (1 + u) % UN
                j = s % GB
                made = group * 4 + (5 + j)
                more = not tail or made < 4 * NG

                def next_queries():
                    queries_high((s // GB + (2 if j == 3 else 1)) % 2, (j + 1) % 4, made + 1)

                if s == 1 and not early(pair, 1):
                    exponentials(n + 1, (s + 1) % 2)
                    outT_copy(pair - 1)
                    if more:
                        next_queries()
                else:
                    if not tail or n + 1 < B:
                        exponentials(n + 1, (s + 1) % 2, (0,))
                    if more:
                        next_queries()
                    if not tail or n + 1 < B:
                        exponentials(n + 1, (s + 1) % 2, (1,))
                product_high(n - 1, (s - 1) % UN)
                chunks_high(n, s % 2)
                if not tail or n + 3 < B:
                    context_high(n + 3, (s + 3) % GB, group + (1 if j else 0))

            def outT_copy(pair):
                act.wait_ge(out_ready, pair + 1)
                if not early(pair, 1):
                    act.wait_ge(out_turned, pair)
                nc.scalar.copy(outT[:], mixed_bank[:, 0:2 * P]).then_inc(outT_ready, 1)

            lambda_exp(nc, m, act)
            for hb in range(4):
                queries_high(0, hb, hb + 1, m.bank[4 + hb])
            exponentials(0, 0)
            exponentials(1, 1)
            queries_high(1, 0, 5)
            queries_high(1, 1, 6)
            chunks_high(0, 0)
            context_high(3, 3, 0)
            for n in range(1, UN + 1):
                step(n, n - 1, n // GB, n // UN, False)
            with act.Fori(1, LOOPS) as i:
                for u in range(UN):
                    step(i * UN + (1 + u), u, i * (UN // GB) + (1 + u) // GB, i + (1 + u) // UN, False)
            for n in TAIL:
                step(n, (n - 1) % UN, n // GB, n // UN, True)
            product_high(B - 1, UN - 1)
            outT_copy(B // UN - 1)

        @block.vector
        def _(dve):
            def maxima(n, par, pair):
                tiles = slice(2 * pair, 2 * pair + 2)
                dve.wait_ge(scores_ready, n * 2 + (pair + 1))
                nc.vector.tensor_reduce(row_top[:, par, tiles], scores[:, tiles, 0:S2], AX.X, ALU.max).then_inc(max_step, 1)
                dve.wait_ge(max_step, n * 2 + (pair + 1))
                nc.vector.tensor_scalar(row_max[:, par, tiles], row_top[:, par, tiles], -XSCALE, None, ALU.mult).then_inc(max_ready, 1)

            def inverses(n, par):
                dve.wait_ge(exp_done, n * NT + NT)
                nc.vector.reciprocal(row_inv[:, par, :], row_sum[:, par, :]).then_inc(inv_ready, 1)

            def chunk_low(n, par, c):
                dve.wait_ge(probsT_high, n * 2 + (1 + c))
                if not early(n, 2):
                    dve.wait_ge(mixed_ready, n - 1)
                nc.vector.tensor_tensor(probsT[1][:, par, c, :], pt_bank[c][:], probsT[0][:, par, c, :].bitcast(F32),
                                        ALU.subtract).then_inc(probsT_out, 1)

            def product_low(n, slot):
                dve.wait_ge(mixed_high, n + 1)
                nc.vector.tensor_tensor(mixed[1][:, :, slot, :], mixed_bank[:].rearrange("p (h t) -> p h t", h=H),
                                        mixed[0][:, :, slot, :].bitcast(F32), ALU.subtract).then_inc(mixed_out, 1)

            def queries_low(gpar, hb, count, bank=q_bank):
                dve.wait_ge(q_high, count)
                nc.vector.tensor_tensor(q[1][:, gpar, :, 4 * hb:4 * hb + 4, :].rearrange("p b h t -> p h b t"),
                                        bank[:].rearrange("p (h b t) -> p h b t", h=4, b=GB),
                                        q[0][:, gpar, :, 4 * hb:4 * hb + 4, :].rearrange("p b h t -> p h b t").bitcast(F32),
                                        ALU.subtract).then_inc(q_out, 1)

            def spread_last(group, par, pair):
                dve.wait_ge(last_t_ready, group + 1)
                if not early(pair, 1 + par):
                    dve.wait_ge(out_ready, pair - par)
                nc.vector.tensor_tensor(last_pd[:, par],
                                        mixed_bank[0:NT * GB, 0:P].rearrange("p (h t) -> p h t", h=HT).unsqueeze(2).to_broadcast([NT * GB, HT, GB, T]),
                                        m.own_entry[:].unsqueeze(1).unsqueeze(3).to_broadcast([NT * GB, HT, GB, T]),
                                        ALU.mult).then_inc(last_pd_ready, 1)

            def add_output(pair):
                dve.wait_ge(out_turned, pair + 1)
                both = m.x[:, bass.ds(pair * 2, 2), :]
                nc.vector.tensor_tensor(both, both, mixed_bank[:, 0:2 * P].rearrange("p (g e) -> p g e", g=2),
                                        ALU.add).then_inc(out_added, 1)

            def step(n, u, group, pair, tail):
                s = (1 + u) % UN
                j = s % GB
                for c in range(CH):
                    chunk_low(n - 1, (s - 1) % 2, c)
                    if not tail or n + 1 < B:
                        maxima(n + 1, (s + 1) % 2, c)
                    if c == 0 and j == 0:
                        spread_last(group - 1, 1 - s // GB, pair)
                    if c == 0 and s == 2 and not early(pair, 1):
                        add_output(pair - 1)
                made = group * 4 + (5 + j)
                more = not tail or made < 4 * NG
                late = s == 1 and not early(pair, 1)
                if more and not late:
                    queries_low((s // GB + (2 if j == 3 else 1)) % 2, (j + 1) % 4, made + 1)
                if not tail or n + 1 < B:
                    inverses(n + 1, (s + 1) % 2)
                if more and late:
                    queries_low((s // GB + (2 if j == 3 else 1)) % 2, (j + 1) % 4, made + 1)
                product_low(n - 1, (s - 1) % UN)

            lambda_sums(nc, m, dve)
            last_row_out(nc, m, dve)
            for hb in range(4):
                queries_low(0, hb, hb + 1, m.bank[4 + hb])
            lambda_factor(nc, m, dve)
            for n in range(2):
                for pair in range(2):
                    maxima(n, n, pair)
                inverses(n, n)
            queries_low(1, 0, 5)
            queries_low(1, 1, 6)
            for n in range(1, UN + 1):
                step(n, n - 1, n // GB, n // UN, False)
            with dve.Fori(1, LOOPS) as i:
                for u in range(UN):
                    step(i * UN + (1 + u), u, i * (UN // GB) + (1 + u) // GB, i + (1 + u) // UN, False)
            for n in TAIL:
                step(n, (n - 1) % UN, n // GB, n // UN, True)
            for c in range(CH):
                chunk_low(B - 1, 1, c)
            product_low(B - 1, UN - 1)
            spread_last(NG - 1, 1, B // UN)
            add_output(B // UN - 1)

        @block.gpsimd
        def _(pool):
            def normalise(n, par, group, gpar, slot):
                pool.wait_ge(inv_ready, n + 1)
                if not early(n, 2 * GB):
                    pool.wait_ge(last_t_ready, group - 1)
                pool.tensor_tensor(last_p[:, gpar, :, slot], probs[:, par, :, S2 - 1], row_inv[:, par, :],
                                   ALU.mult).then_inc(last_p_ready, 1)
                pool.tensor_tensor(probs[:, par, :, 0:S2 - 1], probs[:, par, :, 0:S2 - 1],
                                   row_inv[:, par, :].unsqueeze(2).to_broadcast([P, NT, S2 - 1]), ALU.mult).then_inc(probs_ready, 1)

            def context_low(n, slot):
                pool.wait_ge(cx_high, n + 1)
                pool.tensor_tensor(cx[1][:, slot, :], raw[:, slot, :], cx[0][:, slot, :].bitcast(F32),
                                   ALU.subtract).then_inc(cx_low, 1)

            for n in range(3):
                context_low(n, n)
            for n in range(UN):
                normalise(n, n % 2, n // GB, n // GB, n % GB)
                if n:
                    context_low(n + 2, (n + 2) % GB)
            with pool.Fori(1, B // UN - 1) as i:
                for u in range(UN):
                    normalise(i * UN + u, u % 2, i * (UN // GB) + u // GB, u // GB, u % GB)
                    context_low(i * UN + (u + 2), (u + 2) % GB)
            for n in range(B - UN, B):
                normalise(n, n % 2, n // GB, n // GB % 2, n % GB)
                if n + 2 < B:
                    context_low(n + 2, (n + 2) % GB)


def differential_attention(nc, m):
    with ExitStack() as ctx:
        def sb(name, shape, dt=F32):
            return ctx.enter_context(nc.sbuf_tensor(name, shape, dt))

        def sem(name):
            return ctx.enter_context(nc.semaphore(name))

        xg = [sb(f"d_xg{k}", [P, 2, P], F32R) for k in range(2)]
        xw = sb("d_xw", [P, 2, P])
        q = sb("d_q", [P, 2, 2, GB, NC, T])
        v = sb("d_v", [P, 2, DE])
        e = sb("d_e", [P, 2, GB * 4, T])
        diff = sb("d_diff", [P, 2, 2, GB, T])
        wT = sb("d_wT", [P, 2, DH, GB, T])
        sq = sb("d_sq", [P, 2, DE])
        empty = sb("d_empty", [P, NTILE, SE])
        unused = sb("d_unused", [P, 2])
        mx = sb("d_mx", [P, 2, GB * 4])
        sm = sb("d_sm", [P, 2, GB * 4])
        rc = sb("d_rc", [P, 2, GB * 4])
        rf = sb("d_rf", [P, 2, GB * 4])

        xg_ready = sem("d_xg_ready")
        q_ready = sem("d_q_ready")
        q_out = sem("d_q_out")
        v_ready = sem("d_v_ready")
        v_out = sem("d_v_out")
        scores_ready = sem("d_scores_ready")
        max_ready = sem("d_max_ready")
        shifted = sem("d_shifted")
        exp_done = sem("d_exp_done")
        summed = sem("d_summed")
        scaled = sem("d_scaled")
        diff_ready = sem("d_diff_ready")
        diffT_ready = sem("d_diffT_ready")
        wT_zero = sem("d_wT_zero")
        wT_out = sem("d_wT_out")
        att_ready = sem("d_att_ready")
        att_out = sem("d_att_out")
        squares_summed = sem("d_squares_summed")

        qb = [m.bank[4], m.bank[5]]
        FIRST, LAST = 4, NG - 4
        tb = m.bank[6]
        vb = ab = m.bank[7]
        block = ctx.enter_context(nc.Block())

        @block.gpsimd
        def _(pool):
            for k in range(2):
                pool.memset(wT[:, k], 0.0).then_inc(wT_zero, 1)

            def stage(g, par):
                for a in range(2):
                    pool.tensor_copy(xg[a][:, par, :], m.xT[a][:, bass.ts(g, P)].bitcast(F32))
                pool.tensor_tensor(xw[:, par, :], m.xT[0][:, bass.ts(g, P)].bitcast(F32),
                                   m.xT[1][:, bass.ts(g, P)].bitcast(F32), ALU.add).then_inc(xg_ready, 1)

            def difference(g, par):
                pool.wait_ge(summed, g * 3 + 3)
                pool.tensor_tensor(e[:, par], e[:, par], rf[:, par].unsqueeze(2).to_broadcast([P, GB * 4, T]),
                                   ALU.mult).then_inc(scaled, 1)
                pool.wait_ge(scaled, g + 1)
                if not early(g, 2):
                    pool.wait_ge(diffT_ready, g - 1)
                ev = e[:, par].rearrange("p (b c u) k -> p c u b k", b=GB, c=2)
                pool.tensor_tensor(diff[:, par], ev[:, 0], ev[:, 1], ALU.add).then_inc(diff_ready, 1)

            def step(g, s):
                if not early(g, 1):
                    pool.wait_ge(v_ready, g)
                if not isinstance(g, int) or g + 1 < NG:
                    stage(g + 1, (s + 1) % 2)
                difference(g, s % 2)

            stage(0, 0)
            for g in range(2):
                step(g, g)
            pool.memset(empty[:], 0.0).then_inc(m.zeros_ready, 1)
            pool.wait_ge(m.zeros_ready, 1)
            pool.tensor_copy(empty[:, :, E], m.empty_rows).then_inc(m.zeros_ready, 1)
            pool.wait_ge(m.zeros_ready, 2)
            pool.dma_start(m.slot_rows.rearrange("(j p) d -> p j d", p=P), empty[:]).then_inc(m.slots_zeroed, 16)
            for g in range(2, FIRST):
                step(g, g)
            with pool.Fori(FIRST // 4, LAST // 4) as i:
                for s in range(4):
                    step(i * 4 + s, s)
            for g in range(LAST, NG):
                step(g, g - LAST)
            pool.wait_ge(m.slots_zeroed, 16)

        @block.tensor
        def _(pe):
            def queries(pair, half, k):
                for j in range(2):
                    last = product3(nc, qb[k % 2][:, j * 2 * P:(j + 1) * 2 * P], [a[:, 8 * half + 2 * k + j, :] for a in m.w_dd],
                                    [a[:, bass.ts(pair, 2 * P)] for a in m.xT], True, True)
                last.then_inc(q_ready, 1)

            def values(g, par):
                if not early(g, 2):
                    pe.wait_ge(att_out, g - 1)
                pe.wait_ge(xg_ready, g + 1)
                product3(nc, vb[:], [a[:, par, :] for a in xg], [a[:] for a in m.w_v], True, True).then_inc(v_ready, 1)

            def scores(g, s):
                pe.wait_ge(xg_ready, g + 1)
                if not early(g, 1):
                    pe.wait_ge(shifted, g)
                if s % 2 == 0:
                    pe.wait_ge(q_out, g * 4 + 8)
                for b in range(GB):
                    for cu in range(4):
                        last = nc.tensor.matmul(m.bank[b][:, cu * P:(cu + 1) * P], q[:, s // 2, s % 2, b, 4 * cu:4 * cu + 4, :],
                                                xw[:, s % 2, :], start=True, stop=True)
                last.then_inc(scores_ready, 1)

            def back(g, par):
                pe.wait_ge(diff_ready, g + 1)
                if not early(g, 1):
                    pe.wait_ge(wT_out, g)
                for u in range(2):
                    last = nc.tensor.transpose(tb[:, u * P:(u + 1) * P], diff[:, par, u].rearrange("p b k -> p (b k)"), m.ident)
                last.then_inc(diffT_ready, 1)

            def products(g, par):
                pe.wait_ge(wT_out, g + 1)
                pe.wait_ge(v_out, g + 2 if not isinstance(g, int) or g + 1 < NG else g + 1)
                if isinstance(g, int) and g == NG - 1:
                    pe.wait_ge(att_out, g)
                for h in range(DH):
                    last = nc.tensor.matmul(ab[:, 2 * DD * h:2 * DD * (h + 1)], wT[:, par, h], v[:, par, 2 * DD * h:2 * DD * (h + 1)],
                                            start=True, stop=True)
                last.then_inc(att_ready, 1)

            def step(g, s, pair):
                more = not isinstance(g, int) or g < NG - 2
                for k in range(4):
                    if more:
                        pe.wait_ge(q_out, g * 4 + (7 + k))
                        queries(pair, s % 2, k)
                    if k == 0 and not early(g, 1):
                        back(g - 1, (s - 1) % 2)
                    if k == 1:
                        values(g, s % 2)
                if not early(g, 1):
                    products(g - 1, (s - 1) % 2)
                if not isinstance(g, int) or g + 1 < NG:
                    scores(g + 1, (s + 1) % 4)

            for half in range(2):
                for k in range(4):
                    if half or k >= 2:
                        pe.wait_ge(q_out, 4 * half + k - 1)
                    queries(0, half, k)
            scores(0, 0)
            for g in range(FIRST):
                step(g, g, g // 2 + 1)
            with pe.Fori(FIRST // 4, LAST // 4) as i:
                for s in range(4):
                    step(i * 4 + s, s, i * 2 + (s // 2 + 1))
            for g in range(LAST, NG):
                step(g, g - LAST, g // 2 + 1)
            back(NG - 1, 1)
            products(NG - 1, 1)

        @block.scalar
        def _(act):
            def queries_out(n, pair_par, half, k):
                act.wait_ge(q_ready, n + 1)
                nc.scalar.copy(q[:, pair_par, :, :, 8 * half + 2 * k:8 * half + 2 * k + 2, :].rearrange("p g b h t -> p h (g b) t"),
                               qb[k % 2][:].rearrange("p (h a t) -> p h a t", h=2, t=T)).then_inc(q_out, 1)

            def values_out(g, par):
                act.wait_ge(v_ready, g + 1)
                if not early(g, 2):
                    act.wait_ge(att_ready, g - 1)
                nc.scalar.copy(v[:, par, :], vb[:]).then_inc(v_out, 1)

            def exponentials(g, par):
                act.wait_ge(shifted, g + 1)
                nc.scalar.activation(e[:, par], e[:, par], ACT.Exp, scale=DD ** -0.5).then_inc(exp_done, 1)

            def result_out(g, par):
                act.wait_ge(att_ready, g + 1)
                nc.scalar.copy(m.att[:, g, :], ab[:])
                if not early(g, 2):
                    act.wait_ge(squares_summed, g - 1)
                nc.scalar.activation(sq[:, par, :], ab[:], ACT.Square).then_inc(att_out, 1)

            def step(g, s):
                for k in range(4):
                    if not isinstance(g, int) or g < NG - 2:
                        if k == 0 and not early(g, 1):
                            act.wait_ge(scores_ready, g)
                        queries_out(g * 4 + (8 + k), (s // 2 + 1) % 2, s % 2, k)
                    if k == 0:
                        exponentials(g, s % 2)
                    if k == 1:
                        values_out(g, s % 2)
                if not early(g, 1):
                    result_out(g - 1, (s - 1) % 2)

            nc.scalar.activation(unused[:], m.pair_factor[:], ACT.Exp)
            for half in range(2):
                for k in range(4):
                    queries_out(4 * half + k, 0, half, k)
            for g in range(FIRST):
                step(g, g)
            with act.Fori(FIRST // 4, LAST // 4) as i:
                for s in range(4):
                    step(i * 4 + s, s)
            for g in range(LAST, NG):
                step(g, g - LAST)
            result_out(NG - 1, 1)

        @block.vector
        def _(dve):
            dve.wait_ge(wT_zero, 2)
            own = m.own_scores

            def softmax_front(g, par):
                dve.wait_ge(scores_ready, g + 1)
                if not early(g, 2):
                    dve.wait_ge(diff_ready, g - 1)
                nc.vector.tensor_reduce(mx[:, par].rearrange("p (b c) -> p b c", b=GB), own, AX.X, ALU.max).then_inc(max_ready, 1)
                dve.wait_ge(max_ready, g + 1)
                nc.vector.tensor_tensor(e[:, par].rearrange("p (b c) k -> p b c k", b=GB), own,
                                        mx[:, par].rearrange("p (b c) -> p b c", b=GB).unsqueeze(3).to_broadcast([P, GB, 4, T]),
                                        ALU.subtract).then_inc(shifted, 1)

            def softmax_back(g, par):
                dve.wait_ge(exp_done, g + 1)
                nc.vector.tensor_reduce(sm[:, par], e[:, par], AX.X, ALU.add).then_inc(summed, 1)
                dve.wait_ge(summed, g * 3 + 1)
                nc.vector.reciprocal(rc[:, par], sm[:, par]).then_inc(summed, 1)
                dve.wait_ge(summed, g * 3 + 2)
                nc.vector.tensor_tensor(rf[:, par].rearrange("p (b c u) -> p b c u", b=GB, c=2),
                                        rc[:, par].rearrange("p (b c u) -> p b c u", b=GB, c=2),
                                        m.pair_factor[:].unsqueeze(1).unsqueeze(3).to_broadcast([P, GB, 2, 2]),
                                        ALU.mult).then_inc(summed, 1)

            def blocks_out(g, par):
                dve.wait_ge(diffT_ready, g + 1)
                if not early(g, 2):
                    dve.wait_ge(att_ready, g - 1)
                for b in range(GB):
                    rows = slice(T * b, T * (b + 1))
                    last = nc.vector.tensor_copy(wT[rows, par, :, b, :], tb[rows, 0:2 * P].rearrange("p (h t) -> p h t", h=DH))
                last.then_inc(wT_out, 1)

            def sum_squares(g, par):
                dve.wait_ge(att_out, g + 1)
                nc.vector.tensor_reduce(m.att_squares[:, bass.ts(g, DH)], sq[:, par, :].rearrange("p (h w) -> p h w", w=2 * DD),
                                        AX.X, ALU.add).then_inc(squares_summed, 1)

            def step(g, s):
                softmax_front(g, s % 2)
                if not early(g, 2):
                    sum_squares(g - 2, s % 2)
                if not early(g, 1):
                    blocks_out(g - 1, (s - 1) % 2)
                softmax_back(g, s % 2)

            for g in range(FIRST):
                step(g, g)
            with dve.Fori(FIRST // 4, LAST // 4) as i:
                for s in range(4):
                    step(i * 4 + s, s)
            for g in range(LAST, NG):
                step(g, g - LAST)
            blocks_out(NG - 1, 1)
            sum_squares(NG - 2, 0)
            sum_squares(NG - 1, 1)


def attention_output(nc, m):
    W = 2 * DD
    AHEAD = 2
    with ExitStack() as ctx:
        def sem(name):
            return ctx.enter_context(nc.semaphore(name))

        an = ctx.enter_context(nc.sbuf_tensor("o_an", [P, 2, DE], F32))
        anT = ctx.enter_context(nc.sbuf_tensor("o_anT", [P, 2, DE], F32))
        ss = ctx.enter_context(nc.sbuf_tensor("o_ss", [P, 4, NG * DH], F32))
        summed = sem("o_summed")
        root = sem("o_root")
        inv = sem("o_inv")
        an_ready = sem("o_an_ready")
        anT_ready = sem("o_anT_ready")
        anT_out = sem("o_anT_out")
        out_ready = sem("o_out_ready")
        added = sem("o_added")
        moments_ready = sem("o_moments_ready")
        tb = m.bank[0:2]
        ob = m.bank[2:4]
        block = ctx.enter_context(nc.Block())

        @block.scalar
        def _(act):
            act.wait_ge(summed, 1)
            nc.scalar.activation(ss[:, 2], ss[:, 1], ACT.Sqrt).then_inc(root, 1)

            def turned_out(g, par):
                act.wait_ge(anT_ready, g + 1)
                if not early(g, 2):
                    act.wait_ge(out_ready, g - 1)
                nc.scalar.copy(anT[:, par, :], tb[par][:]).then_inc(anT_out, 1)

            for e in range(AHEAD):
                weights_high(nc, m, act, e)
            for g in range(NG):
                turned_out(g, g % 2)
                if g % 2 and g // 2 + AHEAD < NE:
                    weights_high(nc, m, act, g // 2 + AHEAD)

        @block.sync
        def _(sp):
            load_weights(m, sp, range(RAW, NE))

        @block.vector
        def _(dve):
            nc.vector.tensor_scalar(ss[:, 1], m.att_squares[:], 1.0 / W, None, ALU.mult).then_inc(summed, 1)
            dve.wait_ge(root, 1)
            nc.vector.tensor_scalar(ss[:, 3], ss[:, 2], RMS_EPS, None, ALU.add).then_inc(inv, 1)
            dve.wait_ge(inv, 1)
            nc.vector.reciprocal(ss[:, 0], ss[:, 3]).then_inc(inv, 1)

            def add(g, par):
                dve.wait_ge(out_ready, g + 1)
                nc.vector.tensor_tensor(m.x[:, g, :], m.x[:, g, :], ob[par][:, 0:E], ALU.add).then_inc(added, 1)

            def moments(g):
                dve.wait_ge(added, g + 1)
                nc.vector.bn_stats(m.moments[:, g, :], m.x[:, g, :]).then_inc(moments_ready, 1)

            def mean_and_variance(g):
                dve.wait_ge(moments_ready, g + 1)
                nc.vector.bn_aggr(m.mean_var[:, g, :], m.moments[:, g, :])

            for e in range(AHEAD):
                weights_low(nc, m, dve, e)
            for g in range(NG):
                add(g, g % 2)
                if g >= 1:
                    moments(g - 1)
                if g >= 2:
                    mean_and_variance(g - 2)
                if g % 2 and g // 2 + AHEAD < NE:
                    weights_low(nc, m, dve, g // 2 + AHEAD)
            moments(NG - 1)
            mean_and_variance(NG - 2)
            mean_and_variance(NG - 1)

        @block.gpsimd
        def _(pool):
            pool.wait_ge(inv, 2)

            def normalise(g, par):
                if not early(g, 2):
                    pool.wait_ge(anT_ready, g - 1)
                pool.tensor_tensor(an[:, par, :].rearrange("p (h w) -> p h w", w=W),
                                   m.att[:, g, :].rearrange("p (h w) -> p h w", w=W),
                                   ss[:, 0, bass.ts(g, DH)].unsqueeze(2).to_broadcast([P, DH, W]), ALU.mult).then_inc(an_ready, 1)

            normalise(0, 0)
            normalise(1, 1)
            with pool.Fori(1, NG // 2) as k:
                for par in range(2):
                    normalise(k * 2 + par, par)

        @block.tensor
        def _(pe):
            def turn(g, par):
                pe.wait_ge(an_ready, g + 1)
                if not early(g, 2):
                    pe.wait_ge(anT_out, g - 1)
                for j in range(4):
                    last = nc.tensor.transpose(tb[par][:, j * P:(j + 1) * P], an[:, par, j * P:(j + 1) * P], m.ident)
                last.then_inc(anT_ready, 1)

            def out(g, par):
                pe.wait_ge(anT_out, g + 1)
                if not early(g, 2):
                    pe.wait_ge(added, g - 1)
                for j in range(4):
                    last = nc.tensor.matmul(ob[par][:, 0:E], anT[:, par, j * P:(j + 1) * P], m.w_out[:, j, :],
                                            start=(j == 0), stop=(j == 3))
                last.then_inc(out_ready, 1)

            turn(0, 0)
            turn(1, 1)
            out(0, 0)
            with pe.Fori(1, NG // 2) as k:
                for par in range(2):
                    g = k * 2 + par
                    turn(g, par)
                    out(g - 1, 1 - par)
            out(NG - 1, 1)


def route(nc, m):
    with ExitStack() as ctx:
        def sb(name, shape, dt=F32):
            return ctx.enter_context(nc.sbuf_tensor(name, shape, dt))

        lg = sb("r_lg", [P, NG, NR])
        oh = sb("r_oh", [P, 2, NG, NR])
        tmp = sb("r_tmp", [P, 2, NG, NR])
        top = sb("r_top", [P, 8, NG])
        chosen = sb("r_chosen", [P, NG + 1, NR], BF16)
        counting = sb("r_counting", [P, 2 * P], BF16)
        place = sb("r_place", [P, NG, NR])
        full = sb("r_full", [P, NR, NG])
        tiles = sb("r_tiles", [P, NR])
        ends = sb("r_ends", [P, NR])
        starts = sb("r_starts", [P, NR])
        passed = sb("r_passed", [P, NTILE, NR])
        slot_f = sb("r_slot_f", [P, 2, NG])
        owner = sb("r_owner", [P, 2, NTILE])
        counting_ready = ctx.enter_context(nc.semaphore("r_counting_ready"))
        chosen_zero = ctx.enter_context(nc.semaphore("r_chosen_zero"))
        chosen_ready = ctx.enter_context(nc.semaphore("r_chosen_ready"))
        rank_ready = ctx.enter_context(nc.semaphore("r_rank_ready"))
        chain = ctx.enter_context(nc.semaphore("r_chain"))
        gap_ready = ctx.enter_context(nc.semaphore("r_gap_ready"))
        exp_ready = ctx.enter_context(nc.semaphore("r_exp_ready"))
        block = ctx.enter_context(nc.Block())

        @block.tensor
        def _(pe):
            pe.wait_ge(counting_ready, 1)
            pe.wait_ge(chosen_ready, 1)
            rank = m.bank[5][:, 0:(NG + 1) * NR].rearrange("p (g e) -> p g e", e=NR)
            nc.tensor.matmul(rank, counting[:, 0:P], chosen[:], start=True, stop=False)
            for g in range(NG):
                last = nc.tensor.matmul(rank[:, g + 1:NG + 1, :], counting[:, P:2 * P],
                                        chosen[:, g:g + 1, :].to_broadcast([P, NG - g, NR]),
                                        start=False, stop=(g == NG - 1))
            last.then_inc(rank_ready, 1)

        @block.scalar
        def _(act):
            nc.scalar.copy(counting[:], m.consts[:, P:3 * P]).then_inc(counting_ready, 1)
            nc.scalar.copy(m.slot_source[:, 0, :, 0:E], m.xn[:])
            act.wait_ge(gap_ready, 1)
            nc.scalar.activation(top[:, 3], top[:, 2], ACT.Exp).then_inc(exp_ready, 1)
            nc.scalar.copy(m.slot_source[:, 1, :, 0:E], m.xn[:])

        @block.vector
        def _(dve):
            def wide(a):
                return a.unsqueeze(2).to_broadcast([P, NG, NR])

            nc.vector.tensor_copy(m.slot_source[:, :, :, E], m.token_rows.rearrange("p (k g) -> p k g", k=2))
            preference = m.preference[:].unsqueeze(1).to_broadcast([P, NG, NR])
            sides = m.bank[4][:, 0:2 * NE * NG].rearrange("p (g k e) -> p k g e", k=2, e=NE)[:, :, :, 0:NR]
            nc.vector.tensor_copy(tmp[:, 0], sides[:, 0]).then_inc(chain, 1)
            dve.wait_ge(chain, 1)
            nc.vector.tensor_tensor(lg[:], tmp[:, 0], sides[:, 1], ALU.add).then_inc(chain, 1)
            n = 2
            for k in range(2):
                dve.wait_ge(chain, n)
                nc.vector.tensor_reduce(top[:, k], lg[:], AX.X, ALU.max).then_inc(chain, 1)
                dve.wait_ge(chain, n + 1)
                nc.vector.tensor_tensor(tmp[:, 0], lg[:], wide(top[:, k]), ALU.is_equal).then_inc(chain, 1)
                dve.wait_ge(chain, n + 2)
                nc.vector.tensor_tensor(tmp[:, 1], tmp[:, 0], preference, ALU.mult).then_inc(chain, 1)
                dve.wait_ge(chain, n + 3)
                nc.vector.tensor_reduce(top[:, 7], tmp[:, 1], AX.X, ALU.max).then_inc(chain, 1)
                dve.wait_ge(chain, n + 4)
                nc.vector.tensor_tensor(oh[:, k], tmp[:, 1], wide(top[:, 7]), ALU.is_equal).then_inc(chain, 1)
                n += 5
                if k == 0:
                    dve.wait_ge(chain, n)
                    nc.vector.scalar_tensor_tensor(lg[:], oh[:, 0], LOW, lg[:], ALU.mult, ALU.add).then_inc(chain, 1)
                    n += 1
            dve.wait_ge(chain, n)
            nc.vector.tensor_tensor(top[:, 2], top[:, 1], top[:, 0], ALU.subtract).then_inc(gap_ready, 1)
            dve.wait_ge(chosen_zero, 1)
            nc.vector.tensor_tensor(chosen[:, 0:NG, :], oh[:, 0], oh[:, 1], ALU.add).then_inc(chosen_ready, 1)
            dve.wait_ge(exp_ready, 1)
            nc.vector.tensor_scalar(top[:, 4], top[:, 3], 1.0, None, ALU.add).then_inc(chain, 1)
            dve.wait_ge(chain, n + 1)
            nc.vector.reciprocal(top[:, 5], top[:, 4]).then_inc(chain, 1)
            dve.wait_ge(chain, n + 2)
            nc.vector.tensor_tensor(top[:, 6], top[:, 5], top[:, 3], ALU.mult).then_inc(chain, 1)
            dve.wait_ge(chain, n + 3)
            nc.vector.tensor_copy(m.slot_source[:, :, :, E + 1], top[:, 5:7]).then_inc(chain, 1)
            n += 4

            def then(make):
                nonlocal n
                dve.wait_ge(chain, n)
                make().then_inc(chain, 1)
                n += 1

            rank = m.bank[5][:, 0:(NG + 1) * NR].rearrange("p (g e) -> p g e", e=NR)
            dve.wait_ge(rank_ready, 1)
            then(lambda: nc.vector.tensor_copy(starts[:], rank[:, NG, :]))
            then(lambda: nc.vector.tensor_tensor(full[:], starts[:].unsqueeze(2).to_broadcast([P, NR, NG]),
                                                 m.multiples.unsqueeze(1).to_broadcast([P, NR, NG]), ALU.is_gt))
            then(lambda: nc.vector.tensor_reduce(tiles[:], full[:], AX.X, ALU.add))
            then(lambda: nc.vector.tensor_tensor_scan(ends[:], m.ones[:, 0:NR], tiles[:], 0.0, ALU.mult, ALU.add))
            then(lambda: nc.vector.tensor_tensor(starts[:], ends[:], tiles[:], ALU.subtract))
            then(lambda: nc.vector.tensor_scalar(starts[:], starts[:], float(P), None, ALU.mult))
            then(lambda: nc.vector.tensor_tensor(place[:], rank[:, 0:NG, :], starts[:].unsqueeze(1).to_broadcast([P, NG, NR]),
                                                 ALU.add))
            for k in range(2):
                then(lambda: nc.vector.tensor_tensor(tmp[:, k], place[:], oh[:, k], ALU.mult))
                then(lambda: nc.vector.tensor_reduce(slot_f[:, k], tmp[:, k], AX.X, ALU.add))
            then(lambda: nc.vector.tensor_copy(m.slot[:], slot_f[:]))
            then(lambda: nc.vector.tensor_tensor(passed[:], ends[:].unsqueeze(1).to_broadcast([P, NTILE, NR]),
                                                 m.tile_numbers.unsqueeze(2).to_broadcast([P, NTILE, NR]), ALU.is_le))
            then(lambda: nc.vector.tensor_reduce(owner[:, 0], passed[:], AX.X, ALU.add))
            then(lambda: nc.vector.tensor_scalar(owner[:, 1], owner[:, 0], float(NR - 1), None, ALU.min))
            then(lambda: nc.vector.tensor_copy(m.tile_expert[:], owner[:, 1]))

        @block.gpsimd
        def _(pool):
            pool.memset(chosen[:, NG, :], 0.0).then_inc(chosen_zero, 1)


def experts(nc, m, out):
    with ExitStack() as ctx:
        def sb(name, shape, dt=F32):
            return ctx.enter_context(nc.sbuf_tensor(name, shape, dt))

        def sem(name):
            return ctx.enter_context(nc.semaphore(name))

        rows = sb("f_rows", [P, 4, SE])
        meta = sb("f_meta", [P, 4, 2])
        place = sb("f_place", [P, 4], mybir.dt.uint32)
        xg = [sb(f"f_xg{k}", [P, 2, P], F32R) for k in range(2)]
        gate = sb("f_gate", [P, 2, HID])
        h = sb("f_h", [P, 2, HID])
        hT = [sb(f"f_hT{k}", [P, 2, HID], F32R) for k in range(2)]
        ysb = sb("f_ysb", [P, 4, E])
        back = m.back
        scattered = sem("f_scattered")
        rows_loaded = [sem(f"f_rows_loaded{s}") for s in range(4)]
        rowsT_ready = sem("f_rowsT_ready")
        xg_high = sem("f_xg_high")
        xg_ready = sem("f_xg_ready")
        g_ready = sem("f_g_ready")
        u_ready = sem("f_u_ready")
        gate_ready = sem("f_gate_ready")
        h_ready = sem("f_h_ready")
        hT_ready = sem("f_hT_ready")
        hT_high = sem("f_hT_high")
        hT_out = sem("f_hT_out")
        y_ready = sem("f_y_ready")
        y_out = sem("f_y_out")
        y_stored = [sem(f"f_y_stored{s}") for s in range(4)]
        back_loaded = [sem(f"f_back_loaded{k}") for k in range(NG // 4)]
        mixed = sem("f_mixed")
        y_part = sem("f_y_part")
        stored = sem("f_stored")
        gb, ub, tb, yb, rb = m.bank[0:2], m.bank[2:4], m.bank[4:6], m.bank[6], m.bank[7]
        JOBS = NG + NTILE
        block = ctx.enter_context(nc.Block())

        @block.gpsimd
        def _(pool):
            for g in range(NG):
                for k in range(2):
                    pool.indirect_dma_start(m.slot_rows[:, :], bass.IndirectOffsetOnAxis(m.slot[:, k, g:g + 1], 0),
                                            m.slot_source[:, k, g, :], None).then_inc(scattered, 16)

            for j in range(NTILE):
                s = j % 4
                pool.wait_ge(y_out, j + NG + 1)
                pool.indirect_dma_start(m.results[:, :], bass.IndirectOffsetOnAxis(place[:, s:s + 1], 0),
                                        ysb[:, s, :], None).then_inc(y_stored[s], 16)

        @block.sync
        def _(sp):
            def load(j, s):
                if not early(j, 4):
                    sp.wait_ge(xg_ready, j + (NG - 3))
                sp.dma_start(rows[:, s, :], m.slot_rows[bass.ts(j, P), :]).then_inc(rows_loaded[s], 16)

            sp.wait_ge(scattered, 16 * 2 * NG)
            for j in range(4):
                load(j, j)
            with sp.Fori(1, NTILE // 4) as i:
                for s in range(4):
                    load(i * 4 + s, s)
            for j in range(NTILE // 4 * 4, NTILE):
                load(j, j % 4)
            for s in range(4):
                sp.wait_ge(y_stored[s], 16 * len(range(s, NTILE, 4)))
            rv = m.results[0:2 * TOK, :].rearrange("(k g p) e -> p k g e", k=2, p=P)
            for q in range(NG // 4):
                part = slice(4 * q, 4 * q + 4)
                for k in range(2):
                    sp.dma_start(back[:, k, part, :], rv[:, k, part, :]).then_inc(back_loaded[q], 16)
            ov = out.rearrange("(g p) d -> p g d", p=P)
            for k in range(NG // 4):
                sp.wait_ge(mixed, 2 * (k + 1))
                sp.dma_start(ov[:, 4 * k:4 * k + 4, :], m.x[:, 4 * k:4 * k + 4, :]).then_inc(stored, 16)
            sp.wait_ge(stored, 16 * (NG // 4))

        @block.tensor
        def _(pe):
            def expert_of(n):
                if isinstance(n, int) and n < NG:
                    return NR
                return pe.value_load(m.tile_expert[0:1, bass.ds(n - NG, 1)], min_val=0, max_val=NR - 1)

            def turn_rows(n, s):
                pe.wait_ge(rows_loaded[s], (n - NG - s) * 4 + 16)
                if not early(n, NG + 1):
                    pe.wait_ge(xg_ready, n)
                nc.tensor.transpose(rb[:, 0:P], rows[:, s, 0:E], m.ident).then_inc(rowsT_ready, 1)

            def up(n, par, e):
                pe.wait_ge(xg_ready, n + 1)
                if not early(n, 2):
                    pe.wait_ge(gate_ready, n - 1)
                product3(nc, gb[par][:], [a[:, par, :] for a in xg], [a[:, e, 0:HID] for a in m.w_exp], True, True).then_inc(g_ready, 1)
                if not early(n, 2):
                    pe.wait_ge(h_ready, n - 1)
                product3(nc, ub[par][:], [a[:, par, :] for a in xg], [a[:, e, HID:2 * HID] for a in m.w_exp], True, True).then_inc(u_ready, 1)

            def turn(n, par):
                pe.wait_ge(h_ready, n + 1)
                if not early(n, 2):
                    pe.wait_ge(hT_out, n - 1)
                for j in range(KT):
                    last = nc.tensor.transpose(tb[par][:, j * P:(j + 1) * P], h[:, par, j * P:(j + 1) * P], m.ident)
                last.then_inc(hT_ready, 1)

            def down(n, par, e):
                pe.wait_ge(hT_out, n + 1)
                if not early(n, 1):
                    pe.wait_ge(y_out, n)
                def high(j):
                    return nc.tensor.matmul(yb[:, 0:2 * E], hT[0][:, par, j * P:(j + 1) * P],
                                            m.w_exp_parts[:, :, e, 2 * HID + j * E:2 * HID + (j + 1) * E],
                                            start=(j == 0), stop=(j == KT - 1))

                high(0)
                for j in range(KT):
                    nc.tensor.matmul(yb[:, E:2 * E], hT[1][:, par, j * P:(j + 1) * P],
                                     m.w_exp[0][:, e, 2 * HID + j * E:2 * HID + (j + 1) * E], start=False, stop=False)
                for j in range(1, KT):
                    last = high(j)
                last.then_inc(y_ready, 1)

            def step(n, par, shared, shared_before, rows_next, e=None, e_before=None, read_next=False):
                e_next = None
                if rows_next is not None:
                    turn_rows(n + 1, rows_next)
                if e is None:
                    e = NR if shared else expert_of(n)
                up(n, par, e)
                if not early(n, 1):
                    turn(n - 1, 1 - par)
                if not early(n, 2):
                    if e_before is None:
                        e_before = NR if shared_before else expert_of(n - 2)
                    if read_next:
                        e_next = expert_of(n + 1)
                    down(n - 2, par, e_before)
                return e, e_next

            for n in range(2):
                step(n, n, True, True, None)
            with pe.Fori(1, NG // 2 - 1) as k:
                for par in range(2):
                    step(k * 2 + par, par, True, True, None)
            def straight(first, behind):
                used, e = [None, None], None
                for n in range(first, behind):
                    reads_next = NG <= n + 1 < behind
                    now, e = step(n, n % 2, n < NG, n - 2 < NG, (n + 1) % 4 if NG <= n + 1 < JOBS else None, e,
                                  used[n - first], reads_next)
                    used.append(now)

            straight(NG - 2, NG + 8)
            with pe.Fori(NG // 8 + 1, JOBS // 8) as i:
                used, e = [None, None], None
                for s in range(8):
                    now, e = step(i * 8 + s, s % 2, False, False, (s + 1) % 4, e, used[s], s < 7)
                    used.append(now)
            straight(JOBS // 8 * 8, JOBS)
            turn(JOBS - 1, 1)
            down(JOBS - 2, 0, expert_of(JOBS - 2))
            down(JOBS - 1, 1, expert_of(JOBS - 1))

        @block.scalar
        def _(act):
            def slot_rows_out(n, par):
                act.wait_ge(rowsT_ready, n - (NG - 1))
                act.wait_ge(u_ready, n - 1)
                nc.scalar.copy(xg[0][:, par, :], rb[:, 0:P]).then_inc(xg_high, 1)

            def group_rows(n, par):
                if not early(n, 2):
                    act.wait_ge(u_ready, n - 1)
                nc.scalar.copy(xg[0][:, par, :], m.xT[0][:, bass.ts(n, P)].bitcast(F32)).then_inc(xg_high, 1)

            def turned(n, par):
                act.wait_ge(hT_ready, n + 1)
                if not early(n, 2):
                    act.wait_ge(y_ready, n - 1)
                nc.scalar.copy(hT[0][:, par, :], tb[par][:]).then_inc(hT_high, 1)

            def step(n, par, from_group):
                if from_group is True:
                    group_rows(n + 1, 1 - par)
                elif from_group is False:
                    slot_rows_out(n + 1, 1 - par)
                act.wait_ge(g_ready, n + 1)
                if not early(n, 2):
                    act.wait_ge(h_ready, n - 1)
                nc.scalar.activation(gate[:, par, :], gb[par][:], ACT.Silu).then_inc(gate_ready, 1)
                if not early(n, 1):
                    turned(n - 1, 1 - par)

            group_rows(0, 0)
            for n in range(2):
                step(n, n, True)
            with act.Fori(1, NG // 2 - 1) as k:
                for par in range(2):
                    step(k * 2 + par, par, True)
            for n in range(NG - 2, NG + 4):
                step(n, n % 2, n + 1 < NG)
            with act.Fori(NG // 2 + 2, JOBS // 2 - 1) as k:
                for par in range(2):
                    step(k * 2 + par, par, False)
            step(JOBS - 2, 0, False)
            step(JOBS - 1, 1, None)
            turned(JOBS - 1, 1)

        @block.vector
        def _(dve):
            def result_out(n, slot):
                dve.wait_ge(y_ready, n + 1)
                if slot is None:
                    nc.vector.tensor_tensor(m.x[:, n, :], m.x[:, n, :], yb[:, 0:E], ALU.add).then_inc(y_part, 1)
                    dve.wait_ge(y_part, n + 1)
                    nc.vector.tensor_tensor(m.x[:, n, :], m.x[:, n, :], yb[:, E:2 * E], ALU.add).then_inc(y_out, 1)
                else:
                    if not early(n, NG + 4):
                        dve.wait_ge(y_stored[slot], (n - NG - slot) * 4)
                    nc.vector.tensor_copy(place[:, slot:slot + 1], meta[:, slot, 0:1])
                    nc.vector.tensor_scalar(ysb[:, slot, :], yb[:, 0:E], meta[:, slot, 1:2], None, ALU.mult).then_inc(y_part, 1)
                    dve.wait_ge(y_part, n + 1)
                    nc.vector.scalar_tensor_tensor(ysb[:, slot, :], yb[:, E:2 * E], meta[:, slot, 1:2], ysb[:, slot, :],
                                                   ALU.mult, ALU.add).then_inc(y_out, 1)

            def rows_low(n, par, from_group, slot):
                dve.wait_ge(xg_high, n + 1)
                if from_group:
                    nc.vector.tensor_copy(xg[1][:, par, :], m.xT[1][:, bass.ts(n, P)].bitcast(F32)).then_inc(xg_ready, 1)
                else:
                    if not early(n, NG + 4):
                        dve.wait_ge(y_out, n - 3)
                    nc.vector.tensor_copy(meta[:, slot, :], rows[:, slot, E:SE])
                    nc.vector.tensor_tensor(xg[1][:, par, :], rb[:, 0:P], xg[0][:, par, :].bitcast(F32),
                                            ALU.subtract).then_inc(xg_ready, 1)

            def turned_low(n, par):
                dve.wait_ge(hT_high, n + 1)
                nc.vector.tensor_tensor(hT[1][:, par, :], tb[par][:], hT[0][:, par, :].bitcast(F32),
                                        ALU.subtract).then_inc(hT_out, 1)

            def step(n, par, slot, from_group, next_slot=None):
                if from_group is not None:
                    rows_low(n + 1, 1 - par, from_group, next_slot)
                dve.wait_ge(gate_ready, n + 1)
                dve.wait_ge(u_ready, n + 1)
                if not early(n, 2):
                    dve.wait_ge(hT_ready, n - 1)
                nc.vector.tensor_tensor(h[:, par, :], gate[:, par, :], ub[par][:], ALU.mult).then_inc(h_ready, 1)
                if not early(n, 1):
                    turned_low(n - 1, 1 - par)
                if not early(n, 2):
                    result_out(n - 2, slot)

            rows_low(0, 0, True, None)
            for n in range(2):
                step(n, n, None, True)
            with dve.Fori(1, NG // 2 - 1) as k:
                for par in range(2):
                    step(k * 2 + par, par, None, True)
            for n in range(NG - 2, NG + 8):
                step(n, n % 2, None if n - 2 < NG else (n - 2) % 4, n + 1 < NG, (n + 1) % 4)
            with dve.Fori(NG // 4 + 2, JOBS // 4) as i:
                for s in range(4):
                    step(i * 4 + s, s % 2, (s + 2) % 4, False, (s + 1) % 4)
            for n in range(JOBS // 4 * 4, JOBS):
                step(n, n % 2, (n - 2) % 4, False if n + 1 < JOBS else None, (n + 1) % 4)
            turned_low(JOBS - 1, 1)
            for n in range(JOBS - 2, JOBS):
                result_out(n, n % 4)
            for q in range(NG // 4):
                dve.wait_ge(back_loaded[q], 32)
                part = slice(4 * q, 4 * q + 4)
                for k in range(2):
                    if k:
                        dve.wait_ge(mixed, 2 * q + 1)
                    nc.vector.tensor_tensor(m.x[:, part, :], m.x[:, part, :], back[:, k, part, :], ALU.add).then_inc(mixed, 1)


def perceiver_layer(nc, ins, out):
    with ExitStack() as ctx:
        m = Shared()

        def buffers(stack):
            def sb(name, shape, dt=F32):
                return stack.enter_context(nc.sbuf_tensor(name, shape, dt))
            return sb

        sb = buffers(ctx)

        def pair(make, name, shape):
            return [make(f"{name}{k}", shape, F32R) for k in range(2)]

        def sem(name):
            return ctx.enter_context(nc.semaphore(name))

        psum = ctx.enter_context(nc.psum_tensor("banks", [P, 8, 512], F32))
        m.bank = [psum[:, k, :] for k in range(8)]
        m.scores = psum[:, 0:NT, :]
        step = 512 + T
        m.own_scores = bass.AP(psum, 0, [[8 * 512, P], [step, GB], [P, 4], [1, T]])
        m.x = sb("x", [P, NG, E])
        m.xn = sb("xn", [P, NG, E])
        m.xT = pair(sb, "xT", [P, TOK])
        m.stat = sb("stat", [P, 4, NG])
        m.moments = sb("moments", [P, NG, 6])
        m.mean_var = sb("mean_var", [P, NG, 2])
        m.consts = sb("consts", [P, 3 * P + NR + 3 * NG + 2 * NTILE])
        m.ident, m.ahead, m.ones = (m.consts[:, k * P:(k + 1) * P] for k in range(3))
        m.preference = m.consts[:, 3 * P:3 * P + NR]
        m.multiples = m.consts[:, 3 * P + NR:3 * P + NR + NG]
        at = 3 * P + NR + NG
        m.tile_numbers = m.consts[:, at:at + NTILE]
        at += NTILE
        m.token_rows = m.consts[:, at:at + 2 * NG]
        m.empty_rows = m.consts[:, at + 2 * NG:]
        m.own_entry = sb("own_entry", [NT * GB, GB])
        m.w_out = sb("w_out", [P, DE // P, E])
        m.router_in = sb("router_in", [P, NE])
        m.router_parts = sb("router_parts", [P, 2, NE], F32R)
        m.router = [m.router_parts[:, k] for k in range(2)]
        m.gamma_in = sb("gamma_in", [P, 1])
        m.gamma = sb("gamma", [P, 1])
        m.lam_in = sb("lam_in", [P, 4, DD])
        m.lam_prod = sb("lam_prod", [P, 2, DD])
        m.lam = sb("lam", [P, 5])
        m.pair_factor = sb("pair_factor", [P, 2])
        m.slot = sb("slot", [P, 2, NG], mybir.dt.uint32)
        m.tile_expert = sb("tile_expert", [P, NTILE], mybir.dt.int32)
        m.slot_rows = nc.dram_tensor("slot_rows", [NTILE * P, SE], F32, kind="Internal").ap()
        m.results = nc.dram_tensor("results", [2 * TOK + NTILE * P, E], F32, kind="Internal").ap()
        m.v_scratch = nc.dram_tensor("v_scratch", [B, H * E], F32, kind="Internal").ap()
        m.expert_sources = [(ins["w_gate"][e], ins["w_up"][e], ins["w_down"][e]) for e in range(NR)]
        m.expert_sources.append((ins["sw_gate"][0], ins["sw_up"][0], ins["sw_down"][0]))

        m.ins = ins
        m.x_loaded = [sem(f"x_loaded{k}") for k in range(2)]
        m.cx_high = sem("cx_high")
        m.cx_low = sem("cx_low")
        m.cx_loaded = [sem(f"cx_loaded{s}") for s in range(GB)]
        m.consts_loaded = sem("consts_loaded")
        m.aw_loaded = [sem(f"aw_loaded{n}") for n in range(FOLDS)]
        m.mask_loaded = sem("mask_loaded")
        m.row_loaded = sem("row_loaded")
        m.misc_loaded = sem("misc_loaded")
        m.self_loaded = sem("self_loaded")
        m.v_stored = sem("v_stored")
        m.folded = sem("folded")
        m.folded_high = sem("folded_high")
        m.folded_out = sem("folded_out")
        m.v_row = sem("v_row")
        m.v_row_out = sem("v_row_out")
        m.lam_step = sem("lam_step")
        m.lam_exp = sem("lam_exp")
        m.self_folded = sem("self_folded")
        m.self_folded_high = sem("self_folded_high")
        m.other_high = sem("other_high")
        m.row_high = sem("row_high")
        m.raw_loaded = [sem(f"raw_loaded{k}") for k in range(RAW)]
        m.raw_high = sem("raw_high")
        m.raw_low = sem("raw_low")
        m.zeros_ready = sem("zeros_ready")
        m.slots_zeroed = sem("slots_zeroed")

        with ExitStack() as cross:
            cb = buffers(cross)
            m.mask_add = cb("mask_add", [P, NG, S2], BF16)
            m.spread = cb("spread", [P, GB, P], BF16)
            m.w_qk = pair(cb, "w_qk", [P, H, P])
            m.w_vo = pair(cb, "w_vo", [P, H, P])
            m.cx_raw = cb("cx_raw", [P, GB, PACK])
            m.cx = pair(cb, "cx", [P, GB, PACK])
            m.row_parts = pair(cb, "row_parts", [P, P])
            m.v_rows = m.xn[0:B].rearrange("p g d -> p (g d)").rearrange("p (a n) -> p a n", a=4)
            with ExitStack() as early:
                eb = buffers(early)
                m.aw = eb("aw", [DK, 4, H, P])
                m.last_row = eb("last_row", [P, P])
                m.mask_in = eb("mask_in", [P, NG, S2], U8)
                layer_norm(nc, m, "ln1")
            cross_attention(nc, m, ins["ctx_pack"])
        m.att = sb("att", [P, NG, DE])
        m.att_squares = sb("att_squares", [P, NG * DH])
        m.raw = sb("raw_weights", [P, RAW, EW])
        with ExitStack() as attention:
            ab = buffers(attention)
            with ExitStack() as early:
                m.w_dd = pair(ab, "w_dd", [P, NC, P])
                m.w_v = pair(ab, "w_v", [P, DE])
                eb = buffers(early)
                m.dw = eb("dw", [DD, 2, NC, P])
                m.w_v_in = eb("w_v_in", [P, DE])
                layer_norm(nc, m, "ln2")
            differential_attention(nc, m)
        m.w_exp_parts = sb("w_exp", [P, 2, NE, EW], F32R)
        m.w_exp = [m.w_exp_parts[:, k] for k in range(2)]
        attention_output(nc, m)
        free = m.att[:].rearrange("p g d -> p (g d)")
        layer_norm(nc, m, "ln3")
        m.slot_source = free[:, 0:2 * NG * SE].rearrange("p (k g d) -> p k g d", k=2, g=NG)
        route(nc, m)
        m.back = free[:, 0:2 * NG * E].rearrange("p (k g d) -> p k g d", k=2, g=NG)
        experts(nc, m, out)


def kernel(**inputs):
    from concourse import bacc
    from concourse.bass_utils import run_bass_kernel_spmd

    a = {k: np.ascontiguousarray(v) for k, v in inputs.items()}
    f32 = np.float32
    ctx = a["ctx_1024"]
    nat = ctx[:, :CH * P, :].reshape(B, CH, P, E).transpose(0, 2, 1, 3).reshape(B, P, CH * E)
    row = np.concatenate([np.arange(NR, 0, -1), P * np.arange(NG), np.arange(NTILE)]).astype(f32)
    rows = P * np.arange(2 * NG + NTILE) + np.arange(P)[:, None]
    consts = np.concatenate([np.eye(P, dtype=f32), np.triu(np.ones((P, P), f32), 1), np.ones((P, P), f32),
                             np.tile(row, (P, 1)), rows.astype(f32)], 1)
    spread = np.zeros((P, GB, P), f32)
    for b in range(GB):
        for t in range(T):
            spread[b * T + t, b, t::T] = 1.0
    import ml_dtypes

    def heads_first(w):
        return w.reshape(E, DH, 2, DD).transpose(3, 2, 1, 0).reshape(DD, NC, E)

    arrays = {
        "x": a["x"].reshape(TOK, E),
        "ctx_pack": np.concatenate([nat, ctx.transpose(0, 2, 1), np.zeros((B, P, 1), f32)], 2),
        "last_row": np.concatenate([ctx[:, S2 - 1, :].T, np.zeros((P, P - B), f32)], 1),
        "mask": a["mask_Bx1xSxS2_bf1"].reshape(TOK, S2).view(np.uint8),
        "aw": np.stack([a["L0_xattn_w_q"].transpose(2, 0, 1), a["L0_xattn_w_k"].transpose(2, 0, 1),
                        a["L0_xattn_w_v"].transpose(2, 0, 1), a["L0_xattn_w_o"].transpose(1, 0, 2)], 1),
        "dw": np.stack([heads_first(a["L0_attn_Wq"]), heads_first(a["L0_attn_Wkv"][:, :DE])], 1),
        "w_v": a["L0_attn_Wkv"][:, DE:],
        "w_out": a["L0_attn_Wout"].reshape(DE // P, P, E).transpose(1, 0, 2),
        "gamma": np.tile(a["L0_attn_gamma"], P // (2 * DD)).reshape(P, 1),
        "lam": np.tile(np.stack([a["L0_attn_lambda_q1"], a["L0_attn_lambda_q2"], a["L0_attn_lambda_k1"],
                                 a["L0_attn_lambda_k2"]])[None], (P, 1, 1)),
        "router": np.concatenate([a["L0_ffn_router_w"].T, np.zeros((E, 1), f32)], 1),
        "w_gate": a["L0_ffn_w_gate"], "w_up": a["L0_ffn_w_up"], "w_down": a["L0_ffn_w_down"],
        "sw_gate": a["L0_ffn_sw_gate"], "sw_up": a["L0_ffn_sw_up"], "sw_down": a["L0_ffn_sw_down"],
        "consts": consts,
        "own_entry": np.tile(np.eye(GB, dtype=f32), (NT, 1)),
        "spread": spread.astype(ml_dtypes.bfloat16),
    }
    arrays = {f"in_{k}": np.ascontiguousarray(v) for k, v in arrays.items()}
    nc = bacc.Bacc("TRN2", target_bir_lowering=False, num_devices=1)
    ins = {k[3:]: nc.dram_tensor(k, v.shape, mybir.dt.from_np(v.dtype), kind="ExternalInput").ap()
           for k, v in arrays.items()}
    out = nc.dram_tensor("out", (TOK, E), F32, kind="ExternalOutput").ap()
    perceiver_layer(nc, ins, out)
    r = run_bass_kernel_spmd(nc, [arrays], core_ids=[0])
    return r.results[0]["out"].reshape(B, T, E)
```
